# Optimizing a Trainium2 kernel written in Bass

```python
import numpy as np
import jax
import jax.numpy as jnp

def _softmax(x, axis=-1):
    return jax.nn.softmax(x, axis=axis)

def _gelu(x):
    return jax.nn.gelu(x, approximate=True)

def _silu(x):
    return jax.nn.silu(x)

def _sigmoid(x):
    return jax.nn.sigmoid(x)

def _layernorm(x, axis=-1, eps=1e-05):
    m = jnp.mean(x, axis=axis, keepdims=True)
    v = jnp.var(x, axis=axis, keepdims=True)
    return (x - m) / jnp.sqrt(v + eps)

def _scatter_add(tgt, idx, src, axis=0):
    return tgt.at[idx].add(src)

def _segment_sum(src, seg, n):
    return jax.ops.segment_sum(src, seg, n)
kernel_name = 'mk_flamingo_gated_d2_seqx_r4_5f97be'

def setup_inputs(seed: int=0):
    np.random.seed(seed)
    _w = jnp.asarray

    def _rec_inputs():
        import jax
        import jax.numpy as jnp
        _rk = jax.random.key(seed)
        x = -0.0003929 + 0.9999 * jax.random.normal(jax.random.fold_in(_rk, 1), (1, 2048, 256), jnp.float32)
        _lenS = 2048 - jax.random.randint(jax.random.fold_in(_rk, 7), (1,), 0, max(1, 2048 // 4) + 1, jnp.int32)
        _lenS2 = 1601 - jax.random.randint(jax.random.fold_in(_rk, 8), (1,), 0, max(1, 1601 // 4) + 1, jnp.int32)
        _ctx_2048P = jax.random.normal(jax.random.fold_in(_rk, 11), (1, 16, 512), jnp.float32)
        _ctx_2048c = jax.random.dirichlet(jax.random.fold_in(_rk, 511), 0.3 * jnp.ones((16,), jnp.float32), (1, 1601))
        _ctx_2048t = jnp.einsum('bsk,bkd->bsd', _ctx_2048c, _ctx_2048P)
        _ctx_2048t = _ctx_2048t * jax.lax.rsqrt(jnp.mean(jnp.square(_ctx_2048t)) + 1e-12) * 0.953939
        ctx_2048 = 4.13588e-05 + 0.999923 * (_ctx_2048t + 0.3 * jax.random.normal(jax.random.fold_in(_rk, 611), (1, 1601, 512), jnp.float32))
        _validS = jnp.arange(2048)[None, :] < _lenS[:, None]
        _validS2 = jnp.arange(1601)[None, :] < _lenS2[:, None]
        _causal = jnp.tril(jnp.ones((2048, 2048), dtype=bool))
        mask_BxS2_if0 = jnp.where(jnp.ones((1, 1601), dtype=bool), 4, 0).astype(jnp.int32)
        _g = jax.random.normal(jax.random.fold_in(_rk, 9001), (2, 2), jnp.float32)
        _g = jnp.sign(_g) * jnp.maximum(jnp.abs(_g), 1.0) + (_g == 0) * 1.0
        g_xattn = _g[0]
        g_ffn = _g[1]
        return (x, ctx_2048, mask_BxS2_if0, g_xattn, g_ffn)
    x, ctx_2048, mask_BxS2_if0, g_xattn, g_ffn = _rec_inputs()

    def _L0_xattn_setup():
        import jax, jax.numpy as jnp
        import numpy as np
        B, L, P = (4, 1024, 256)
        D_MODEL = 256
        D_GLOBAL = 512
        HEADDIM = 32
        EPSILON = 0.001
        RMS_EPS = 1e-05

        def rmsnorm(x, g, eps=RMS_EPS):
            var = jnp.mean(jnp.square(x), axis=-1, keepdims=True)
            return x * jax.lax.rsqrt(var + eps) * g

        def _hnet_depool(h, h_patch_full, patch_lens):
            h_patch = h_patch_full[..., :D_MODEL]
            bsz, plen = (h_patch.shape[0], h_patch.shape[1])
            seqlen = h.shape[1]
            logp = jnp.full((bsz, plen), -EPSILON, dtype=jnp.float32)
            bidx = jnp.cumsum(patch_lens, axis=1) - 1
            boundary_mask = jnp.zeros((bsz, seqlen), dtype=jnp.int32)
            boundary_mask = boundary_mask.at[jnp.arange(bsz)[:, None], bidx].set(1)
            dt = (-jnp.log(-jnp.expm1(logp))).astype(h_patch.dtype)
            x = h_patch / dt[..., None]
            n_heads = D_MODEL // HEADDIM
            A = -jnp.ones((n_heads,), dtype=jnp.float32)
            bcoef = jnp.exp(logp).astype(h_patch.dtype)
            x4 = x.reshape(bsz, plen, n_heads, HEADDIM)
            a = jnp.exp(dt[:, :, None] * A[None, None, :])
            u = (dt * bcoef)[:, :, None, None] * x4
            a_b = jnp.broadcast_to(a[..., None], u.shape)

            def comb(lft, rgt):
                aL, uL = lft
                aR, uR = rgt
                return (aL * aR, uL * aR + uR)
            _, s = jax.lax.associative_scan(comb, (a_b, u), axis=1)
            depool = s.reshape(bsz, plen, D_MODEL)
            plug = jnp.clip(jnp.cumsum(boundary_mask, axis=1) - 1, 0, plen - 1)
            depool_out = depool[jnp.arange(bsz)[:, None], plug]
            return depool_out + h
        key = jax.random.key(seed)
        k1, k2, k3, k4 = jax.random.split(key, 4)
        embeds = jax.random.normal(k1, (B, L, D_MODEL), dtype=jnp.float32)
        patch_embeds = jax.random.normal(k2, (B, P, D_GLOBAL), dtype=jnp.float32)
        patch_lens = jnp.full((B, P), L // P, dtype=jnp.int64)
        W_in = jax.random.normal(k3, (D_MODEL, D_MODEL), dtype=jnp.float32) * 0.02
        b_in = jnp.zeros((D_MODEL,), dtype=jnp.float32)
        g_res = jnp.ones((D_MODEL,), dtype=jnp.float32)
        g_init = jnp.ones((D_GLOBAL,), dtype=jnp.float32)
        return {'embeds': embeds, 'patch_embeds': patch_embeds, 'patch_lens': patch_lens, 'W_in': W_in, 'b_in': b_in, 'g_res': g_res, 'g_init': g_init}
    _L0_xattn_all = _L0_xattn_setup()
    _L0_xattn_in = {k: v for k, v in _L0_xattn_all.items() if k in ('W_in', 'b_in', 'g_res', 'g_init')}
    del _L0_xattn_all

    def _L0_ffn_setup():
        import jax, jax.numpy as jnp
        import numpy as np
        B, S, IN, OUT, E, R = (8, 1024, 256, 256, 8, 8)
        LORA_ALPHA = 16
        SCALING = LORA_ALPHA / R
        key = jax.random.key(seed)
        k = jax.random.split(key, 6)
        x = jax.random.normal(k[0], (B, S, IN), dtype=jnp.float32)
        base_w = jax.random.normal(k[1], (OUT, IN), dtype=jnp.float32) * 0.02
        base_b = jnp.zeros((OUT,), dtype=jnp.float32)
        lora_A = jax.random.normal(k[2], (IN, R), dtype=jnp.float32) * 0.02
        lora_B = jax.random.normal(k[3], (E, R, OUT), dtype=jnp.float32) * 0.02
        router_w = jax.random.normal(k[4], (E, IN), dtype=jnp.float32) * 0.02
        router_b = jnp.zeros((E,), dtype=jnp.float32)
        return {'x': x, 'base_w': base_w, 'base_b': base_b, 'lora_A': lora_A, 'lora_B': lora_B, 'router_w': router_w, 'router_b': router_b}
    _L0_ffn_all = _L0_ffn_setup()
    _L0_ffn_in = {k: v for k, v in _L0_ffn_all.items() if k in ('base_w', 'base_b', 'lora_A', 'lora_B', 'router_w', 'router_b')}
    del _L0_ffn_all

    def _L1_xattn_setup():
        import jax, jax.numpy as jnp
        import numpy as np
        NUM_HEADS = 16
        key = jax.random.key(seed)
        ks = jax.random.split(key, 5)
        dim = 256
        B, N, N_c = (4, 256, 64)
        x = jax.random.normal(ks[0], (B, N, dim), dtype=jnp.float32)
        context = jax.random.normal(ks[1], (B, N_c, 2 * dim), dtype=jnp.float32)
        w_qkv = jax.random.normal(ks[2], (3 * dim, dim), dtype=jnp.float32) * 0.02
        w_proj = jax.random.normal(ks[3], (dim, dim), dtype=jnp.float32) * 0.02
        b_proj = jax.random.normal(ks[4], (dim,), dtype=jnp.float32) * 0.02
        return {'x': x, 'context': context, 'w_qkv': w_qkv, 'w_proj': w_proj, 'b_proj': b_proj}
    _L1_xattn_all = _L1_xattn_setup()
    _L1_xattn_in = {k: v for k, v in _L1_xattn_all.items() if k in ('w_qkv', 'w_proj', 'b_proj')}
    del _L1_xattn_all

    def _L1_ffn_setup():
        import jax, jax.numpy as jnp
        import numpy as np
        SL, BS, HS = (512, 4, 256)
        FF = 1024
        E, RANK, TOPK = (8, 64, 2)
        key = jax.random.key(seed)
        ks = jax.random.split(key, 7)
        s = 0.02
        return {'x': jax.random.normal(ks[0], (SL, BS, HS), jnp.float32), 'expert_weights': jax.random.uniform(ks[1], (SL * BS, TOPK), jnp.float32), 'expert_indices': jax.random.randint(ks[2], (SL * BS, TOPK), 0, E).astype(jnp.int32), 'w1_A': jax.random.normal(ks[3], (E * RANK, HS), jnp.float32) * s, 'w1_B': jax.random.normal(ks[4], (E * RANK, FF), jnp.float32) * s, 'w2_A': jax.random.normal(ks[5], (E * RANK, FF), jnp.float32) * s, 'w2_B': jax.random.normal(ks[6], (E * RANK, HS), jnp.float32) * s}
    _L1_ffn_all = _L1_ffn_setup()
    _L1_ffn_in = {k: v for k, v in _L1_ffn_all.items() if k in ('expert_weights', 'expert_indices', 'w1_A', 'w1_B', 'w2_A', 'w2_B')}
    del _L1_ffn_all
    return {'x': x, 'ctx_2048': ctx_2048, 'mask_BxS2_if0': mask_BxS2_if0, 'g_xattn': g_xattn, 'g_ffn': g_ffn, 'L0_xattn_W_in': _L0_xattn_in['W_in'], 'L0_xattn_b_in': _L0_xattn_in['b_in'], 'L0_xattn_g_res': _L0_xattn_in['g_res'], 'L0_xattn_g_init': _L0_xattn_in['g_init'], 'L0_ffn_base_w': _L0_ffn_in['base_w'], 'L0_ffn_base_b': _L0_ffn_in['base_b'], 'L0_ffn_lora_A': _L0_ffn_in['lora_A'], 'L0_ffn_lora_B': _L0_ffn_in['lora_B'], 'L0_ffn_router_w': _L0_ffn_in['router_w'], 'L0_ffn_router_b': _L0_ffn_in['router_b'], 'L1_xattn_w_qkv': _L1_xattn_in['w_qkv'], 'L1_xattn_w_proj': _L1_xattn_in['w_proj'], 'L1_xattn_b_proj': _L1_xattn_in['b_proj'], 'L1_ffn_expert_weights': _L1_ffn_in['expert_weights'], 'L1_ffn_expert_indices': _L1_ffn_in['expert_indices'], 'L1_ffn_w1_A': _L1_ffn_in['w1_A'], 'L1_ffn_w1_B': _L1_ffn_in['w1_B'], 'L1_ffn_w2_A': _L1_ffn_in['w2_A'], 'L1_ffn_w2_B': _L1_ffn_in['w2_B']}

def reference(x, ctx_2048, mask_BxS2_if0, g_xattn, g_ffn, L0_xattn_W_in, L0_xattn_b_in, L0_xattn_g_res, L0_xattn_g_init, L0_ffn_base_w, L0_ffn_base_b, L0_ffn_lora_A, L0_ffn_lora_B, L0_ffn_router_w, L0_ffn_router_b, L1_xattn_w_qkv, L1_xattn_w_proj, L1_xattn_b_proj, L1_ffn_expert_weights, L1_ffn_expert_indices, L1_ffn_w1_A, L1_ffn_w1_B, L1_ffn_w2_A, L1_ffn_w2_B):
    import jax
    import jax.numpy as jnp

    def _L0_xattn_ref(embeds, patch_embeds, patch_lens, W_in, b_in, g_res, g_init):
        import jax, jax.numpy as jnp
        import numpy as np
        B, L, P = (4, 1024, 256)
        D_MODEL = 256
        D_GLOBAL = 512
        HEADDIM = 32
        EPSILON = 0.001
        RMS_EPS = 1e-05

        def rmsnorm(x, g, eps=RMS_EPS):
            var = jnp.mean(jnp.square(x), axis=-1, keepdims=True)
            return x * jax.lax.rsqrt(var + eps) * g

        def _hnet_depool(h, h_patch_full, patch_lens):
            h_patch = h_patch_full[..., :D_MODEL]
            bsz, plen = (h_patch.shape[0], h_patch.shape[1])
            seqlen = h.shape[1]
            logp = jnp.full((bsz, plen), -EPSILON, dtype=jnp.float32)
            bidx = jnp.cumsum(patch_lens, axis=1) - 1
            boundary_mask = jnp.zeros((bsz, seqlen), dtype=jnp.int32)
            boundary_mask = boundary_mask.at[jnp.arange(bsz)[:, None], bidx].set(1)
            dt = (-jnp.log(-jnp.expm1(logp))).astype(h_patch.dtype)
            x = h_patch / dt[..., None]
            n_heads = D_MODEL // HEADDIM
            A = -jnp.ones((n_heads,), dtype=jnp.float32)
            bcoef = jnp.exp(logp).astype(h_patch.dtype)
            x4 = x.reshape(bsz, plen, n_heads, HEADDIM)
            a = jnp.exp(dt[:, :, None] * A[None, None, :])
            u = (dt * bcoef)[:, :, None, None] * x4
            a_b = jnp.broadcast_to(a[..., None], u.shape)

            def comb(lft, rgt):
                aL, uL = lft
                aR, uR = rgt
                return (aL * aR, uL * aR + uR)
            _, s = jax.lax.associative_scan(comb, (a_b, u), axis=1)
            depool = s.reshape(bsz, plen, D_MODEL)
            plug = jnp.clip(jnp.cumsum(boundary_mask, axis=1) - 1, 0, plen - 1)
            depool_out = depool[jnp.arange(bsz)[:, None], plug]
            return depool_out + h
        h = rmsnorm(embeds, g_res)
        h = jnp.einsum('bld,ed->ble', h, W_in) + b_in
        h_patch = rmsnorm(patch_embeds, g_init)
        return _hnet_depool(h, h_patch, patch_lens)

    def _L0_ffn_ref(x, base_w, base_b, lora_A, lora_B, router_w, router_b):
        import jax, jax.numpy as jnp
        import numpy as np
        B, S, IN, OUT, E, R = (8, 1024, 256, 256, 8, 8)
        LORA_ALPHA = 16
        SCALING = LORA_ALPHA / R
        result = jnp.einsum('bsd,od->bso', x, base_w) + base_b
        logits = jnp.einsum('bsd,ed->bse', x, router_w) + router_b
        gating = jax.nn.softmax(logits, axis=-1).astype(jnp.bfloat16)
        mid = jnp.einsum('bsd,dr->bsr', x, lora_A)
        lora_out = jnp.einsum('bsr,erd,bse->bsd', mid, lora_B, gating.astype(jnp.float32))
        return result + lora_out * SCALING

    def _L1_xattn_ref(x, context, w_qkv, w_proj, b_proj):
        import jax, jax.numpy as jnp
        import numpy as np
        NUM_HEADS = 16
        B, N, C = x.shape
        H = NUM_HEADS
        D = C // H
        scale = D ** (-0.5)
        qkv = (x @ w_qkv.T).reshape(B, N, 3, H, D).transpose(2, 0, 3, 1, 4)
        q, k, v = (qkv[0], qkv[1], qkv[2])
        N_c = context.shape[1]
        kv = context.reshape(B, N_c, 2, H, D).transpose(2, 0, 3, 1, 4)
        extra_k, extra_v = (kv[0], kv[1])
        k = jnp.concatenate([extra_k, k], axis=2)
        v = jnp.concatenate([extra_v, v], axis=2)
        dtype = q.dtype
        attn = jnp.einsum('bhnd,bhmd->bhnm', q * scale, k).astype(jnp.float32)
        attn = jax.nn.softmax(attn, axis=-1).astype(dtype)
        out = jnp.einsum('bhnm,bhmd->bhnd', attn, v)
        out = out.transpose(0, 2, 1, 3).reshape(B, N, C)
        return out @ w_proj.T + b_proj

    def _L1_ffn_ref(x, expert_weights, expert_indices, w1_A, w1_B, w2_A, w2_B):
        import jax, jax.numpy as jnp
        import numpy as np
        SL, BS, HS = (512, 4, 256)
        FF = 1024
        E, RANK, TOPK = (8, 64, 2)
        sl, bs, hs = x.shape
        T = sl * bs
        top_k = expert_indices.shape[-1]
        flat_e = expert_indices.reshape(-1)
        flat_w = expert_weights.reshape(-1)
        order = jnp.argsort(flat_e, stable=True)
        bin_ids = flat_e[order]
        tok = order // top_k
        xr = x.reshape(T, hs)[tok]
        w1A = w1_A.reshape(E, RANK, hs)
        w1B = w1_B.reshape(E, RANK, FF)
        w2A = w2_A.reshape(E, RANK, FF)
        w2B = w2_B.reshape(E, RANK, hs)
        out = jnp.zeros_like(xr)
        for e in range(E):
            mask = (bin_ids == e).astype(xr.dtype)[:, None]
            h = jax.nn.gelu(xr @ w1A[e].T @ w1B[e], approximate=False)
            ye = h @ w2A[e].T @ w2B[e]
            out = out + mask * ye
        y = jnp.zeros((T, hs), xr.dtype).at[tok].add(flat_w[order][:, None] * out)
        return y.reshape(sl, bs, hs)
    x = x + jnp.tanh(g_xattn[0]) * _L0_xattn_ref(_layernorm(x, axis=-1), ctx_2048, mask_BxS2_if0, L0_xattn_W_in, L0_xattn_b_in, L0_xattn_g_res, L0_xattn_g_init)
    x = x + jnp.tanh(g_ffn[0]) * _L0_ffn_ref(_layernorm(x, axis=-1), L0_ffn_base_w, L0_ffn_base_b, L0_ffn_lora_A, L0_ffn_lora_B, L0_ffn_router_w, L0_ffn_router_b)
    x = x + jnp.tanh(g_xattn[1]) * _L1_xattn_ref(_layernorm(x, axis=-1), ctx_2048, L1_xattn_w_qkv, L1_xattn_w_proj, L1_xattn_b_proj)
    x = x + jnp.tanh(g_ffn[1]) * _L1_ffn_ref(_layernorm(x, axis=-1), L1_ffn_expert_weights, L1_ffn_expert_indices, L1_ffn_w1_A, L1_ffn_w1_B, L1_ffn_w2_A, L1_ffn_w2_B)
    return x

_drawn_inputs = setup_inputs


def setup_inputs(seed=0):
    import zlib

    import numpy as np

    out = dict(_drawn_inputs(seed))
    spreads = {'g_ffn': (-1.0, 0.6),
     'L0_xattn_b_in': (0.0, 0.1),
     'L0_xattn_g_res': (1.0, 0.2),
     'L0_xattn_g_init': (1.0, 0.2),
     'L0_ffn_base_b': (0.0, 0.1),
     'L0_ffn_router_b': (0.0, 0.8)}
    factors = {'L0_ffn_lora_A': 7.715,
     'L0_ffn_lora_B': 7.425,
     'L0_ffn_router_w': 8.0,
     'L1_xattn_w_qkv': 3.723,
     'L1_xattn_b_proj': 4.132,
     'L1_ffn_expert_weights': 8.0,
     'L1_ffn_w1_A': 8.0,
     'L1_ffn_w1_B': 8.0,
     'L1_ffn_w2_A': 8.0,
     'L1_ffn_w2_B': 8.0}
    for name, (base, spread) in spreads.items():
        noise = np.random.default_rng([zlib.crc32(name.encode()), seed]).standard_normal(out[name].shape)
        drawn = base * np.exp(spread * noise) if base else spread * noise
        out[name] = jnp.asarray(drawn.astype(out[name].dtype))
    for name, factor in factors.items():
        out[name] = (out[name] * factor).astype(out[name].dtype)
    return out
```

```python
import math
from contextlib import ExitStack

import numpy as np

import concourse.bass as bass
from concourse import mybir

F32 = mybir.dt.float32
BF16 = mybir.dt.bfloat16
I32 = mybir.dt.int32
U32 = mybir.dt.uint32
ALU = mybir.AluOpType
ACT = mybir.ActivationFunctionType
AX = mybir.AxisListType.X

P = 128
T, C = 2048, 256
CC = C // P
NT = T // P
U = 4
NC = 1601
CT = -(-NC // P)
TAIL = NC - (CT - 1) * P
HEADS, D = 16, 16
G = 4
NG = HEADS // G
QB = 512
NQ = T // QB
KEYS = T + NC
KT = NT + CT
KPAD = KT * P
CH = 512
NCH = -(-KEYS // CH)
SLOTS = 6
K_PART = (0, 1, 2, 0, 1, 0)
Q_PART = (0, 0, 0, 1, 1, 2)
SR = SLOTS * D
E, RK, FF = 8, 64, 1024
NF = FF // P
NP = E // 2
R8 = 8
LN_EPS = 1e-5
PR = 3

C_ID, C_TRI, C_ONE, C_L0, C_L1, C_EC = 0, P, 2 * P, 3 * P, 4 * P, 5 * P
C_IOTA = C_EC + NP
C_ALL = C_IOTA + T


def width(c):
    return min(CH, KEYS - c * CH)


def rows(kt):
    return P if kt < KT - 1 else TAIL


def build(nc, a, out):
    logp = np.float32(-1e-3)
    dt = np.float32(-np.log(-np.expm1(logp)))
    u_scale = float(np.float32(dt * np.exp(logp)) / dt)

    qd = nc.dram_tensor("q_stack", (HEADS, SR, T), BF16)
    kd = nc.dram_tensor("k_stack", (HEADS, SR, KPAD), BF16)
    depool = nc.dram_tensor("depool", (CT * P, C), F32)

    ctx = ExitStack()
    with ctx:
        def sb(name, shape, dtype=F32, stack=ctx):
            return stack.enter_context(nc.sbuf_tensor(name, shape, dtype))

        def sem(name):
            return ctx.enter_context(nc.semaphore(name))

        sc_ps = [ctx.enter_context(nc.psum_tensor(f"sc_ps{i}", [P, 2, 512], F32)) for i in range(2)]
        pv_ps = ctx.enter_context(nc.psum_tensor("pv_ps", [P, 512], F32))
        mx_ps = [ctx.enter_context(nc.psum_tensor(f"mx_ps{i}", [P, 512], F32)) for i in range(2)]
        tr_ps = ctx.enter_context(nc.psum_tensor("tr_ps", [P, 512], F32))
        out_bank = [sc_ps[0][:, 0, :], sc_ps[0][:, 1, :], sc_ps[1][:, 0, :], sc_ps[1][:, 1, :]]
        tr_bank = [pv_ps[:, :], mx_ps[0][:, :], mx_ps[1][:, :], tr_ps[:, :]]

        X = sb("X", [P, NT, C])
        cst = sb("cst", [P, C_IOTA])
        ident, tri, ones = cst[:, C_ID:C_ID + P], cst[:, C_TRI:C_TRI + P], cst[:, C_ONE:C_ONE + P]
        lmat0, lmat1 = cst[:, C_L0:C_L0 + P], cst[:, C_L1:C_L1 + P]
        ident_b = sb("ident_b", [P, P], BF16)
        gates = sb("gates", [P, 4])
        gates_in = sb("gates_in", [P, 4])
        bn = sb("bn", [P, U, 6])
        mv = sb("mv", [P, NT, 2])
        lnv = sb("lnv", [P, NT])
        lns = sb("lns", [P, NT])
        rstd = sb("rstd", [P, NT])
        rstd2 = sb("rstd2", [P, NT])
        xs = [sb(f"xs{u}", [P, C]) for u in range(U)]
        hT = [sb(f"hT{u}", [P, CC, P]) for u in range(U)]
        tmp = [sb(f"tmp{u}", [P, C]) for u in range(U)]
        mvu = sb("mvu", [P, U, 2])
        xnew = [sb(f"xnew{u}", [P, C]) for u in range(U)]
        w_pr = sb("w_pr", [P, CC, C])
        b_pr = sb("b_pr", [P, C])
        attn = sb("attn", [P, NT, C])
        values = ExitStack()
        V = sb("V", [P, KT, C], F32, values)

        consts_in, x_in, ck_in, cv_in, mask_in = (sem(n) for n in ("consts_in", "x_in", "ck_in", "cv_in", "mask_in"))
        weights_in = sem("weights_in")
        pads_zero, dve, acte, idb_ready = sem("pads_zero"), sem("dve"), sem("acte"), sem("idb_ready")
        tanh_done, sq_done = sem("tanh_done"), sem("sq_done")
        sqrt_in, sqrt_out = sem("sqrt_in"), sem("sqrt_out")
        cum_in, cum_mm, hot_ready, cnt_mm, cum2_in, cum2_mm, plug_ready = (sem(n) for n in (
            "cum_in", "cum_mm", "hot_ready", "cnt_mm", "cum2_in", "cum2_mm", "plug_ready"))
        u_ready, dep_mm, dep_ev, dep_out, gathered, gb_ready = (sem(n) for n in (
            "u_ready", "dep_mm", "dep_ev", "dep_out", "gathered", "gb_ready"))
        ck_tr, ck_p0, ck_r1, ck_p1, ck_p2 = (sem(n) for n in ("ck_tr", "ck_p0", "ck_r1", "ck_p1", "ck_p2"))
        ck_out = sem("ck_out")
        ph = {}
        for n in "abce":
            for s in ("xs_ready", "xT_mm", "hT_ready", "out_mm"):
                ph[n, s] = sem(f"{n}_{s}")
        lg_ready, ex_ready, m64_ready, m64_tr, m64_ev, lora_mm = (sem(n) for n in (
            "lg_ready", "ex_ready", "m64_ready", "m64_tr", "m64_ev", "lora_mm"))
        c_p0, c_r1, c_p1, c_p2, qk_out = (sem(n) for n in ("c_p0", "c_r1", "c_p1", "c_p2", "qk_out"))
        km_in = [sem(f"km_in{c}") for c in range(NCH)]
        kx_in = [sem(f"kx_in{c}") for c in range(NCH)]
        q_in = [sem(f"q_in{i}") for i in range(NQ)]
        fill_done, vg_ready, qk_mm, exp_done, pv_mm, mx_mm, mx_red = (sem(n) for n in (
            "fill_done", "vg_ready", "qk_mm", "exp_done", "pv_mm", "mx_mm", "mx_red"))
        mst_ready, mrow_mm, mrow_ready, m_in, oT_ready, oT_tr, norm_done = (sem(n) for n in (
            "mst_ready", "mrow_mm", "mrow_ready", "m_in", "oT_ready", "oT_tr", "norm_done"))
        moe_w_in, tok_in, f_xs, f_tr, f_hT, s1_mm, u_ev, s2_mm, gelu_done, s3_mm, z_ready, y_mm, y_done, y_out = (
            sem(n) for n in ("moe_w_in", "tok_in", "f_xs", "f_tr", "f_hT", "s1_mm", "u_ev", "s2_mm",
                             "gelu_done", "s3_mm", "z_ready", "y_mm", "y_done", "y_out"))
        cb_base = None

        early = ExitStack()
        w_in = sb("w_in", [P, CC, C], F32, early)
        w_b0 = sb("w_b0", [P, CC, C + 2 * R8], F32, early)
        w_qkv = sb("w_qkv", [P, CC, 3 * C], F32, early)
        w_lb = sb("w_lb", [RK, C], F32, early)
        b_in, b_b0 = sb("b_in", [P, C], F32, early), sb("b_b0", [P, C], F32, early)
        b_rt = sb("b_rt", [P, R8], F32, early)
        g_ini = sb("g_ini", [P, C], F32, early)
        g_res = sb("g_res", [P, CC], F32, early)
        ss = sb("ss", [P, CT, 2], F32, early)
        crs = sb("crs", [P, CT], F32, early)
        crt = sb("crt", [P, CT], F32, early)
        sq_junk = sb("sq_junk", [P, C], F32, early)
        mask_i = sb("mask_i", [P, CT], I32, early)
        mask_f = sb("mask_f", [P, CT], F32, early)
        off = sb("off", [P, CT], F32, early)
        bidx = sb("bidx", [P, CT], F32, early)
        neg = sb("neg", [P, CT], F32, early)
        onesb = sb("onesb", [P, 1], BF16, early)
        bnd = sb("bnd", [P, NT], F32, early)
        off2 = sb("off2", [P, NT], F32, early)
        plug = sb("plug", [P, NT], F32, early)
        plug_i = sb("plug_i", [P, NT], U32, early)
        lg = [sb(f"lg{u}", [P, R8], F32, early) for u in range(U)]
        lmx = [sb(f"lmx{u}", [P, 1], F32, early) for u in range(U)]
        ex = [sb(f"ex{u}", [P, R8], F32, early) for u in range(U)]
        esum = [sb(f"esum{u}", [P, 1], F32, early) for u in range(U)]
        gate = [sb(f"gate{u}", [P, R8], BF16, early) for u in range(U)]
        m64 = [sb(f"m64{u}", [P, 2 * R8, R8], F32, early) for u in range(U)]
        m64T = [sb(f"m64T{u}", [RK, P], F32, early) for u in range(U)]
        later = ExitStack()
        PB = sb("PB", [P, 3, 4, T], BF16, later)
        CP = sb("CP", [P, 3, CC, CT * P], BF16, later)
        GB = sb("GB", [P, NT, C], F32, later)
        rest = [sb(f"rest{u}", [P, 4 * P], F32, later) for u in range(U)]
        later.close()
        iota = sb("iota", [P, T], F32, early)
        CK = sb("CK", [P, CT, C], F32, early)
        UU = sb("UU", [P, CT, C], F32, early)
        sb("to_PB_end", [P, 3 * 4 * T // 2 - T - 2 * CT * C], F32, early)
        HOT = sb("HOT", [P, CT, T], BF16, early)
        early.close()

        att = ExitStack()
        KM = sb("KM", [P, G, KEYS], BF16, att)
        KX = sb("KX", [P, G, KEYS], BF16, att)
        Vg = sb("Vg", [P, KT, G, 2 * D], F32, att)
        QS = [sb(f"QS{i}", [P, G, QB], BF16, att) for i in range(NQ)]
        PX = [sb(f"PX{i}", [P, G, QB], F32, att) for i in range(PR)]
        mp = sb("mp", [P, 4 * G, NCH], F32, att)
        mm = sb("mm", [P, 4, G], F32, att)
        mr = sb("mr", [P, 4, G], F32, att)
        mst = sb("mst", [P, 4, 3, G], BF16, att)
        mrow = sb("mrow", [3 * G, QB], BF16, att)
        oT = sb("oT", [P, QB], F32, att)
        rcp = sb("rcp", [P, 4, G], F32, att)
        att.close()
        values.close()

        moe = ExitStack()
        w1a = sb("w1a", [P, CC, E * RK], F32, moe)
        w1b = sb("w1b", [P, E, FF], F32, moe)
        w2a = sb("w2a", [P, NF, E, RK], F32, moe)
        w2b = sb("w2b", [P, NP, C], F32, moe)
        idx = sb("idx", [P, 2, T], I32, moe)
        wts = sb("wts", [P, 2, T], F32, moe)
        ecol = cst[:, C_EC:C_EC + NP]
        XT = sb("XT", [P, CC, QB], F32, moe)
        UT = sb("UT", [P, NP, QB], F32, moe)
        GE = [sb(f"GE{i}", [P, 2, QB], F32, moe) for i in range(2)]
        CB = sb("CB", [P, NP, QB], F32, moe)
        CB1 = sb("CB1", [P, QB], F32, moe)
        Z = sb("Z", [P, NP, QB], F32, moe)
        moe.close()

        block = ctx.enter_context(nc.Block())

        EXP0, PV0, RED0 = 2, 3, 2

        def step_of(kt, i):
            if kt >= PR:
                return KT * i + kt - PR
            return KT * (i - 1) + max(k for k in range(KT) if k % PR == kt % PR)

        M_STEPS = KT - 3
        M_OPS = 4 * G * NCH

        def m_ops(kt):
            return range(M_OPS * kt // M_STEPS, M_OPS * (kt + 1) // M_STEPS) if kt < M_STEPS else range(0)

        N_W = 13
        TOKB = [slice(4 * i, 4 * i + 4) for i in range(NQ)]

        @block.sync
        def _(sp):
            sp.dma_start(cst[:, :], a["consts"][:, 0:C_IOTA]).then_inc(consts_in, 16)
            sp.dma_start(mask_i[:, :], a["mask"]).then_inc(mask_in, 16)
            sp.dma_start(iota[:, :], a["consts"][:, C_IOTA:C_ALL]).then_inc(consts_in, 16)
            full = (CT - 1) * P
            sp.dma_start(CK[:, 0:CT - 1, :], a["ctx"][0:full, 0:C].rearrange("(j p) c -> p j c", p=P)).then_inc(ck_in, 16)
            sp.dma_start(V[:, NT:KT - 1, :], a["ctx"][0:full, C:2 * C].rearrange("(j p) c -> p j c", p=P)).then_inc(cv_in, 16)
            sp.wait_ge(pads_zero, 1)
            sp.dma_start(CK[0:TAIL, CT - 1, :], a["ctx"][full:NC, 0:C]).then_inc(ck_in, 16)
            sp.dma_start(V[0:TAIL, KT - 1, :], a["ctx"][full:NC, C:2 * C]).then_inc(cv_in, 16)
            sp.dma_start(X[:, :, :], a["x"].rearrange("(j p) c -> p j c", p=P)).then_inc(x_in, 16)
            sp.wait_ge(dep_ev, CT)
            sp.dma_start(depool.rearrange("(j p) c -> p j c", p=P), UU[:, :, :]).then_inc(dep_out, 16)
            sp.wait_ge(ck_p2, 2 * 4)
            for s in range(SLOTS):
                for c in range(CC):
                    sp.dma_start(kd[8 * c:8 * c + 8, D * s:D * s + D, T:KPAD], CP[:, K_PART[s], c, :]).then_inc(ck_out, 16)
            with sp.Fori(0, NT // U) as i:
                sp.wait_ge(c_p2, i * U + U)
                tok = bass.ds(i * QB, QB)
                for s in range(SLOTS):
                    for c in range(CC):
                        sp.dma_start(kd[8 * c:8 * c + 8, D * s:D * s + D, tok], PB[:, K_PART[s], CC + c, tok]).then_inc(qk_out, 16)
                        sp.dma_start(qd[8 * c:8 * c + 8, D * s:D * s + D, tok], PB[:, Q_PART[s], c, tok]).then_inc(qk_out, 16)

            sp.wait_ge(ck_out, 16 * SLOTS * CC)
            sp.wait_ge(qk_out, 16 * SLOTS * CC * 2 * (NT // U))
            sp.wait_ge(c_p2, NT)

            def load_q(g, qb):
                sp.dma_start(QS[qb][0:SR, :, :], qd[bass.ds(g * G, G), :, qb * QB:(qb + 1) * QB]
                             .rearrange("h p q -> p h q")).then_inc(q_in[qb], 16)

            def load_k(dst, done, g, c):
                cols = slice(c * CH, c * CH + width(c))
                sp.dma_start(dst[0:SR, :, cols], kd[bass.ds(g * G, G), :, cols].rearrange("h p k -> p h k")).then_inc(done[c], 16)

            def load_m(j):
                sp.wait_ge(mrow_ready, j + 1)
                sp.dma_start(QS[(j if isinstance(j, int) else 0) % NQ][SR:SR + 3, :, :], mrow[:, :]).then_inc(m_in, 16)

            load_q(0, 0)
            for c in range(NCH):
                load_k(KM, km_in, 0, c)
            load_q(0, 1)
            sp.wait_ge(fill_done, 1)
            for c in range(NCH):
                load_k(KX, kx_in, 0, c)
            load_m(0)

            def group(g, last):
                for qb in range(NQ):
                    i = g * NQ + qb
                    sp.wait_ge(qk_mm, i * 2 * KT + 1)
                    if not last or qb + 2 < NQ:
                        load_q(g + (qb + 2) // NQ, (qb + 2) % NQ)
                    if last and qb == NQ - 1:
                        continue
                    if qb == NQ - 2 and not last:
                        for c in range(NCH):
                            sp.wait_ge(mx_mm, (i + 1) * M_OPS + 4 * G * (c + 1))
                            load_k(KM, km_in, g + 1, c)
                    if qb == NQ - 1:
                        for c in range(NCH - 2):
                            sp.wait_ge(qk_mm, i * 2 * KT + 2 * 4 * (c + 1))
                            load_k(KX, kx_in, g + 1, c)
                    sp.wait_ge(mrow_ready, i + 2)
                    sp.dma_start(QS[(qb + 1) % NQ][SR:SR + 3, :, :], mrow[:, :]).then_inc(m_in, 16)
                    if qb == NQ - 1:
                        for c in range(NCH - 2, NCH):
                            sp.wait_ge(qk_mm, i * 2 * KT + min(2 * 4 * (c + 1), 2 * KT))
                            load_k(KX, kx_in, g + 1, c)

            with sp.Fori(0, NG - 1) as g:
                group(g, False)
            group(NG - 1, True)

            sp.wait_ge(norm_done, NG * NQ)
            sp.dma_start(w1a[:, :, :], a["w1a"].rearrange("(c p) n -> p c n", p=P)).then_inc(moe_w_in, 16)
            for e in range(E):
                sp.dma_start(w1b[:, e, :], a["w1b"][e]).then_inc(moe_w_in, 16)
            sp.dma_start(w2a[:, :, :, :], a["w2a"].rearrange("(f p) e r -> p f e r", p=P)).then_inc(moe_w_in, 16)
            sp.dma_start(w2b[:, :, :], a["w2b"].rearrange("(a p) c -> p a c", p=P)).then_inc(moe_w_in, 16)
            for k in range(2):
                sp.dma_start(idx[:, k, :], a["idx"][k:k + 1, :].to_broadcast([P, T])).then_inc(tok_in, 16)
                sp.dma_start(wts[:, k, :], a["wts"][k:k + 1, :].to_broadcast([P, T])).then_inc(tok_in, 16)
            with sp.Fori(0, NQ) as b:
                sp.wait_ge(y_done, b * 4 + 4)
                sp.dma_start(out.rearrange("(j p) c -> p j c", p=P)[:, bass.ds(b * 4, 4), :],
                             X[:, bass.ds(b * 4, 4), :]).then_inc(y_out, 16)
            sp.wait_ge(y_out, 16 * NQ)

        @block.gpsimd
        def _(pool):
            pool.memset(CK[:, CT - 1, :], 0.0)
            pool.memset(V[:, KT - 1, :], 0.0)
            for u in range(U):
                pool.memset(m64[u][:, R8:2 * R8, :], 0.0)
            pool.memset(onesb[:, :], 1.0).then_inc(pads_zero, 1)
            pool.wait_ge(dep_out, 16)
            pool.wait_ge(plug_ready, 1)
            for t in range(NT):
                pool.indirect_dma_start(out=GB[:, t, :], out_offset=None, in_=depool[:, :],
                                        in_offset=bass.IndirectOffsetOnAxis(ap=plug_i[:, t:t + 1], axis=0)).then_inc(gathered, 16)
            pool.wait_ge(gathered, 16 * NT)
            pool.wait_ge(weights_in, 16 * N_W)
            pool.tensor_tensor(out=GB[:, :, :], in0=GB[:, :, :], in1=b_in[:, :].unsqueeze(1).to_broadcast([P, NT, C]),
                               op=ALU.add).then_inc(gb_ready, 1)
            pool.wait_ge(c_p2, NT)
            pool.wait_ge(qk_out, 16 * SLOTS * CC * 2 * (NT // U))
            pool.wait_ge(ck_out, 16 * SLOTS * CC)
            pool.memset(KX[SR:SR + 32, :, :], 1.0).then_inc(fill_done, 1)
            pool.wait_ge(fill_done, 1)
            pool.memset(Vg[:, :, :, D:2 * D], 1.0).then_inc(fill_done, 1)
            pool.wait_ge(cv_in, 32)

            def copy_v(g, c):
                n = min(4, KT - 4 * c)
                r = P if 4 * c + n < KT else TAIL
                src = V[0:r, 4 * c:4 * c + n, bass.ds(g * G * D, G * D)].rearrange("p k (h d) -> p k h d", h=G)
                pool.tensor_copy(Vg[0:r, 4 * c:4 * c + n, :, 0:D], src).then_inc(vg_ready, 1)

            for c in range(NCH):
                copy_v(0, c)
            with pool.Fori(0, NG - 1) as g:
                for c in range(NCH):
                    pool.wait_ge(pv_mm, g * (NQ * KT) + (NQ - 1) * KT + min(4 * c + 4, KT) + PV0)
                    copy_v(g + 1, c)

        @block.scalar
        def _(act):
            act.dma_start(gates_in[:, 0:4], a["gates"].to_broadcast([P, 4])).then_inc(weights_in, 16)
            act.dma_start(w_in[:, :, :], a["w_in"].rearrange("(c p) n -> p c n", p=P)).then_inc(weights_in, 16)
            act.dma_start(w_b0[:, :, :], a["w_b0"].rearrange("(c p) n -> p c n", p=P)).then_inc(weights_in, 16)
            act.dma_start(w_qkv[:, :, :], a["w_qkv"].rearrange("(c p) n -> p c n", p=P)).then_inc(weights_in, 16)
            act.dma_start(w_pr[:, :, :], a["w_pr"].rearrange("(c p) n -> p c n", p=P)).then_inc(weights_in, 16)
            act.dma_start(w_lb[:, :], a["w_lb"]).then_inc(weights_in, 16)
            act.dma_start(b_in[:, :], a["b_in"].to_broadcast([P, C])).then_inc(weights_in, 16)
            act.dma_start(b_b0[:, :], a["b_b0"].to_broadcast([P, C])).then_inc(weights_in, 16)
            act.dma_start(b_pr[:, :], a["b_pr"].to_broadcast([P, C])).then_inc(weights_in, 16)
            act.dma_start(b_rt[:, :], a["b_rt"].to_broadcast([P, R8])).then_inc(weights_in, 16)
            act.dma_start(g_ini[:, :], a["g_ini"].to_broadcast([P, C])).then_inc(weights_in, 16)
            act.dma_start(g_res[:, :], a["g_res"]).then_inc(weights_in, 16)
            act.dma_start(bn[:, 0, :], a["consts"][:, 0:6]).then_inc(weights_in, 16)
            act.wait_ge(weights_in, 16 * N_W)
            act.activation(gates[:, :], gates_in[:, :], ACT.Tanh).then_inc(tanh_done, 1)
            act.wait_ge(ck_in, 32)
            act.wait_ge(cv_in, 32)
            for j in range(CT):
                for h, src in enumerate((CK[:, j, :], V[:, NT + j, :])):
                    act.activation(sq_junk[:, :], src, ACT.Square, accum_out=ss[:, j, h:h + 1]).then_inc(sq_done, 1)
                    act.wait_ge(sq_done, 2 * j + h + 1)

            def sqrt(dst, src, n):
                act.wait_ge(sqrt_in, n)
                act.activation(dst, src, ACT.Sqrt).then_inc(sqrt_out, 1)

            sqrt(crt[:, :], crs[:, :], 1)
            for j in range(CT):
                act.wait_ge(dep_mm, min(j + 2, CT))
                act.activation(UU[:, j, :], out_bank[j % 4][:, 0:C], ACT.Copy).then_inc(dep_ev, 1)
            for k in range(2 * 4):
                blk, c = divmod(k, CC)
                n = min(4, CT - 4 * blk) * P
                cols = slice(blk * QB, blk * QB + n)
                act.wait_ge(ck_tr, k + 1)
                act.activation(CP[:, 0, c, cols], tr_bank[k % 4][:, 0:n], ACT.Copy).then_inc(ck_p0, 1)
                act.wait_ge(ck_r1, k + 1)
                act.activation(CP[:, 1, c, cols], rest[k % 4][:, 0:n], ACT.Copy).then_inc(ck_p1, 1)

            sqrt(lns[:, :], lnv[:, :], 2)
            sqrt(lns[:, :], lnv[:, :], 3)
            with act.Fori(0, NT // U) as i:
                for u in range(U):
                    act.wait_ge(ph["a", "xT_mm"], i * U + u + 1)
                    for c in range(CC):
                        ins = act.activation(hT[u][:, c, :], tr_bank[u][:, c * P:(c + 1) * P], ACT.Copy, scale=g_res[:, c:c + 1])
                    ins.then_inc(ph["a", "hT_ready"], 1)

            def copy_hT(n, u, i):
                act.wait_ge(ph[n, "xT_mm"], i * U + u + 1)
                act.activation(hT[u][:, :, :].rearrange("p c t -> p (c t)"), tr_bank[u][:, 0:C], ACT.Copy).then_inc(ph[n, "hT_ready"], 1)

            sqrt(lns[:, :], lnv[:, :], 4)
            with act.Fori(0, NT // U) as i:
                for u in range(U):
                    copy_hT("b", u, i)
                for u in range(U):
                    act.wait_ge(lg_ready, i * U + u + 1)
                    act.activation(ex[u][:, :], lg[u][:, :], ACT.Exp, accum_out=esum[u][:, :]).then_inc(ex_ready, 1)
                for u in range(U):
                    act.wait_ge(m64_tr, i * U + u + 1)
                    act.activation(m64T[u][:, :], tr_bank[u][0:RK, C:C + P], ACT.Copy, scale=2.0).then_inc(m64_ev, 1)

            sqrt(lns[:, :], lnv[:, :], 5)
            with act.Fori(0, NT // U) as i:
                for u in range(U):
                    copy_hT("c", u, i)
                for u in range(U):
                    cols = bass.ds(i * QB + u * P, P)
                    act.wait_ge(ph["c", "out_mm"], i * U + u + 1)
                    act.activation(PB[:, 0, :, cols], out_bank[u].rearrange("p (k t) -> p k t", k=4), ACT.Copy).then_inc(c_p0, 1)
                for u in range(U):
                    cols = bass.ds(i * QB + u * P, P)
                    act.wait_ge(c_r1, i * U + u + 1)
                    act.activation(PB[:, 1, :, cols], rest[u][:, :].rearrange("p (k t) -> p k t", k=4), ACT.Copy).then_inc(c_p1, 1)

            act.wait_ge(qk_out, 16 * SLOTS * CC * 2 * (NT // U))
            act.wait_ge(ck_out, 16 * SLOTS * CC)
            act.wait_ge(c_p2, NT)
            act.sem_inc(exp_done, EXP0)

            def block_exps(g, qb):
                i = g * NQ + qb
                for kt in range(KT):
                    r = rows(kt)
                    for p in range(2):
                        if p == 0:
                            act.wait_ge(pv_mm, PV0 + step_of(kt, i) + 1)
                        act.wait_ge(qk_mm, i * 2 * KT + 2 * kt + p + 1)
                        act.activation(PX[kt % PR][0:r, 2 * p:2 * p + 2, :], sc_ps[p][0:r, :, :], ACT.Exp,
                                       scale=D ** -0.5).then_inc(exp_done, 1)

            with act.Fori(0, NG) as g:
                for qb in range(NQ):
                    block_exps(g, qb)

            with act.Fori(0, NT // U) as i:
                for u in range(U):
                    copy_hT("e", u, i)

            sqrt(lns[:, :], lnv[:, :], 6)
            with act.Fori(0, NQ) as b:
                for u in range(4):
                    act.wait_ge(f_tr, b * 4 + u + 1)
                    act.activation(XT[:, :, u * P:(u + 1) * P], tr_bank[u][:, 0:C].rearrange("p (c t) -> p c t", c=CC),
                                   ACT.Copy).then_inc(f_hT, 1)
                for p in range(NP):
                    act.wait_ge(s1_mm, b * NP + p + 1)
                    act.activation(UT[:, p, :], mx_ps[p % 2][:, :], ACT.Copy).then_inc(u_ev, 1)
                for p in range(NP):
                    for f in range(NF):
                        act.wait_ge(s2_mm, b * (NP * NF) + p * NF + f + 1)
                        act.activation(GE[f % 2][:, :, :], sc_ps[f % 2][:, :, :], ACT.Gelu).then_inc(gelu_done, 1)

        @block.vector
        def _(v):
            cnt = [0]
            base = [0]

            def link(ins):
                cnt[0] += 1
                ins.then_inc(dve, 1)
                v.wait_ge(dve, base[0] + cnt[0])

            def enter(i, per):
                base[0] = fixed[0] + i * per
                cnt[0] = 0

            def leave(n, per):
                assert cnt[0] == per, (cnt[0], per)
                fixed[0] += n * per
                base[0], cnt[0] = fixed[0], 0

            def mark():
                fixed[0] = base[0] + cnt[0]

            fixed = [0]

            v.wait_ge(consts_in, 32)
            link(v.tensor_copy(ident_b[:, :], ident))
            v.wait_ge(mask_in, 16)
            v.tensor_copy(mask_f[:, :], mask_i[:, :]).then_inc(cum_in, 1)
            v.wait_ge(cum_mm, 1)
            link(v.tensor_tensor_scan(off[:, :], ones[:, 0:CT], tr_bank[0][:, CT:2 * CT], 0.0, ALU.mult, ALU.add))
            link(v.tensor_tensor(out=off[:, :], in0=off[:, :], in1=tr_bank[0][:, CT:2 * CT], op=ALU.subtract))
            link(v.scalar_tensor_tensor(out=bidx[:, :], in0=off[:, :], scalar=-1.0, in1=tr_bank[0][:, 0:CT], op0=ALU.add, op1=ALU.add))
            link(v.tensor_scalar(neg[:, :], bidx[:, :], 0.0, float(T), ALU.is_lt, ALU.mult))
            link(v.tensor_tensor(out=bidx[:, :], in0=bidx[:, :], in1=neg[:, :], op=ALU.add))
            for j in range(CT):
                v.tensor_scalar(HOT[:, j, :], iota[:, :], bidx[:, j:j + 1], None, ALU.is_equal).then_inc(hot_ready, 1)
            v.wait_ge(sq_done, 2 * CT)
            link(v.tensor_tensor(out=crs[:, :], in0=ss[:, :, 0], in1=ss[:, :, 1], op=ALU.add))
            v.tensor_scalar(crs[:, :], crs[:, :], 1.0 / (2 * C), 1e-5, ALU.mult, ALU.add).then_inc(sqrt_in, 1)
            v.wait_ge(sqrt_out, 1)
            link(v.reciprocal(crs[:, :], crt[:, :]))
            link(v.tensor_scalar(crs[:, :], crs[:, :], u_scale, None, ALU.mult))
            v.wait_ge(weights_in, 16 * N_W)
            for j in range(CT):
                v.scalar_tensor_tensor(out=UU[:, j, :], in0=CK[:, j, :], scalar=crs[:, j:j + 1], in1=g_ini[:, :],
                                       op0=ALU.mult, op1=ALU.mult).then_inc(u_ready, 1)
            v.wait_ge(cnt_mm, 1)
            v.tensor_scalar(bnd[:, :], tr_bank[1][:, 0:NT], 1.0, None, ALU.min).then_inc(cum2_in, 1)
            v.wait_ge(cum2_mm, 1)
            link(v.tensor_tensor_scan(off2[:, :], ones[:, 0:NT], tr_bank[2][:, NT:2 * NT], 0.0, ALU.mult, ALU.add))
            link(v.tensor_tensor(out=off2[:, :], in0=off2[:, :], in1=tr_bank[2][:, NT:2 * NT], op=ALU.subtract))
            link(v.scalar_tensor_tensor(out=plug[:, :], in0=off2[:, :], scalar=-1.0, in1=tr_bank[2][:, 0:NT], op0=ALU.add, op1=ALU.add))
            v.tensor_scalar(plug_i[:, :], plug[:, :], 0.0, float(NC - 1), ALU.max, ALU.min).then_inc(plug_ready, 1)
            for k in range(2 * 4):
                blk, c = divmod(k, CC)
                n = min(4, CT - 4 * blk) * P
                cols = slice(blk * QB, blk * QB + n)
                v.wait_ge(ck_p0, k + 1)
                v.tensor_tensor(out=rest[k % 4][:, 0:n], in0=tr_bank[k % 4][:, 0:n], in1=CP[:, 0, c, cols], op=ALU.subtract).then_inc(ck_r1, 1)
                v.wait_ge(ck_p1, k + 1)
                v.tensor_tensor(out=CP[:, 2, c, cols], in0=rest[k % 4][:, 0:n], in1=CP[:, 1, c, cols], op=ALU.subtract).then_inc(ck_p2, 1)

            def update(u, t, o, bias, gate):
                link(v.tensor_tensor(out=tmp[u][:, :], in0=o, in1=bias, op=ALU.add))
                link(v.scalar_tensor_tensor(out=xnew[u][:, :], in0=tmp[u][:, :], scalar=gates[:, gate:gate + 1], in1=X[:, t, :], op0=ALU.mult, op1=ALU.add))
                link(v.bn_stats(bn[:, u, :], xnew[u][:, :]))
                v.tensor_scalar(X[:, t, :], xnew[u][:, :], 1.0, None, ALU.mult).then_inc(dve, 1)
                cnt[0] += 1
                link(v.bn_aggr(mvu[:, u, :], bn[:, u, :]))
                link(v.tensor_scalar(mv[:, t, :], mvu[:, u, :], 1.0, None, ALU.mult))

            def layernorm_scale(n):
                v.tensor_scalar(lnv[:, :], mv[:, :, 1], 1.0, LN_EPS, ALU.mult, ALU.add).then_inc(sqrt_in, 1)
                v.wait_ge(sqrt_out, n)
                link(v.reciprocal(rstd[:, :], lns[:, :]))

            def normalise(u, i, scale, done):
                t = i * U + u
                v.tensor_scalar(xs[u][:, :], X[:, t, :], mv[:, t, 0:1], scale[:, bass.ds(t, 1)],
                                ALU.subtract, ALU.mult).then_inc(done, 1)

            v.wait_ge(x_in, 16)
            mark()
            for t in range(NT):
                link(v.bn_stats(bn[:, t % U, :], X[:, t, :]))
                link(v.bn_aggr(mv[:, t, :], bn[:, t % U, :]))
            layernorm_scale(2)
            link(v.tensor_tensor(out=rstd2[:, :], in0=rstd[:, :], in1=rstd[:, :], op=ALU.mult))
            link(v.tensor_tensor(out=rstd2[:, :], in0=rstd2[:, :], in1=mv[:, :, 1], op=ALU.mult))
            v.tensor_scalar(lnv[:, :], rstd2[:, :], 1.0, 1e-5, ALU.mult, ALU.add).then_inc(sqrt_in, 1)
            v.wait_ge(sqrt_out, 3)
            link(v.reciprocal(rstd2[:, :], lns[:, :]))
            link(v.tensor_tensor(out=rstd[:, :], in0=rstd[:, :], in1=rstd2[:, :], op=ALU.mult))
            v.wait_ge(tanh_done, 1)
            v.wait_ge(gb_ready, 1)
            mark()
            with v.Fori(0, NT // U) as i:
                enter(i, 6 * U)
                for u in range(U):
                    normalise(u, i, rstd, ph["a", "xs_ready"])
                for u in range(U):
                    t = i * U + u
                    v.wait_ge(ph["a", "out_mm"], t + 1)
                    update(u, t, out_bank[u][:, 0:C], GB[:, t, :], 0)
            leave(NT // U, 6 * U)

            layernorm_scale(4)
            mark()
            with v.Fori(0, NT // U) as i:
                enter(i, 10 * U)
                for u in range(U):
                    normalise(u, i, rstd, ph["b", "xs_ready"])
                for u in range(U):
                    v.wait_ge(ph["b", "out_mm"], i * U + u + 1)
                    link(v.tensor_tensor(out=lg[u][:, :], in0=out_bank[u][:, C:C + R8], in1=b_rt[:, :], op=ALU.add))
                    link(v.reduce_max(lmx[u][:, :], lg[u][:, :], AX))
                    v.tensor_scalar(lg[u][:, :], lg[u][:, :], lmx[u][:, :], None, ALU.subtract).then_inc(lg_ready, 1)
                for u in range(U):
                    v.wait_ge(ex_ready, i * U + u + 1)
                    link(v.reciprocal(esum[u][:, :], esum[u][:, :]))
                    link(v.tensor_scalar(gate[u][:, :], ex[u][:, :], esum[u][:, :], None, ALU.mult))
                    v.tensor_tensor(out=m64[u][:, 0:R8, :],
                                    in0=out_bank[u][:, C + R8:C + 2 * R8].unsqueeze(1).to_broadcast([P, R8, R8]),
                                    in1=gate[u][:, :].unsqueeze(2).to_broadcast([P, R8, R8]), op=ALU.mult).then_inc(m64_ready, 1)
                for u in range(U):
                    t = i * U + u
                    v.wait_ge(lora_mm, t + 1)
                    update(u, t, out_bank[u][:, 0:C], b_b0[:, :], 1)
            leave(NT // U, 10 * U)

            layernorm_scale(5)
            mark()
            with v.Fori(0, NT // U) as i:
                enter(i, U)
                for u in range(U):
                    normalise(u, i, rstd, ph["c", "xs_ready"])
                for u in range(U):
                    cols = bass.ds(i * QB + u * P, P)
                    v.wait_ge(c_p0, i * U + u + 1)
                    v.tensor_tensor(out=rest[u][:, :].rearrange("p (k t) -> p k t", k=4),
                                    in0=out_bank[u].rearrange("p (k t) -> p k t", k=4), in1=PB[:, 0, :, cols],
                                    op=ALU.subtract).then_inc(c_r1, 1)
                    link(v.tensor_copy(V[:, i * U + u, :], tr_bank[u][:, C:2 * C]))
                for u in range(U):
                    cols = bass.ds(i * QB + u * P, P)
                    v.wait_ge(c_p1, i * U + u + 1)
                    v.tensor_tensor(out=PB[:, 2, :, cols], in0=rest[u][:, :].rearrange("p (k t) -> p k t", k=4),
                                    in1=PB[:, 1, :, cols], op=ALU.subtract).then_inc(c_p2, 1)
            leave(NT // U, U)

            v.wait_ge(qk_out, 16 * SLOTS * CC * 2 * (NT // U))
            v.wait_ge(ck_out, 16 * SLOTS * CC)

            def maxima(j, kt):
                for n in m_ops(kt):
                    c, q = divmod(n, 4 * G)
                    v.wait_ge(mx_mm, j * M_OPS + n + 1)
                    v.reduce_max(mp[:, q, c:c + 1], mx_ps[n % 2][:, 0:width(c)], AX).then_inc(mx_red, 1)

            def negated_maxima(j):
                v.wait_ge(mx_red, RED0 + (j + 1) * M_OPS)
                link(v.reduce_max(mm[:, :, :].rearrange("p t h -> p (t h)"), mp[:, :, :], AX))
                link(v.tensor_scalar(mst[:, :, 0, :], mm[:, :, :], -1.0, None, ALU.mult))
                link(v.scalar_tensor_tensor(out=mr[:, :, :], in0=mm[:, :, :], scalar=-1.0, in1=mst[:, :, 0, :], op0=ALU.mult, op1=ALU.subtract))
                link(v.tensor_copy(mst[:, :, 1, :], mr[:, :, :]))
                v.tensor_tensor(out=mst[:, :, 2, :], in0=mr[:, :, :], in1=mst[:, :, 1, :], op=ALU.subtract).then_inc(mst_ready, 1)
                v.wait_ge(mrow_mm, j + 1)
                if not (isinstance(j, int) and j == 0):
                    v.wait_ge(m_in, 16 * j)
                v.tensor_copy(mrow[:, :], tr_ps[0:3 * G, :]).then_inc(mrow_ready, 1)

            def evacuate(i):
                v.wait_ge(pv_mm, PV0 + KT * (i + 1))
                v.tensor_copy(oT[:, :], pv_ps[:, :]).then_inc(oT_ready, 1)

            def normalise_out(g, qb):
                i = g * NQ + qb
                v.wait_ge(oT_tr, i + 1)
                ps = tr_ps[:, :].rearrange("p (t h d) -> p t h d", t=4, h=G)
                link(v.reciprocal(rcp[:, :, :], ps[:, :, :, D]))
                v.tensor_tensor(out=attn[:, TOKB[qb], bass.ds(g * G * D, G * D)].rearrange("p t (h d) -> p t h d", h=G),
                                in0=ps[:, :, :, 0:D], in1=rcp[:, :, :].unsqueeze(3).to_broadcast([P, 4, G, D]),
                                op=ALU.mult).then_inc(norm_done, 1)

            v.sem_inc(mx_red, RED0)
            mark()
            enter(0, 0)
            for kt in range(KT):
                maxima(0, kt)
            negated_maxima(0)
            mark()

            def group(g, last):
                for qb in range(NQ):
                    i = g * NQ + qb
                    more = not (last and qb == NQ - 1)
                    for kt in range(KT):
                        if more:
                            maxima(i + 1, kt)
                        if kt == 0 and qb > 0:
                            evacuate(i - 1)
                        if kt == 2 and qb > 0:
                            normalise_out(g, qb - 1)
                    if more:
                        negated_maxima(i + 1)
                evacuate(g * NQ + NQ - 1)
                normalise_out(g, NQ - 1)

            per = 5 * NQ
            with v.Fori(0, NG - 1) as g:
                enter(g, per)
                group(g, False)
            leave(NG - 1, per)
            group(NG - 1, True)

            v.wait_ge(norm_done, NG * NQ)
            mark()
            with v.Fori(0, NT // U) as i:
                enter(i, 6 * U)
                for u in range(U):
                    v.tensor_copy(xs[u][:, :], attn[:, i * U + u, :]).then_inc(ph["e", "xs_ready"], 1)
                for u in range(U):
                    t = i * U + u
                    v.wait_ge(ph["e", "out_mm"], t + 1)
                    update(u, t, out_bank[u][:, 0:C], b_pr[:, :], 2)
            leave(NT // U, 6 * U)

            layernorm_scale(6)
            v.wait_ge(tok_in, 64)
            mark()
            with v.Fori(0, NQ) as b:
                enter(b, 2 * NP)
                for u in range(4):
                    normalise(u, b, rstd, f_xs)
                tok = bass.ds(b * QB, QB)
                for p in range(NP):
                    v.scalar_tensor_tensor(out=CB[:, p, :], in0=idx[:, 0, tok], scalar=ecol[:, p:p + 1], in1=wts[:, 0, tok],
                                           op0=ALU.is_equal, op1=ALU.mult)
                    link(v.scalar_tensor_tensor(out=CB1[:, :], in0=idx[:, 1, tok], scalar=ecol[:, p:p + 1], in1=wts[:, 1, tok],
                                                op0=ALU.is_equal, op1=ALU.mult))
                    link(v.tensor_tensor(out=CB[:, p, :], in0=CB[:, p, :], in1=CB1[:, :], op=ALU.add))
                for p in range(NP):
                    v.wait_ge(s3_mm, b * (NP * NF) + (p + 1) * NF)
                    v.tensor_tensor(out=Z[:, p, :], in0=(pv_ps, tr_ps)[p % 2][:, :], in1=CB[:, p, :], op=ALU.mult).then_inc(z_ready, 1)
                for u in range(4):
                    t = b * 4 + u
                    v.wait_ge(y_mm, t + 1)
                    v.scalar_tensor_tensor(out=X[:, t, :], in0=out_bank[u][:, 0:C], scalar=gates[:, 3:4],
                                           in1=X[:, t, :], op0=ALU.mult, op1=ALU.add).then_inc(y_done, 1)
            leave(NQ, 2 * NP)

        @block.tensor
        def _(pe):
            def mm2(o, l, r, start=True, stop=True):
                return pe.matmul(o, l, r, start=start, stop=stop)

            pe.wait_ge(consts_in, 32)
            pe.wait_ge(cum_in, 1)
            mm2(tr_bank[0][:, 0:CT], tri, mask_f[:, :])
            mm2(tr_bank[0][:, CT:2 * CT], ones, mask_f[:, :]).then_inc(cum_mm, 1)
            pe.wait_ge(pads_zero, 1)
            pe.wait_ge(hot_ready, CT)
            for t in range(NT):
                for j in range(CT):
                    r = P if j < CT - 1 else TAIL
                    ins = mm2(tr_bank[1][:, t:t + 1], HOT[0:r, j, t * P:(t + 1) * P], onesb[0:r, :], j == 0, j == CT - 1)
            ins.then_inc(cnt_mm, 1)
            pe.wait_ge(cum2_in, 1)
            mm2(tr_bank[2][:, 0:NT], tri, bnd[:, :])
            mm2(tr_bank[2][:, NT:2 * NT], ones, bnd[:, :]).then_inc(cum2_mm, 1)
            for j in range(CT):
                pe.wait_ge(u_ready, CT)
                if j >= 4:
                    pe.wait_ge(dep_ev, j - 3)
                ins = mm2(out_bank[j % 4][:, 0:C], lmat0, UU[:, j, :], True, j == 0)
                if j:
                    ins = mm2(out_bank[j % 4][:, 0:C], lmat1, UU[:, j - 1, :], False, True)
                ins.then_inc(dep_mm, 1)
            for k in range(2 * 4):
                blk, c = divmod(k, CC)
                if k >= 4:
                    pe.wait_ge(ck_p2, k - 3)
                elif k in (0, 1, 2):
                    pe.wait_ge(plug_ready, 1)
                for jj in range(min(4, CT - 4 * blk)):
                    ins = pe.transpose(tr_bank[k % 4][:, jj * P:(jj + 1) * P], CK[:, 4 * blk + jj, c * P:(c + 1) * P], ident)
                ins.then_inc(ck_tr, 1)
            pe.wait_ge(ck_p2, 8)

            def transposes(n, u, i):
                pe.wait_ge(ph[n, "xs_ready"], i * U + u + 1)
                for c in range(CC):
                    ins = pe.transpose(tr_bank[u][:, c * P:(c + 1) * P], xs[u][:, c * P:(c + 1) * P], ident)
                ins.then_inc(ph[n, "xT_mm"], 1)

            def project(n, u, i, w, stop=True):
                pe.wait_ge(ph[n, "hT_ready"], i * U + u + 1)
                for c in range(CC):
                    ins = mm2(out_bank[u][:, 0:C], hT[u][:, c, :], w[:, c, 0:C], c == 0, stop and c == CC - 1)
                return ins

            pe.wait_ge(weights_in, 16 * N_W)
            with pe.Fori(0, NT // U) as i:
                for u in range(U):
                    transposes("a", u, i)
                for u in range(U):
                    project("a", u, i, w_in).then_inc(ph["a", "out_mm"], 1)

            with pe.Fori(0, NT // U) as i:
                for u in range(U):
                    transposes("b", u, i)
                for u in range(U):
                    pe.wait_ge(ph["b", "hT_ready"], i * U + u + 1)
                    for c in range(CC):
                        mm2(out_bank[u][:, C:C + 2 * R8], hT[u][:, c, :], w_b0[:, c, C:C + 2 * R8], c == 0, c == CC - 1)
                    project("b", u, i, w_b0, stop=False).then_inc(ph["b", "out_mm"], 1)
                for u in range(U):
                    pe.wait_ge(m64_ready, i * U + u + 1)
                    pe.transpose(tr_bank[u][:, C:C + P], m64[u][:, :, :].rearrange("p e r -> p (e r)"), ident).then_inc(m64_tr, 1)
                for u in range(U):
                    pe.wait_ge(m64_ev, i * U + u + 1)
                    mm2(out_bank[u][:, 0:C], m64T[u][:, :], w_lb[:, :], False, True).then_inc(lora_mm, 1)

            with pe.Fori(0, NT // U) as i:
                for u in range(U):
                    transposes("c", u, i)
                for u in range(U):
                    pe.wait_ge(ph["c", "hT_ready"], i * U + u + 1)
                    for c in range(CC):
                        mm2(tr_bank[u][:, C:2 * C], hT[u][:, c, :], w_qkv[:, c, 2 * C:3 * C], c == 0, c == CC - 1)
                    for k in range(4):
                        for c in range(CC):
                            ins = mm2(out_bank[u][:, k * P:(k + 1) * P], w_qkv[:, c, k * P:(k + 1) * P], hT[u][:, c, :],
                                      c == 0, c == CC - 1)
                    ins.then_inc(ph["c", "out_mm"], 1)

            pe.wait_ge(c_p2, NT)
            pe.sem_inc(pv_mm, PV0)

            def maxima(j, qb, g, kt):
                for n in m_ops(kt):
                    c, q = divmod(n, 4 * G)
                    t, h = divmod(q, G)
                    if n == 0:
                        pe.wait_ge(q_in[qb], 16 * (g + 1))
                    if q == 0 and qb == 0:
                        pe.wait_ge(km_in[c], 16 * (g + 1))
                    pe.wait_ge(mx_red, RED0 + j * M_OPS + n - 1)
                    pe.matmul(mx_ps[n % 2][:, 0:width(c)], QS[qb][0:SR, h, t * P:(t + 1) * P],
                              KM[0:SR, h, c * CH:c * CH + width(c)], start=True, stop=True).then_inc(mx_mm, 1)

            def turn_maxima(j):
                pe.wait_ge(mst_ready, j + 1)
                for t in range(4):
                    ins = pe.matmul(tr_ps[0:3 * G, t * P:(t + 1) * P], mst[:, t, :, :].rearrange("p r h -> p (r h)"), ident_b[:, :],
                                    start=True, stop=True)
                ins.then_inc(mrow_mm, 1)

            def scores(g, qb, kt, p):
                i = g * NQ + qb
                r = rows(kt)
                if qb == 0 and p == 0 and kt % 4 == 0:
                    pe.wait_ge(kx_in[kt // 4], 16 * (g + 1))
                pe.wait_ge(exp_done, i * 2 * KT + 2 * kt + p - 1 + EXP0)
                for h in (2 * p, 2 * p + 1):
                    ins = pe.matmul(sc_ps[p][0:r, h % 2, :], KX[0:SR + 3, h, kt * P:kt * P + r], QS[qb][0:SR + 3, h, :],
                                    start=True, stop=True)
                ins.then_inc(qk_mm, 1)

            def weigh(g, qb, kt):
                i = g * NQ + qb
                r = rows(kt)
                if qb == 0 and kt % 4 == 0:
                    pe.wait_ge(vg_ready, g * NCH + kt // 4 + 1)
                pe.wait_ge(exp_done, i * 2 * KT + 2 * kt + 2 + EXP0)
                for h in range(G):
                    ins = pe.matmul(pv_ps[32 * h:32 * h + 32, :], Vg[0:r, kt, h, :], PX[kt % PR][0:r, h, :],
                                    start=kt == 0, stop=kt == KT - 1)
                ins.then_inc(pv_mm, 1)

            def turn_out(i):
                pe.wait_ge(oT_ready, i + 1)
                for t in range(4):
                    ins = pe.transpose(tr_ps[:, t * P:(t + 1) * P], oT[:, t * P:(t + 1) * P], ident)
                ins.then_inc(oT_tr, 1)

            for kt in range(KT):
                maxima(0, 0, 0, kt)
            turn_maxima(0)
            pe.wait_ge(fill_done, 2)

            def group(g, last):
                for qb in range(NQ):
                    i = g * NQ + qb
                    pe.wait_ge(m_in, 16 * (i + 1))
                    for kt in range(KT):
                        scores(g, qb, kt, 0)
                        scores(g, qb, kt, 1)
                        if kt:
                            if kt == 1 and qb:
                                pe.wait_ge(oT_ready, i)
                            weigh(g, qb, kt - 1)
                        elif qb:
                            weigh(g, qb - 1, KT - 1)
                        if not (last and qb == NQ - 1):
                            maxima(i + 1, (qb + 1) % NQ, g + (qb + 1) // NQ, kt)
                        if kt == 2 and qb:
                            pe.wait_ge(mrow_ready, i + 1)
                            turn_out(i - 1)
                        if kt == KT - 2 and not (last and qb == NQ - 1):
                            if qb:
                                pe.wait_ge(norm_done, i)
                            turn_maxima(i + 1)
                weigh(g, NQ - 1, KT - 1)
                turn_out(g * NQ + NQ - 1)
                pe.wait_ge(norm_done, (g + 1) * NQ)

            with pe.Fori(0, NG - 1) as g:
                group(g, False)
            group(NG - 1, True)

            with pe.Fori(0, NT // U) as i:
                for u in range(U):
                    transposes("e", u, i)
                for u in range(U):
                    project("e", u, i, w_pr).then_inc(ph["e", "out_mm"], 1)

            pe.wait_ge(moe_w_in, 16 * (E + 3))
            with pe.Fori(0, NQ) as b:
                for u in range(4):
                    pe.wait_ge(f_xs, b * 4 + u + 1)
                    for c in range(CC):
                        ins = pe.transpose(tr_bank[u][:, c * P:(c + 1) * P], xs[u][:, c * P:(c + 1) * P], ident)
                    ins.then_inc(f_tr, 1)
                pe.wait_ge(f_hT, b * 4 + 4)
                for p in range(NP):
                    if p >= 2:
                        pe.wait_ge(u_ev, b * NP + p - 1)
                    for c in range(CC):
                        ins = mm2(mx_ps[p % 2][:, :], w1a[:, c, p * P:(p + 1) * P], XT[:, c, :], c == 0, c == CC - 1)
                    ins.then_inc(s1_mm, 1)

                def up(p, f):
                    n = p * NF + f
                    if f == 0:
                        pe.wait_ge(u_ev, b * NP + p + 1)
                    if n >= 2:
                        pe.wait_ge(gelu_done, b * (NP * NF) + n - 1)
                    for e in range(2):
                        ins = mm2(sc_ps[f % 2][:, e, :], w1b[:, 2 * p + e, f * P:(f + 1) * P], UT[:, p, :])
                    ins.then_inc(s2_mm, 1)

                def down(p, f):
                    n = p * NF + f
                    if f == 0 and p >= 2:
                        pe.wait_ge(z_ready, b * NP + p - 1)
                    pe.wait_ge(gelu_done, b * (NP * NF) + n + 1)
                    for e in range(2):
                        ins = mm2((pv_ps, tr_ps)[p % 2][RK * e:RK * e + RK, :], w2a[:, f, 2 * p + e, :], GE[f % 2][:, e, :], f == 0, f == NF - 1)
                    ins.then_inc(s3_mm, 1)

                for n in range(NP * NF + 1):
                    if n < NP * NF:
                        up(*divmod(n, NF))
                    if n:
                        down(*divmod(n - 1, NF))
                pe.wait_ge(z_ready, b * NP + NP)
                for u in range(4):
                    for p in range(NP):
                        ins = mm2(out_bank[u][:, 0:C], Z[:, p, u * P:(u + 1) * P], w2b[:, p, :],
                                  p == 0, p == NP - 1)
                    ins.then_inc(y_mm, 1)


def constants():
    logp = np.float32(-1e-3)
    dt = np.float32(-np.log(-np.expm1(logp)))
    factor = np.float64(np.exp(-dt))
    c = np.zeros((P, C_ALL), np.float32)
    q, p = np.arange(P)[:, None], np.arange(P)[None, :]
    c[:, C_ID:C_ID + P] = q == p
    c[:, C_TRI:C_TRI + P] = q <= p
    c[:, C_ONE:C_ONE + P] = 1
    c[:, C_L0:C_L0 + P] = np.where(q <= p, factor ** np.maximum(p - q, 0), 0)
    c[:, C_L1:C_L1 + P] = factor ** (p + P - q)
    c[:, C_EC:C_EC + NP] = 2 * np.arange(NP)[None, :] + q // RK
    c[:, C_IOTA:] = np.arange(T)
    return c


def kernel(**inputs):
    import concourse.bacc as _bacc
    from concourse import mybir as _mybir
    from concourse.bass_utils import run_bass_kernel_spmd as _run

    x = {k: np.asarray(v) for k, v in inputs.items()}
    mask = np.zeros((CT * P,), np.int32)
    mask[:NC] = x["mask_BxS2_if0"][0]
    w1b = np.zeros((E, P, FF), np.float32)
    for e in range(E):
        w1b[e, RK * (e % 2):RK * (e % 2) + RK] = x["L1_ffn_w1_B"].reshape(E, RK, FF)[e]
    arrays = {
        "x": x["x"][0], "ctx": x["ctx_2048"][0], "mask": mask.reshape(CT, P).T, "consts": constants(),
        "gates": np.stack([x["g_xattn"], x["g_ffn"]], 1).reshape(1, 4),
        "w_in": x["L0_xattn_W_in"].T, "b_in": x["L0_xattn_b_in"][None], "g_res": x["L0_xattn_g_res"].reshape(CC, P).T,
        "g_ini": x["L0_xattn_g_init"][None, :C],
        "w_b0": np.concatenate([x["L0_ffn_base_w"].T, x["L0_ffn_router_w"].T, x["L0_ffn_lora_A"]], 1),
        "b_b0": x["L0_ffn_base_b"][None], "b_rt": x["L0_ffn_router_b"][None],
        "w_lb": x["L0_ffn_lora_B"].reshape(RK, C),
        "w_qkv": x["L1_xattn_w_qkv"].T, "w_pr": x["L1_xattn_w_proj"].T, "b_pr": x["L1_xattn_b_proj"][None],
        "idx": x["L1_ffn_expert_indices"].T, "wts": x["L1_ffn_expert_weights"].T,
        "w1a": x["L1_ffn_w1_A"].T, "w1b": w1b,
        "w2a": x["L1_ffn_w2_A"].reshape(E, RK, FF).transpose(2, 0, 1), "w2b": x["L1_ffn_w2_B"],
    }
    nc = _bacc.Bacc("TRN2", target_bir_lowering=False, num_devices=1)
    feeds, aps = {}, {}
    for name, arr in arrays.items():
        arr = np.ascontiguousarray(arr)
        feeds["in_" + name] = arr
        aps[name] = nc.dram_tensor("in_" + name, arr.shape, _mybir.dt.from_np(arr.dtype), kind="ExternalInput").ap()
    out = nc.dram_tensor("out_0", (T, C), _mybir.dt.float32, kind="ExternalOutput").ap()
    build(nc, aps, out)
    r = _run(nc, [feeds], core_ids=[0])
    return r.results[0]["out_0"].reshape(1, T, C)
```

```python
import math
from contextlib import ExitStack

import numpy as np

import concourse.bass as bass
from concourse import mybir

F32 = mybir.dt.float32
BF16 = mybir.dt.bfloat16
I32 = mybir.dt.int32
U32 = mybir.dt.uint32
ALU = mybir.AluOpType
ACT = mybir.ActivationFunctionType
AX = mybir.AxisListType.X

P = 128
T, C = 2048, 256
CC = C // P
NT = T // P
U = 4
NC = 1601
CT = -(-NC // P)
TAIL = NC - (CT - 1) * P
HEADS, D = 16, 16
G = 4
NG = HEADS // G
QB = 512
NQ = T // QB
KEYS = T + NC
KT = NT + CT
KPAD = KT * P
CH = 512
NCH = -(-KEYS // CH)
SLOTS = 6
K_PART = (0, 1, 2, 0, 1, 0)
Q_PART = (0, 0, 0, 1, 1, 2)
SR = SLOTS * D
E, RK, FF = 8, 64, 1024
NF = FF // P
NP = E // 2
R8 = 8
LN_EPS = 1e-5
PR = 3

C_ID, C_TRI, C_ONE, C_L0, C_L1, C_EC = 0, P, 2 * P, 3 * P, 4 * P, 5 * P
C_IOTA = C_EC + NP
C_ALL = C_IOTA + T


def width(c):
    return min(CH, KEYS - c * CH)


def rows(kt):
    return P if kt < KT - 1 else TAIL


def build(nc, a, out):
    logp = np.float32(-1e-3)
    dt = np.float32(-np.log(-np.expm1(logp)))
    u_scale = float(np.float32(dt * np.exp(logp)) / dt)

    qd = nc.dram_tensor("q_stack", (HEADS, SR, T), BF16)
    kd = nc.dram_tensor("k_stack", (HEADS, SR, KPAD), BF16)
    depool = nc.dram_tensor("depool", (CT * P, C), F32)

    ctx = ExitStack()
    with ctx:
        def sb(name, shape, dtype=F32, stack=ctx):
            return stack.enter_context(nc.sbuf_tensor(name, shape, dtype))

        def sem(name):
            return ctx.enter_context(nc.semaphore(name))

        sc_ps = [ctx.enter_context(nc.psum_tensor(f"sc_ps{i}", [P, 2, 512], F32)) for i in range(2)]
        pv_ps = ctx.enter_context(nc.psum_tensor("pv_ps", [P, 512], F32))
        mx_ps = [ctx.enter_context(nc.psum_tensor(f"mx_ps{i}", [P, 512], F32)) for i in range(3)]
        tr_ps = mx_ps[2]
        out_bank = [sc_ps[0][:, 0, :], sc_ps[0][:, 1, :], sc_ps[1][:, 0, :], sc_ps[1][:, 1, :]]
        tr_bank = [pv_ps[:, :], mx_ps[0][:, :], mx_ps[1][:, :], tr_ps[:, :]]

        X = sb("X", [P, NT, C])
        cst = sb("cst", [P, C_IOTA])
        ident, tri, ones = cst[:, C_ID:C_ID + P], cst[:, C_TRI:C_TRI + P], cst[:, C_ONE:C_ONE + P]
        lmat0, lmat1 = cst[:, C_L0:C_L0 + P], cst[:, C_L1:C_L1 + P]
        ident_b = sb("ident_b", [P, P], BF16)
        gates = sb("gates", [P, 4])
        gates_in = sb("gates_in", [P, 4])
        bn = sb("bn", [P, U, 6])
        mv = sb("mv", [P, NT, 2])
        lnv = sb("lnv", [P, NT])
        lns = sb("lns", [P, NT])
        rstd = sb("rstd", [P, NT])
        rstd2 = sb("rstd2", [P, NT])
        xs = [sb(f"xs{u}", [P, C]) for u in range(U)]
        hT = [sb(f"hT{u}", [P, CC, P]) for u in range(U)]
        tmp = [sb(f"tmp{u}", [P, C]) for u in range(U)]
        mvu = sb("mvu", [P, U, 2])
        xnew = [sb(f"xnew{u}", [P, C]) for u in range(U)]
        w_pr = sb("w_pr", [P, CC, C])
        b_pr = sb("b_pr", [P, C])
        attn = sb("attn", [P, NT, C])
        values = ExitStack()
        V = sb("V", [P, KT, C], F32, values)

        consts_in, x_in, ck_in, cv_in, mask_in = (sem(n) for n in ("consts_in", "x_in", "ck_in", "cv_in", "mask_in"))
        weights_in = sem("weights_in")
        pads_zero, dve, acte, idb_ready = sem("pads_zero"), sem("dve"), sem("acte"), sem("idb_ready")
        tanh_done, sq_done = sem("tanh_done"), sem("sq_done")
        sqrt_in, sqrt_out = sem("sqrt_in"), sem("sqrt_out")
        cum_in, cum_mm, hot_ready, cnt_mm, cum2_in, cum2_mm, plug_ready = (sem(n) for n in (
            "cum_in", "cum_mm", "hot_ready", "cnt_mm", "cum2_in", "cum2_mm", "plug_ready"))
        u_ready, dep_mm, dep_ev, dep_out, gathered, gb_ready = (sem(n) for n in (
            "u_ready", "dep_mm", "dep_ev", "dep_out", "gathered", "gb_ready"))
        ck_tr, ck_p0, ck_r1, ck_p1, ck_p2 = (sem(n) for n in ("ck_tr", "ck_p0", "ck_r1", "ck_p1", "ck_p2"))
        ck_out = sem("ck_out")
        ph = {}
        for n in "abce":
            for s in ("xs_ready", "xT_mm", "hT_ready", "out_mm"):
                ph[n, s] = sem(f"{n}_{s}")
        lg_ready, ex_ready, m64_ready, m64_tr, m64_ev, lora_mm = (sem(n) for n in (
            "lg_ready", "ex_ready", "m64_ready", "m64_tr", "m64_ev", "lora_mm"))
        c_p0, c_r1, c_p1, c_p2, qk_out = (sem(n) for n in ("c_p0", "c_r1", "c_p1", "c_p2", "qk_out"))
        km_in = [sem(f"km_in{c}") for c in range(NCH)]
        kx_in = [sem(f"kx_in{c}") for c in range(NCH)]
        q_in = [sem(f"q_in{i}") for i in range(NQ)]
        fill_done, vg_ready, qk_mm, exp_done, pv_mm, mx_mm, mx_red = (sem(n) for n in (
            "fill_done", "vg_ready", "qk_mm", "exp_done", "pv_mm", "mx_mm", "mx_red"))
        mst_ready, mrow_mm, mrow_ready, m_in, oT_ready, oT_tr, norm_done = (sem(n) for n in (
            "mst_ready", "mrow_mm", "mrow_ready", "m_in", "oT_ready", "oT_tr", "norm_done"))
        moe_w_in, tok_in, f_xs, f_tr, f_hT, s1_mm, u_ev, s2_mm, gelu_done, s3_mm, z_ready, y_mm, y_done, y_out = (
            sem(n) for n in ("moe_w_in", "tok_in", "f_xs", "f_tr", "f_hT", "s1_mm", "u_ev", "s2_mm",
                             "gelu_done", "s3_mm", "z_ready", "y_mm", "y_done", "y_out"))
        cb_base = None

        early = ExitStack()
        w_in = sb("w_in", [P, CC, C], F32, early)
        w_b0 = sb("w_b0", [P, CC, C + 2 * R8], F32, early)
        w_qkv = sb("w_qkv", [P, CC, 3 * C], F32, early)
        w_lb = sb("w_lb", [RK, C], F32, early)
        b_in, b_b0 = sb("b_in", [P, C], F32, early), sb("b_b0", [P, C], F32, early)
        b_rt = sb("b_rt", [P, R8], F32, early)
        g_ini = sb("g_ini", [P, C], F32, early)
        g_res = sb("g_res", [P, CC], F32, early)
        ss = sb("ss", [P, CT, 2], F32, early)
        crs = sb("crs", [P, CT], F32, early)
        crt = sb("crt", [P, CT], F32, early)
        sq_junk = sb("sq_junk", [P, C], F32, early)
        mask_i = sb("mask_i", [P, CT], I32, early)
        mask_f = sb("mask_f", [P, CT], F32, early)
        off = sb("off", [P, CT], F32, early)
        bidx = sb("bidx", [P, CT], F32, early)
        neg = sb("neg", [P, CT], F32, early)
        onesb = sb("onesb", [P, 1], BF16, early)
        bnd = sb("bnd", [P, NT], F32, early)
        off2 = sb("off2", [P, NT], F32, early)
        plug = sb("plug", [P, NT], F32, early)
        plug_i = sb("plug_i", [P, NT], U32, early)
        lg = [sb(f"lg{u}", [P, R8], F32, early) for u in range(U)]
        lmx = [sb(f"lmx{u}", [P, 1], F32, early) for u in range(U)]
        ex = [sb(f"ex{u}", [P, R8], F32, early) for u in range(U)]
        esum = [sb(f"esum{u}", [P, 1], F32, early) for u in range(U)]
        gate = [sb(f"gate{u}", [P, R8], BF16, early) for u in range(U)]
        m64 = [sb(f"m64{u}", [P, 2 * R8, R8], F32, early) for u in range(U)]
        m64T = [sb(f"m64T{u}", [RK, P], F32, early) for u in range(U)]
        later = ExitStack()
        PB = sb("PB", [P, 3, 4, T], BF16, later)
        CP = sb("CP", [P, 3, CC, CT * P], BF16, later)
        GB = sb("GB", [P, NT, C], F32, later)
        rest = [sb(f"rest{u}", [P, 4 * P], F32, later) for u in range(U)]
        later.close()
        iota = sb("iota", [P, T], F32, early)
        CK = sb("CK", [P, CT, C], F32, early)
        UU = sb("UU", [P, CT, C], F32, early)
        sb("to_PB_end", [P, 3 * 4 * T // 2 - T - 2 * CT * C], F32, early)
        HOT = sb("HOT", [P, CT, T], BF16, early)
        early.close()

        att = ExitStack()
        KM = sb("KM", [P, G, KEYS], BF16, att)
        KX = sb("KX", [P, G, KEYS], BF16, att)
        Vg = sb("Vg", [P, KT, G, 2 * D], F32, att)
        QS = [sb(f"QS{i}", [P, G, QB], BF16, att) for i in range(NQ)]
        PX = [sb(f"PX{i}", [P, G, QB], F32, att) for i in range(PR)]
        mp = sb("mp", [P, 4 * G, NCH], F32, att)
        mm = sb("mm", [P, 4, G], F32, att)
        mr = sb("mr", [P, 4, G], F32, att)
        mst = sb("mst", [P, 4, 3, G], BF16, att)
        mrow = sb("mrow", [3 * G, QB], BF16, att)
        oT = sb("oT", [P, QB], F32, att)
        rcp = sb("rcp", [P, 4, G], F32, att)
        att.close()
        values.close()

        moe = ExitStack()
        w1a = sb("w1a", [P, CC, E * RK], F32, moe)
        w1b = sb("w1b", [P, E, FF], F32, moe)
        w2a = sb("w2a", [P, NF, E, RK], F32, moe)
        w2b = sb("w2b", [P, NP, C], F32, moe)
        idx = sb("idx", [P, 2, T], I32, moe)
        wts = sb("wts", [P, 2, T], F32, moe)
        ecol = cst[:, C_EC:C_EC + NP]
        XT = sb("XT", [P, CC, QB], F32, moe)
        UT = sb("UT", [P, NP, QB], F32, moe)
        GE = [sb(f"GE{i}", [P, 2, QB], F32, moe) for i in range(2)]
        CB = sb("CB", [P, NP, QB], F32, moe)
        CB1 = sb("CB1", [P, QB], F32, moe)
        Z = sb("Z", [P, NP, QB], F32, moe)
        moe.close()

        block = ctx.enter_context(nc.Block())

        EXP0, PV0 = 2, 3

        def step_of(kt, i):
            if kt >= PR:
                return KT * i + kt - PR
            return KT * (i - 1) + max(k for k in range(KT) if k % PR == kt % PR)

        M_OPS = 4 * G * NCH
        LEAD = 4

        def m_ops(kt):
            at = range(M_OPS * (kt + LEAD) // KT, M_OPS * (kt + 1 + LEAD) // KT)
            return [(1 + n // M_OPS, n % M_OPS) for n in at]

        TURN = KT - LEAD

        ring = []
        for qb in range(NQ):
            for kt in range(KT):
                ring += [("m", qb, kt, k) for k in range(len(m_ops(kt)))]
                ring += [("out", qb, 2, 0)] * (kt == 2) + [("turn", qb, TURN, 0)] * (kt == TURN)
        ring += [None] * (-len(ring) % 3)
        ring_at = {use: n for n, use in enumerate(ring)}

        def ring_bank(use):
            return mx_ps[ring_at[use] % 3]

        def taken(g, last_use):
            kind, qb, kt, k = last_use
            i = g * NQ + qb
            known = isinstance(g, int)
            if kind == "m":
                ahead, n = m_ops(kt)[k]
                if known and not 0 <= i + ahead < NG * NQ:
                    return None
                return mx_red, (i + ahead) * M_OPS + n + 1
            if kind == "out":
                return None if known and i < 1 else (norm_done, i)
            return None if known and not 0 <= i + 1 < NG * NQ else (mrow_ready, i + 2)

        def wait_ring(pe, g, use):
            at = ring_at[use] - 3
            while at > -len(ring):
                before = ring[at]
                got = before and taken(g if at >= 0 else g - 1, before)
                if got:
                    pe.wait_ge(*got)
                    return
                at -= 3

        N_W = 13
        TOKB = [slice(4 * i, 4 * i + 4) for i in range(NQ)]

        @block.sync
        def _(sp):
            sp.dma_start(cst[:, :], a["consts"][:, 0:C_IOTA]).then_inc(consts_in, 16)
            sp.dma_start(mask_i[:, :], a["mask"]).then_inc(mask_in, 16)
            sp.dma_start(iota[:, :], a["consts"][:, C_IOTA:C_ALL]).then_inc(consts_in, 16)
            full = (CT - 1) * P
            sp.dma_start(CK[:, 0:CT - 1, :], a["ctx"][0:full, 0:C].rearrange("(j p) c -> p j c", p=P)).then_inc(ck_in, 16)
            sp.dma_start(V[:, NT:KT - 1, :], a["ctx"][0:full, C:2 * C].rearrange("(j p) c -> p j c", p=P)).then_inc(cv_in, 16)
            sp.wait_ge(pads_zero, 1)
            sp.dma_start(CK[0:TAIL, CT - 1, :], a["ctx"][full:NC, 0:C]).then_inc(ck_in, 16)
            sp.dma_start(V[0:TAIL, KT - 1, :], a["ctx"][full:NC, C:2 * C]).then_inc(cv_in, 16)
            sp.dma_start(X[:, :, :], a["x"].rearrange("(j p) c -> p j c", p=P)).then_inc(x_in, 16)
            sp.wait_ge(dep_ev, CT)
            sp.dma_start(depool.rearrange("(j p) c -> p j c", p=P), UU[:, :, :]).then_inc(dep_out, 16)
            sp.wait_ge(ck_p2, 2 * 4)
            for s in range(SLOTS):
                for c in range(CC):
                    sp.dma_start(kd[8 * c:8 * c + 8, D * s:D * s + D, T:KPAD], CP[:, K_PART[s], c, :]).then_inc(ck_out, 16)
            with sp.Fori(0, NT // U) as i:
                sp.wait_ge(c_p2, i * U + U)
                tok = bass.ds(i * QB, QB)
                for s in range(SLOTS):
                    for c in range(CC):
                        sp.dma_start(kd[8 * c:8 * c + 8, D * s:D * s + D, tok], PB[:, K_PART[s], CC + c, tok]).then_inc(qk_out, 16)
                        sp.dma_start(qd[8 * c:8 * c + 8, D * s:D * s + D, tok], PB[:, Q_PART[s], c, tok]).then_inc(qk_out, 16)

            sp.wait_ge(ck_out, 16 * SLOTS * CC)
            sp.wait_ge(qk_out, 16 * SLOTS * CC * 2 * (NT // U))
            sp.wait_ge(c_p2, NT)

            def load_q(g, qb):
                sp.dma_start(QS[qb][0:SR, :, :], qd[bass.ds(g * G, G), :, qb * QB:(qb + 1) * QB]
                             .rearrange("h p q -> p h q")).then_inc(q_in[qb], 16)

            def load_k(dst, done, g, c):
                cols = slice(c * CH, c * CH + width(c))
                sp.dma_start(dst[0:SR, :, cols], kd[bass.ds(g * G, G), :, cols].rearrange("h p k -> p h k")).then_inc(done[c], 16)

            def load_m(j):
                sp.wait_ge(mrow_ready, j + 1)
                sp.dma_start(QS[(j if isinstance(j, int) else 0) % NQ][SR:SR + 3, :, :], mrow[:, :]).then_inc(m_in, 16)

            load_q(0, 0)
            for c in range(NCH):
                load_k(KM, km_in, 0, c)
            load_q(0, 1)
            sp.wait_ge(fill_done, 1)
            for c in range(NCH):
                load_k(KX, kx_in, 0, c)
            load_m(0)

            def group(g, last):
                for qb in range(NQ):
                    i = g * NQ + qb
                    sp.wait_ge(qk_mm, i * 2 * KT + 1)
                    if not last or qb + 2 < NQ:
                        load_q(g + (qb + 2) // NQ, (qb + 2) % NQ)
                    if last and qb == NQ - 1:
                        continue
                    if qb == NQ - 2 and not last:
                        for c in range(NCH):
                            sp.wait_ge(mx_mm, (i + 1) * M_OPS + 4 * G * (c + 1))
                            load_k(KM, km_in, g + 1, c)
                    if qb == NQ - 1:
                        for c in range(NCH - 2):
                            sp.wait_ge(qk_mm, i * 2 * KT + 2 * 4 * (c + 1))
                            load_k(KX, kx_in, g + 1, c)
                    sp.wait_ge(mrow_ready, i + 2)
                    sp.dma_start(QS[(qb + 1) % NQ][SR:SR + 3, :, :], mrow[:, :]).then_inc(m_in, 16)
                    if qb == NQ - 1:
                        for c in range(NCH - 2, NCH):
                            sp.wait_ge(qk_mm, i * 2 * KT + min(2 * 4 * (c + 1), 2 * KT))
                            load_k(KX, kx_in, g + 1, c)

            group(0, False)
            with sp.Fori(1, NG - 1) as g:
                group(g, False)
            group(NG - 1, True)

            sp.wait_ge(norm_done, NG * NQ)
            sp.dma_start(w1a[:, :, :], a["w1a"].rearrange("(c p) n -> p c n", p=P)).then_inc(moe_w_in, 16)
            for e in range(E):
                sp.dma_start(w1b[:, e, :], a["w1b"][e]).then_inc(moe_w_in, 16)
            sp.dma_start(w2a[:, :, :, :], a["w2a"].rearrange("(f p) e r -> p f e r", p=P)).then_inc(moe_w_in, 16)
            sp.dma_start(w2b[:, :, :], a["w2b"].rearrange("(a p) c -> p a c", p=P)).then_inc(moe_w_in, 16)
            for k in range(2):
                sp.dma_start(idx[:, k, :], a["idx"][k:k + 1, :].to_broadcast([P, T])).then_inc(tok_in, 16)
                sp.dma_start(wts[:, k, :], a["wts"][k:k + 1, :].to_broadcast([P, T])).then_inc(tok_in, 16)
            with sp.Fori(0, NQ) as b:
                sp.wait_ge(y_done, b * 4 + 4)
                sp.dma_start(out.rearrange("(j p) c -> p j c", p=P)[:, bass.ds(b * 4, 4), :],
                             X[:, bass.ds(b * 4, 4), :]).then_inc(y_out, 16)
            sp.wait_ge(y_out, 16 * NQ)

        @block.gpsimd
        def _(pool):
            pool.memset(CK[:, CT - 1, :], 0.0)
            pool.memset(V[:, KT - 1, :], 0.0)
            for u in range(U):
                pool.memset(m64[u][:, R8:2 * R8, :], 0.0)
            pool.memset(onesb[:, :], 1.0).then_inc(pads_zero, 1)
            pool.wait_ge(dep_out, 16)
            pool.wait_ge(plug_ready, 1)
            for t in range(NT):
                pool.indirect_dma_start(out=GB[:, t, :], out_offset=None, in_=depool[:, :],
                                        in_offset=bass.IndirectOffsetOnAxis(ap=plug_i[:, t:t + 1], axis=0)).then_inc(gathered, 16)
            pool.wait_ge(gathered, 16 * NT)
            pool.wait_ge(weights_in, 16 * N_W)
            pool.tensor_tensor(out=GB[:, :, :], in0=GB[:, :, :], in1=b_in[:, :].unsqueeze(1).to_broadcast([P, NT, C]),
                               op=ALU.add).then_inc(gb_ready, 1)
            pool.wait_ge(c_p2, NT)
            pool.wait_ge(qk_out, 16 * SLOTS * CC * 2 * (NT // U))
            pool.wait_ge(ck_out, 16 * SLOTS * CC)
            pool.memset(KX[SR:SR + 32, :, :], 1.0).then_inc(fill_done, 1)
            pool.wait_ge(fill_done, 1)
            pool.memset(Vg[:, :, :, D:2 * D], 1.0).then_inc(fill_done, 1)
            pool.wait_ge(cv_in, 32)

            def copy_v(g, c):
                n = min(4, KT - 4 * c)
                r = P if 4 * c + n < KT else TAIL
                src = V[0:r, 4 * c:4 * c + n, bass.ds(g * G * D, G * D)].rearrange("p k (h d) -> p k h d", h=G)
                pool.tensor_copy(Vg[0:r, 4 * c:4 * c + n, :, 0:D], src).then_inc(vg_ready, 1)

            for c in range(NCH):
                copy_v(0, c)
            with pool.Fori(0, NG - 1) as g:
                for c in range(NCH):
                    pool.wait_ge(pv_mm, g * (NQ * KT) + (NQ - 1) * KT + min(4 * c + 4, KT) + PV0)
                    copy_v(g + 1, c)

        @block.scalar
        def _(act):
            act.dma_start(gates_in[:, 0:4], a["gates"].to_broadcast([P, 4])).then_inc(weights_in, 16)
            act.dma_start(w_in[:, :, :], a["w_in"].rearrange("(c p) n -> p c n", p=P)).then_inc(weights_in, 16)
            act.dma_start(w_b0[:, :, :], a["w_b0"].rearrange("(c p) n -> p c n", p=P)).then_inc(weights_in, 16)
            act.dma_start(w_qkv[:, :, :], a["w_qkv"].rearrange("(c p) n -> p c n", p=P)).then_inc(weights_in, 16)
            act.dma_start(w_pr[:, :, :], a["w_pr"].rearrange("(c p) n -> p c n", p=P)).then_inc(weights_in, 16)
            act.dma_start(w_lb[:, :], a["w_lb"]).then_inc(weights_in, 16)
            act.dma_start(b_in[:, :], a["b_in"].to_broadcast([P, C])).then_inc(weights_in, 16)
            act.dma_start(b_b0[:, :], a["b_b0"].to_broadcast([P, C])).then_inc(weights_in, 16)
            act.dma_start(b_pr[:, :], a["b_pr"].to_broadcast([P, C])).then_inc(weights_in, 16)
            act.dma_start(b_rt[:, :], a["b_rt"].to_broadcast([P, R8])).then_inc(weights_in, 16)
            act.dma_start(g_ini[:, :], a["g_ini"].to_broadcast([P, C])).then_inc(weights_in, 16)
            act.dma_start(g_res[:, :], a["g_res"]).then_inc(weights_in, 16)
            act.dma_start(bn[:, 0, :], a["consts"][:, 0:6]).then_inc(weights_in, 16)
            act.wait_ge(weights_in, 16 * N_W)
            act.activation(gates[:, :], gates_in[:, :], ACT.Tanh).then_inc(tanh_done, 1)
            act.wait_ge(ck_in, 32)
            act.wait_ge(cv_in, 32)
            for j in range(CT):
                for h, src in enumerate((CK[:, j, :], V[:, NT + j, :])):
                    act.activation(sq_junk[:, :], src, ACT.Square, accum_out=ss[:, j, h:h + 1]).then_inc(sq_done, 1)
                    act.wait_ge(sq_done, 2 * j + h + 1)

            def sqrt(dst, src, n):
                act.wait_ge(sqrt_in, n)
                act.activation(dst, src, ACT.Sqrt).then_inc(sqrt_out, 1)

            sqrt(crt[:, :], crs[:, :], 1)
            for j in range(CT):
                act.wait_ge(dep_mm, min(j + 2, CT))
                act.activation(UU[:, j, :], out_bank[j % 4][:, 0:C], ACT.Copy).then_inc(dep_ev, 1)
            for k in range(2 * 4):
                blk, c = divmod(k, CC)
                n = min(4, CT - 4 * blk) * P
                cols = slice(blk * QB, blk * QB + n)
                act.wait_ge(ck_tr, k + 1)
                act.activation(CP[:, 0, c, cols], tr_bank[k % 4][:, 0:n], ACT.Copy).then_inc(ck_p0, 1)
                act.wait_ge(ck_r1, k + 1)
                act.activation(CP[:, 1, c, cols], rest[k % 4][:, 0:n], ACT.Copy).then_inc(ck_p1, 1)

            sqrt(lns[:, :], lnv[:, :], 2)
            sqrt(lns[:, :], lnv[:, :], 3)
            with act.Fori(0, NT // U) as i:
                for u in range(U):
                    act.wait_ge(ph["a", "xT_mm"], i * U + u + 1)
                    for c in range(CC):
                        ins = act.activation(hT[u][:, c, :], tr_bank[u][:, c * P:(c + 1) * P], ACT.Copy, scale=g_res[:, c:c + 1])
                    ins.then_inc(ph["a", "hT_ready"], 1)

            def copy_hT(n, u, i):
                act.wait_ge(ph[n, "xT_mm"], i * U + u + 1)
                act.activation(hT[u][:, :, :].rearrange("p c t -> p (c t)"), tr_bank[u][:, 0:C], ACT.Copy).then_inc(ph[n, "hT_ready"], 1)

            sqrt(lns[:, :], lnv[:, :], 4)
            with act.Fori(0, NT // U) as i:
                for u in range(U):
                    copy_hT("b", u, i)
                for u in range(U):
                    act.wait_ge(lg_ready, i * U + u + 1)
                    act.activation(ex[u][:, :], lg[u][:, :], ACT.Exp, accum_out=esum[u][:, :]).then_inc(ex_ready, 1)
                for u in range(U):
                    act.wait_ge(m64_tr, i * U + u + 1)
                    act.activation(m64T[u][:, :], tr_bank[u][0:RK, C:C + P], ACT.Copy, scale=2.0).then_inc(m64_ev, 1)

            sqrt(lns[:, :], lnv[:, :], 5)
            with act.Fori(0, NT // U) as i:
                for u in range(U):
                    copy_hT("c", u, i)
                for u in range(U):
                    cols = bass.ds(i * QB + u * P, P)
                    act.wait_ge(ph["c", "out_mm"], i * U + u + 1)
                    act.activation(PB[:, 0, :, cols], out_bank[u].rearrange("p (k t) -> p k t", k=4), ACT.Copy).then_inc(c_p0, 1)
                for u in range(U):
                    cols = bass.ds(i * QB + u * P, P)
                    act.wait_ge(c_r1, i * U + u + 1)
                    act.activation(PB[:, 1, :, cols], rest[u][:, :].rearrange("p (k t) -> p k t", k=4), ACT.Copy).then_inc(c_p1, 1)

            act.wait_ge(qk_out, 16 * SLOTS * CC * 2 * (NT // U))
            act.wait_ge(ck_out, 16 * SLOTS * CC)
            act.wait_ge(c_p2, NT)
            act.sem_inc(exp_done, EXP0)

            def block_exps(g, qb):
                i = g * NQ + qb
                for kt in range(KT):
                    r = rows(kt)
                    for p in range(2):
                        if p == 0:
                            act.wait_ge(pv_mm, PV0 + step_of(kt, i) + 1)
                        act.wait_ge(qk_mm, i * 2 * KT + 2 * kt + p + 1)
                        act.activation(PX[kt % PR][0:r, 2 * p:2 * p + 2, :], sc_ps[p][0:r, :, :], ACT.Exp,
                                       scale=D ** -0.5).then_inc(exp_done, 1)

            with act.Fori(0, NG) as g:
                for qb in range(NQ):
                    block_exps(g, qb)

            with act.Fori(0, NT // U) as i:
                for u in range(U):
                    copy_hT("e", u, i)

            sqrt(lns[:, :], lnv[:, :], 6)
            with act.Fori(0, NQ) as b:
                for u in range(4):
                    act.wait_ge(f_tr, b * 4 + u + 1)
                    act.activation(XT[:, :, u * P:(u + 1) * P], tr_bank[u][:, 0:C].rearrange("p (c t) -> p c t", c=CC),
                                   ACT.Copy).then_inc(f_hT, 1)
                for p in range(NP):
                    act.wait_ge(s1_mm, b * NP + p + 1)
                    act.activation(UT[:, p, :], mx_ps[p % 2][:, :], ACT.Copy).then_inc(u_ev, 1)
                for p in range(NP):
                    for f in range(NF):
                        act.wait_ge(s2_mm, b * (NP * NF) + p * NF + f + 1)
                        act.activation(GE[f % 2][:, :, :], sc_ps[f % 2][:, :, :], ACT.Gelu).then_inc(gelu_done, 1)

        @block.vector
        def _(v):
            cnt = [0]
            base = [0]

            def link(ins):
                cnt[0] += 1
                ins.then_inc(dve, 1)
                v.wait_ge(dve, base[0] + cnt[0])

            def enter(i, per):
                base[0] = fixed[0] + i * per
                cnt[0] = 0

            def leave(n, per):
                assert cnt[0] == per, (cnt[0], per)
                fixed[0] += n * per
                base[0], cnt[0] = fixed[0], 0

            def mark():
                fixed[0] = base[0] + cnt[0]

            fixed = [0]

            v.wait_ge(consts_in, 32)
            link(v.tensor_copy(ident_b[:, :], ident))
            v.wait_ge(mask_in, 16)
            v.tensor_copy(mask_f[:, :], mask_i[:, :]).then_inc(cum_in, 1)
            v.wait_ge(cum_mm, 1)
            link(v.tensor_tensor_scan(off[:, :], ones[:, 0:CT], tr_bank[0][:, CT:2 * CT], 0.0, ALU.mult, ALU.add))
            link(v.tensor_tensor(out=off[:, :], in0=off[:, :], in1=tr_bank[0][:, CT:2 * CT], op=ALU.subtract))
            link(v.scalar_tensor_tensor(out=bidx[:, :], in0=off[:, :], scalar=-1.0, in1=tr_bank[0][:, 0:CT], op0=ALU.add, op1=ALU.add))
            link(v.tensor_scalar(neg[:, :], bidx[:, :], 0.0, float(T), ALU.is_lt, ALU.mult))
            link(v.tensor_tensor(out=bidx[:, :], in0=bidx[:, :], in1=neg[:, :], op=ALU.add))
            for j in range(CT):
                v.tensor_scalar(HOT[:, j, :], iota[:, :], bidx[:, j:j + 1], None, ALU.is_equal).then_inc(hot_ready, 1)
            v.wait_ge(sq_done, 2 * CT)
            link(v.tensor_tensor(out=crs[:, :], in0=ss[:, :, 0], in1=ss[:, :, 1], op=ALU.add))
            v.tensor_scalar(crs[:, :], crs[:, :], 1.0 / (2 * C), 1e-5, ALU.mult, ALU.add).then_inc(sqrt_in, 1)
            v.wait_ge(sqrt_out, 1)
            link(v.reciprocal(crs[:, :], crt[:, :]))
            link(v.tensor_scalar(crs[:, :], crs[:, :], u_scale, None, ALU.mult))
            v.wait_ge(weights_in, 16 * N_W)
            for j in range(CT):
                v.scalar_tensor_tensor(out=UU[:, j, :], in0=CK[:, j, :], scalar=crs[:, j:j + 1], in1=g_ini[:, :],
                                       op0=ALU.mult, op1=ALU.mult).then_inc(u_ready, 1)
            v.wait_ge(cnt_mm, 1)
            v.tensor_scalar(bnd[:, :], tr_bank[1][:, 0:NT], 1.0, None, ALU.min).then_inc(cum2_in, 1)
            v.wait_ge(cum2_mm, 1)
            link(v.tensor_tensor_scan(off2[:, :], ones[:, 0:NT], tr_bank[2][:, NT:2 * NT], 0.0, ALU.mult, ALU.add))
            link(v.tensor_tensor(out=off2[:, :], in0=off2[:, :], in1=tr_bank[2][:, NT:2 * NT], op=ALU.subtract))
            link(v.scalar_tensor_tensor(out=plug[:, :], in0=off2[:, :], scalar=-1.0, in1=tr_bank[2][:, 0:NT], op0=ALU.add, op1=ALU.add))
            v.tensor_scalar(plug_i[:, :], plug[:, :], 0.0, float(NC - 1), ALU.max, ALU.min).then_inc(plug_ready, 1)
            for k in range(2 * 4):
                blk, c = divmod(k, CC)
                n = min(4, CT - 4 * blk) * P
                cols = slice(blk * QB, blk * QB + n)
                v.wait_ge(ck_p0, k + 1)
                v.tensor_tensor(out=rest[k % 4][:, 0:n], in0=tr_bank[k % 4][:, 0:n], in1=CP[:, 0, c, cols], op=ALU.subtract).then_inc(ck_r1, 1)
                v.wait_ge(ck_p1, k + 1)
                v.tensor_tensor(out=CP[:, 2, c, cols], in0=rest[k % 4][:, 0:n], in1=CP[:, 1, c, cols], op=ALU.subtract).then_inc(ck_p2, 1)

            def update(u, t, o, bias, gate):
                link(v.tensor_tensor(out=tmp[u][:, :], in0=o, in1=bias, op=ALU.add))
                link(v.scalar_tensor_tensor(out=xnew[u][:, :], in0=tmp[u][:, :], scalar=gates[:, gate:gate + 1], in1=X[:, t, :], op0=ALU.mult, op1=ALU.add))
                link(v.bn_stats(bn[:, u, :], xnew[u][:, :]))
                v.tensor_scalar(X[:, t, :], xnew[u][:, :], 1.0, None, ALU.mult).then_inc(dve, 1)
                cnt[0] += 1
                link(v.bn_aggr(mvu[:, u, :], bn[:, u, :]))
                link(v.tensor_scalar(mv[:, t, :], mvu[:, u, :], 1.0, None, ALU.mult))

            def layernorm_scale(n):
                v.tensor_scalar(lnv[:, :], mv[:, :, 1], 1.0, LN_EPS, ALU.mult, ALU.add).then_inc(sqrt_in, 1)
                v.wait_ge(sqrt_out, n)
                link(v.reciprocal(rstd[:, :], lns[:, :]))

            def normalise(u, i, scale, done):
                t = i * U + u
                v.tensor_scalar(xs[u][:, :], X[:, t, :], mv[:, t, 0:1], scale[:, bass.ds(t, 1)],
                                ALU.subtract, ALU.mult).then_inc(done, 1)

            v.wait_ge(x_in, 16)
            mark()
            for t in range(NT):
                link(v.bn_stats(bn[:, t % U, :], X[:, t, :]))
                link(v.bn_aggr(mv[:, t, :], bn[:, t % U, :]))
            layernorm_scale(2)
            link(v.tensor_tensor(out=rstd2[:, :], in0=rstd[:, :], in1=rstd[:, :], op=ALU.mult))
            link(v.tensor_tensor(out=rstd2[:, :], in0=rstd2[:, :], in1=mv[:, :, 1], op=ALU.mult))
            v.tensor_scalar(lnv[:, :], rstd2[:, :], 1.0, 1e-5, ALU.mult, ALU.add).then_inc(sqrt_in, 1)
            v.wait_ge(sqrt_out, 3)
            link(v.reciprocal(rstd2[:, :], lns[:, :]))
            link(v.tensor_tensor(out=rstd[:, :], in0=rstd[:, :], in1=rstd2[:, :], op=ALU.mult))
            v.wait_ge(tanh_done, 1)
            v.wait_ge(gb_ready, 1)
            mark()
            with v.Fori(0, NT // U) as i:
                enter(i, 6 * U)
                for u in range(U):
                    normalise(u, i, rstd, ph["a", "xs_ready"])
                for u in range(U):
                    t = i * U + u
                    v.wait_ge(ph["a", "out_mm"], t + 1)
                    update(u, t, out_bank[u][:, 0:C], GB[:, t, :], 0)
            leave(NT // U, 6 * U)

            layernorm_scale(4)
            mark()
            with v.Fori(0, NT // U) as i:
                enter(i, 10 * U)
                for u in range(U):
                    normalise(u, i, rstd, ph["b", "xs_ready"])
                for u in range(U):
                    v.wait_ge(ph["b", "out_mm"], i * U + u + 1)
                    link(v.tensor_tensor(out=lg[u][:, :], in0=out_bank[u][:, C:C + R8], in1=b_rt[:, :], op=ALU.add))
                    link(v.reduce_max(lmx[u][:, :], lg[u][:, :], AX))
                    v.tensor_scalar(lg[u][:, :], lg[u][:, :], lmx[u][:, :], None, ALU.subtract).then_inc(lg_ready, 1)
                for u in range(U):
                    v.wait_ge(ex_ready, i * U + u + 1)
                    link(v.reciprocal(esum[u][:, :], esum[u][:, :]))
                    link(v.tensor_scalar(gate[u][:, :], ex[u][:, :], esum[u][:, :], None, ALU.mult))
                    v.tensor_tensor(out=m64[u][:, 0:R8, :],
                                    in0=out_bank[u][:, C + R8:C + 2 * R8].unsqueeze(1).to_broadcast([P, R8, R8]),
                                    in1=gate[u][:, :].unsqueeze(2).to_broadcast([P, R8, R8]), op=ALU.mult).then_inc(m64_ready, 1)
                for u in range(U):
                    t = i * U + u
                    v.wait_ge(lora_mm, t + 1)
                    update(u, t, out_bank[u][:, 0:C], b_b0[:, :], 1)
            leave(NT // U, 10 * U)

            layernorm_scale(5)
            mark()
            with v.Fori(0, NT // U) as i:
                enter(i, U)
                for u in range(U):
                    normalise(u, i, rstd, ph["c", "xs_ready"])
                for u in range(U):
                    cols = bass.ds(i * QB + u * P, P)
                    v.wait_ge(c_p0, i * U + u + 1)
                    v.tensor_tensor(out=rest[u][:, :].rearrange("p (k t) -> p k t", k=4),
                                    in0=out_bank[u].rearrange("p (k t) -> p k t", k=4), in1=PB[:, 0, :, cols],
                                    op=ALU.subtract).then_inc(c_r1, 1)
                    link(v.tensor_copy(V[:, i * U + u, :], tr_bank[u][:, C:2 * C]))
                for u in range(U):
                    cols = bass.ds(i * QB + u * P, P)
                    v.wait_ge(c_p1, i * U + u + 1)
                    v.tensor_tensor(out=PB[:, 2, :, cols], in0=rest[u][:, :].rearrange("p (k t) -> p k t", k=4),
                                    in1=PB[:, 1, :, cols], op=ALU.subtract).then_inc(c_p2, 1)
            leave(NT // U, U)

            v.wait_ge(qk_out, 16 * SLOTS * CC * 2 * (NT // U))
            v.wait_ge(ck_out, 16 * SLOTS * CC)

            def maxima(g, qb, kt, part=slice(0, None)):
                for k, (ahead, n) in list(enumerate(m_ops(kt)))[part]:
                    if isinstance(g, int) and not 0 <= g * NQ + qb + ahead < NG * NQ:
                        continue
                    c, q = divmod(n, 4 * G)
                    v.wait_ge(mx_mm, (g * NQ + qb + ahead) * M_OPS + n + 1)
                    v.reduce_max(mp[:, q, c:c + 1], ring_bank(("m", qb, kt, k))[:, 0:width(c)], AX).then_inc(mx_red, 1)

            def negated_maxima(j):
                v.wait_ge(mx_red, (j + 1) * M_OPS)
                link(v.reduce_max(mm[:, :, :].rearrange("p t h -> p (t h)"), mp[:, :, :], AX))
                link(v.tensor_scalar(mst[:, :, 0, :], mm[:, :, :], -1.0, None, ALU.mult))
                link(v.scalar_tensor_tensor(out=mr[:, :, :], in0=mm[:, :, :], scalar=-1.0, in1=mst[:, :, 0, :], op0=ALU.mult, op1=ALU.subtract))
                link(v.tensor_copy(mst[:, :, 1, :], mr[:, :, :]))
                v.tensor_tensor(out=mst[:, :, 2, :], in0=mr[:, :, :], in1=mst[:, :, 1, :], op=ALU.subtract).then_inc(mst_ready, 1)

            def keep_turned(j, qb):
                v.wait_ge(mrow_mm, j + 1)
                if not (isinstance(j, int) and j == 0):
                    v.wait_ge(m_in, 16 * j)
                v.tensor_copy(mrow[:, :], ring_bank(("turn", qb, TURN, 0))[0:3 * G, :]).then_inc(mrow_ready, 1)

            def evacuate(i):
                v.wait_ge(pv_mm, PV0 + KT * (i + 1))
                v.tensor_copy(oT[:, :], pv_ps[:, :]).then_inc(oT_ready, 1)

            def normalise_out(g, qb, bank):
                i = g * NQ + qb
                v.wait_ge(oT_tr, i + 1)
                ps = bank[:, :].rearrange("p (t h d) -> p t h d", t=4, h=G)
                link(v.reciprocal(rcp[:, :, :], ps[:, :, :, D]))
                v.tensor_tensor(out=attn[:, TOKB[qb], bass.ds(g * G * D, G * D)].rearrange("p t (h d) -> p t h d", h=G),
                                in0=ps[:, :, :, 0:D], in1=rcp[:, :, :].unsqueeze(3).to_broadcast([P, 4, G, D]),
                                op=ALU.mult).then_inc(norm_done, 1)

            def group(g, blocks=range(NQ), steps=range(KT), exps=True):
                for qb in blocks:
                    i = g * NQ + qb
                    known = isinstance(g, int)
                    follows = not (known and i + 1 >= NG * NQ)
                    behind = exps and not (known and i == 0)
                    for kt in steps:
                        maxima(g, qb, kt, slice(0, 1))
                        if kt == 3 and behind:
                            normalise_out(g - (qb == 0), (qb - 1) % NQ, ring_bank(("out", qb, 2, 0)))
                        if kt == TURN + 1 and follows:
                            keep_turned(i + 1, qb)
                        maxima(g, qb, kt, slice(1, None))
                        if kt == 0 and behind:
                            evacuate(i - 1)
                        if kt == TURN - 1 and follows:
                            negated_maxima(i + 1)

            for kt in range(TURN, KT):
                maxima(-1, NQ - 2, kt)
            group(-1, [NQ - 1], range(KT), False)

            group(0)
            mark()
            per = 5 * NQ
            with v.Fori(1, NG - 1) as g:
                enter(g - 1, per)
                group(g)
            leave(NG - 2, per)
            group(NG - 1)
            evacuate(NG * NQ - 1)
            normalise_out(NG - 1, NQ - 1, mx_ps[0])

            v.wait_ge(norm_done, NG * NQ)
            mark()
            with v.Fori(0, NT // U) as i:
                enter(i, 6 * U)
                for u in range(U):
                    v.tensor_copy(xs[u][:, :], attn[:, i * U + u, :]).then_inc(ph["e", "xs_ready"], 1)
                for u in range(U):
                    t = i * U + u
                    v.wait_ge(ph["e", "out_mm"], t + 1)
                    update(u, t, out_bank[u][:, 0:C], b_pr[:, :], 2)
            leave(NT // U, 6 * U)

            layernorm_scale(6)
            v.wait_ge(tok_in, 64)
            mark()
            with v.Fori(0, NQ) as b:
                enter(b, 2 * NP)
                for u in range(4):
                    normalise(u, b, rstd, f_xs)
                tok = bass.ds(b * QB, QB)
                for p in range(NP):
                    v.scalar_tensor_tensor(out=CB[:, p, :], in0=idx[:, 0, tok], scalar=ecol[:, p:p + 1], in1=wts[:, 0, tok],
                                           op0=ALU.is_equal, op1=ALU.mult)
                    link(v.scalar_tensor_tensor(out=CB1[:, :], in0=idx[:, 1, tok], scalar=ecol[:, p:p + 1], in1=wts[:, 1, tok],
                                                op0=ALU.is_equal, op1=ALU.mult))
                    link(v.tensor_tensor(out=CB[:, p, :], in0=CB[:, p, :], in1=CB1[:, :], op=ALU.add))
                for p in range(NP):
                    v.wait_ge(s3_mm, b * (NP * NF) + (p + 1) * NF)
                    v.tensor_tensor(out=Z[:, p, :], in0=(pv_ps, tr_ps)[p % 2][:, :], in1=CB[:, p, :], op=ALU.mult).then_inc(z_ready, 1)
                for u in range(4):
                    t = b * 4 + u
                    v.wait_ge(y_mm, t + 1)
                    v.scalar_tensor_tensor(out=X[:, t, :], in0=out_bank[u][:, 0:C], scalar=gates[:, 3:4],
                                           in1=X[:, t, :], op0=ALU.mult, op1=ALU.add).then_inc(y_done, 1)
            leave(NQ, 2 * NP)

        @block.tensor
        def _(pe):
            def mm2(o, l, r, start=True, stop=True):
                return pe.matmul(o, l, r, start=start, stop=stop)

            pe.wait_ge(consts_in, 32)
            pe.wait_ge(cum_in, 1)
            mm2(tr_bank[0][:, 0:CT], tri, mask_f[:, :])
            mm2(tr_bank[0][:, CT:2 * CT], ones, mask_f[:, :]).then_inc(cum_mm, 1)
            pe.wait_ge(pads_zero, 1)
            pe.wait_ge(hot_ready, CT)
            for t in range(NT):
                for j in range(CT):
                    r = P if j < CT - 1 else TAIL
                    ins = mm2(tr_bank[1][:, t:t + 1], HOT[0:r, j, t * P:(t + 1) * P], onesb[0:r, :], j == 0, j == CT - 1)
            ins.then_inc(cnt_mm, 1)
            pe.wait_ge(cum2_in, 1)
            mm2(tr_bank[2][:, 0:NT], tri, bnd[:, :])
            mm2(tr_bank[2][:, NT:2 * NT], ones, bnd[:, :]).then_inc(cum2_mm, 1)
            for j in range(CT):
                pe.wait_ge(u_ready, CT)
                if j >= 4:
                    pe.wait_ge(dep_ev, j - 3)
                ins = mm2(out_bank[j % 4][:, 0:C], lmat0, UU[:, j, :], True, j == 0)
                if j:
                    ins = mm2(out_bank[j % 4][:, 0:C], lmat1, UU[:, j - 1, :], False, True)
                ins.then_inc(dep_mm, 1)
            for k in range(2 * 4):
                blk, c = divmod(k, CC)
                if k >= 4:
                    pe.wait_ge(ck_p2, k - 3)
                elif k in (0, 1, 2):
                    pe.wait_ge(plug_ready, 1)
                for jj in range(min(4, CT - 4 * blk)):
                    ins = pe.transpose(tr_bank[k % 4][:, jj * P:(jj + 1) * P], CK[:, 4 * blk + jj, c * P:(c + 1) * P], ident)
                ins.then_inc(ck_tr, 1)
            pe.wait_ge(ck_p2, 8)

            def transposes(n, u, i):
                pe.wait_ge(ph[n, "xs_ready"], i * U + u + 1)
                for c in range(CC):
                    ins = pe.transpose(tr_bank[u][:, c * P:(c + 1) * P], xs[u][:, c * P:(c + 1) * P], ident)
                ins.then_inc(ph[n, "xT_mm"], 1)

            def project(n, u, i, w, stop=True):
                pe.wait_ge(ph[n, "hT_ready"], i * U + u + 1)
                for c in range(CC):
                    ins = mm2(out_bank[u][:, 0:C], hT[u][:, c, :], w[:, c, 0:C], c == 0, stop and c == CC - 1)
                return ins

            pe.wait_ge(weights_in, 16 * N_W)
            with pe.Fori(0, NT // U) as i:
                for u in range(U):
                    transposes("a", u, i)
                for u in range(U):
                    project("a", u, i, w_in).then_inc(ph["a", "out_mm"], 1)

            with pe.Fori(0, NT // U) as i:
                for u in range(U):
                    transposes("b", u, i)
                for u in range(U):
                    pe.wait_ge(ph["b", "hT_ready"], i * U + u + 1)
                    for c in range(CC):
                        mm2(out_bank[u][:, C:C + 2 * R8], hT[u][:, c, :], w_b0[:, c, C:C + 2 * R8], c == 0, c == CC - 1)
                    project("b", u, i, w_b0, stop=False).then_inc(ph["b", "out_mm"], 1)
                for u in range(U):
                    pe.wait_ge(m64_ready, i * U + u + 1)
                    pe.transpose(tr_bank[u][:, C:C + P], m64[u][:, :, :].rearrange("p e r -> p (e r)"), ident).then_inc(m64_tr, 1)
                for u in range(U):
                    pe.wait_ge(m64_ev, i * U + u + 1)
                    mm2(out_bank[u][:, 0:C], m64T[u][:, :], w_lb[:, :], False, True).then_inc(lora_mm, 1)

            with pe.Fori(0, NT // U) as i:
                for u in range(U):
                    transposes("c", u, i)
                for u in range(U):
                    pe.wait_ge(ph["c", "hT_ready"], i * U + u + 1)
                    for c in range(CC):
                        mm2(tr_bank[u][:, C:2 * C], hT[u][:, c, :], w_qkv[:, c, 2 * C:3 * C], c == 0, c == CC - 1)
                    for k in range(4):
                        for c in range(CC):
                            ins = mm2(out_bank[u][:, k * P:(k + 1) * P], w_qkv[:, c, k * P:(k + 1) * P], hT[u][:, c, :],
                                      c == 0, c == CC - 1)
                    ins.then_inc(ph["c", "out_mm"], 1)

            pe.wait_ge(c_p2, NT)
            pe.sem_inc(pv_mm, PV0)

            def maxima(g, qb, kt, part):
                for k, (ahead, n) in list(enumerate(m_ops(kt)))[part]:
                    if isinstance(g, int) and not 0 <= g * NQ + qb + ahead < NG * NQ:
                        continue
                    c, q = divmod(n, 4 * G)
                    t, h = divmod(q, G)
                    gj, qj = g + (qb + ahead) // NQ, (qb + ahead) % NQ
                    if n == 0:
                        pe.wait_ge(q_in[qj], 16 * (gj + 1))
                    if q == 0 and qj == 0:
                        pe.wait_ge(km_in[c], 16 * (gj + 1))
                    wait_ring(pe, g, ("m", qb, kt, k))
                    pe.matmul(ring_bank(("m", qb, kt, k))[:, 0:width(c)], QS[qj][0:SR, h, t * P:(t + 1) * P],
                              KM[0:SR, h, c * CH:c * CH + width(c)], start=True, stop=True).then_inc(mx_mm, 1)

            def turn_maxima(g, qb):
                pe.wait_ge(mst_ready, g * NQ + qb + 2)
                use = ("turn", qb, TURN, 0)
                wait_ring(pe, g, use)
                for t in range(4):
                    ins = pe.matmul(ring_bank(use)[0:3 * G, t * P:(t + 1) * P], mst[:, t, :, :].rearrange("p r h -> p (r h)"), ident_b[:, :],
                                    start=True, stop=True)
                ins.then_inc(mrow_mm, 1)

            def scores(g, qb, kt, p):
                i = g * NQ + qb
                r = rows(kt)
                if qb == 0 and p == 0 and kt % 4 == 0:
                    pe.wait_ge(kx_in[kt // 4], 16 * (g + 1))
                pe.wait_ge(exp_done, i * 2 * KT + 2 * kt + p - 1 + EXP0)
                for h in (2 * p, 2 * p + 1):
                    ins = pe.matmul(sc_ps[p][0:r, h % 2, :], KX[0:SR + 3, h, kt * P:kt * P + r], QS[qb][0:SR + 3, h, :],
                                    start=True, stop=True)
                ins.then_inc(qk_mm, 1)

            def weigh(g, qb, kt):
                i = g * NQ + qb
                r = rows(kt)
                if qb == 0 and kt % 4 == 0:
                    pe.wait_ge(vg_ready, g * NCH + kt // 4 + 1)
                pe.wait_ge(exp_done, i * 2 * KT + 2 * kt + 2 + EXP0)
                for h in range(G):
                    ins = pe.matmul(pv_ps[32 * h:32 * h + 32, :], Vg[0:r, kt, h, :], PX[kt % PR][0:r, h, :],
                                    start=kt == 0, stop=kt == KT - 1)
                ins.then_inc(pv_mm, 1)

            def turn_out(i, bank):
                pe.wait_ge(oT_ready, i + 1)
                for t in range(4):
                    ins = pe.transpose(bank[:, t * P:(t + 1) * P], oT[:, t * P:(t + 1) * P], ident)
                ins.then_inc(oT_tr, 1)

            for kt in range(TURN, KT):
                maxima(-1, NQ - 2, kt, slice(0, None))
            for kt in range(KT):
                maxima(-1, NQ - 1, kt, slice(0, None))
                if kt == TURN:
                    turn_maxima(-1, NQ - 1)
            pe.wait_ge(fill_done, 2)

            def group(g):
                for qb in range(NQ):
                    i = g * NQ + qb
                    known = isinstance(g, int)
                    follows = not (known and i + 1 >= NG * NQ)
                    behind = not (known and i == 0)
                    pe.wait_ge(m_in, 16 * (i + 1))
                    for kt in range(KT):
                        scores(g, qb, kt, 0)
                        maxima(g, qb, kt, slice(0, 1))
                        scores(g, qb, kt, 1)
                        maxima(g, qb, kt, slice(1, 3))
                        if kt:
                            if kt == 1 and behind:
                                pe.wait_ge(oT_ready, i)
                            weigh(g, qb, kt - 1)
                        elif behind:
                            weigh(g - (qb == 0), (qb - 1) % NQ, KT - 1)
                        maxima(g, qb, kt, slice(3, None))
                        if kt == 2 and behind:
                            wait_ring(pe, g, ("out", qb, 2, 0))
                            turn_out(i - 1, ring_bank(("out", qb, 2, 0)))
                        if kt == TURN and follows:
                            turn_maxima(g, qb)

            group(0)
            with pe.Fori(1, NG - 1) as g:
                group(g)
            group(NG - 1)
            weigh(NG - 1, NQ - 1, KT - 1)
            pe.wait_ge(mx_red, NG * NQ * M_OPS)
            pe.wait_ge(mrow_ready, NG * NQ)
            pe.wait_ge(norm_done, NG * NQ - 1)
            turn_out(NG * NQ - 1, mx_ps[0])
            pe.wait_ge(norm_done, NG * NQ)

            with pe.Fori(0, NT // U) as i:
                for u in range(U):
                    transposes("e", u, i)
                for u in range(U):
                    project("e", u, i, w_pr).then_inc(ph["e", "out_mm"], 1)

            pe.wait_ge(moe_w_in, 16 * (E + 3))
            with pe.Fori(0, NQ) as b:
                for u in range(4):
                    pe.wait_ge(f_xs, b * 4 + u + 1)
                    for c in range(CC):
                        ins = pe.transpose(tr_bank[u][:, c * P:(c + 1) * P], xs[u][:, c * P:(c + 1) * P], ident)
                    ins.then_inc(f_tr, 1)
                pe.wait_ge(f_hT, b * 4 + 4)
                for p in range(NP):
                    if p >= 2:
                        pe.wait_ge(u_ev, b * NP + p - 1)
                    for c in range(CC):
                        ins = mm2(mx_ps[p % 2][:, :], w1a[:, c, p * P:(p + 1) * P], XT[:, c, :], c == 0, c == CC - 1)
                    ins.then_inc(s1_mm, 1)

                def up(p, f):
                    n = p * NF + f
                    if f == 0:
                        pe.wait_ge(u_ev, b * NP + p + 1)
                    if n >= 2:
                        pe.wait_ge(gelu_done, b * (NP * NF) + n - 1)
                    for e in range(2):
                        ins = mm2(sc_ps[f % 2][:, e, :], w1b[:, 2 * p + e, f * P:(f + 1) * P], UT[:, p, :])
                    ins.then_inc(s2_mm, 1)

                def down(p, f):
                    n = p * NF + f
                    if f == 0 and p >= 2:
                        pe.wait_ge(z_ready, b * NP + p - 1)
                    pe.wait_ge(gelu_done, b * (NP * NF) + n + 1)
                    for e in range(2):
                        ins = mm2((pv_ps, tr_ps)[p % 2][RK * e:RK * e + RK, :], w2a[:, f, 2 * p + e, :], GE[f % 2][:, e, :], f == 0, f == NF - 1)
                    ins.then_inc(s3_mm, 1)

                for n in range(NP * NF + 1):
                    if n < NP * NF:
                        up(*divmod(n, NF))
                    if n:
                        down(*divmod(n - 1, NF))
                pe.wait_ge(z_ready, b * NP + NP)
                for u in range(4):
                    for p in range(NP):
                        ins = mm2(out_bank[u][:, 0:C], Z[:, p, u * P:(u + 1) * P], w2b[:, p, :],
                                  p == 0, p == NP - 1)
                    ins.then_inc(y_mm, 1)


def constants():
    logp = np.float32(-1e-3)
    dt = np.float32(-np.log(-np.expm1(logp)))
    factor = np.float64(np.exp(-dt))
    c = np.zeros((P, C_ALL), np.float32)
    q, p = np.arange(P)[:, None], np.arange(P)[None, :]
    c[:, C_ID:C_ID + P] = q == p
    c[:, C_TRI:C_TRI + P] = q <= p
    c[:, C_ONE:C_ONE + P] = 1
    c[:, C_L0:C_L0 + P] = np.where(q <= p, factor ** np.maximum(p - q, 0), 0)
    c[:, C_L1:C_L1 + P] = factor ** (p + P - q)
    c[:, C_EC:C_EC + NP] = 2 * np.arange(NP)[None, :] + q // RK
    c[:, C_IOTA:] = np.arange(T)
    return c


def kernel(**inputs):
    import concourse.bacc as _bacc
    from concourse import mybir as _mybir
    from concourse.bass_utils import run_bass_kernel_spmd as _run

    x = {k: np.asarray(v) for k, v in inputs.items()}
    mask = np.zeros((CT * P,), np.int32)
    mask[:NC] = x["mask_BxS2_if0"][0]
    w1b = np.zeros((E, P, FF), np.float32)
    for e in range(E):
        w1b[e, RK * (e % 2):RK * (e % 2) + RK] = x["L1_ffn_w1_B"].reshape(E, RK, FF)[e]
    arrays = {
        "x": x["x"][0], "ctx": x["ctx_2048"][0], "mask": mask.reshape(CT, P).T, "consts": constants(),
        "gates": np.stack([x["g_xattn"], x["g_ffn"]], 1).reshape(1, 4),
        "w_in": x["L0_xattn_W_in"].T, "b_in": x["L0_xattn_b_in"][None], "g_res": x["L0_xattn_g_res"].reshape(CC, P).T,
        "g_ini": x["L0_xattn_g_init"][None, :C],
        "w_b0": np.concatenate([x["L0_ffn_base_w"].T, x["L0_ffn_router_w"].T, x["L0_ffn_lora_A"]], 1),
        "b_b0": x["L0_ffn_base_b"][None], "b_rt": x["L0_ffn_router_b"][None],
        "w_lb": x["L0_ffn_lora_B"].reshape(RK, C),
        "w_qkv": x["L1_xattn_w_qkv"].T, "w_pr": x["L1_xattn_w_proj"].T, "b_pr": x["L1_xattn_b_proj"][None],
        "idx": x["L1_ffn_expert_indices"].T, "wts": x["L1_ffn_expert_weights"].T,
        "w1a": x["L1_ffn_w1_A"].T, "w1b": w1b,
        "w2a": x["L1_ffn_w2_A"].reshape(E, RK, FF).transpose(2, 0, 1), "w2b": x["L1_ffn_w2_B"],
    }
    nc = _bacc.Bacc("TRN2", target_bir_lowering=False, num_devices=1)
    feeds, aps = {}, {}
    for name, arr in arrays.items():
        arr = np.ascontiguousarray(arr)
        feeds["in_" + name] = arr
        aps[name] = nc.dram_tensor("in_" + name, arr.shape, _mybir.dt.from_np(arr.dtype), kind="ExternalInput").ap()
    out = nc.dram_tensor("out_0", (T, C), _mybir.dt.float32, kind="ExternalOutput").ap()
    build(nc, aps, out)
    r = _run(nc, [feeds], core_ids=[0])
    return r.results[0]["out_0"].reshape(1, T, C)
```

```python
import math
from contextlib import ExitStack

import numpy as np

import concourse.bass as bass
from concourse import mybir

F32 = mybir.dt.float32
BF16 = mybir.dt.bfloat16
I32 = mybir.dt.int32
U32 = mybir.dt.uint32
ALU = mybir.AluOpType
ACT = mybir.ActivationFunctionType
AX = mybir.AxisListType.X

P = 128
T, C = 2048, 256
CC = C // P
NT = T // P
U = 4
NC = 1601
CT = -(-NC // P)
TAIL = NC - (CT - 1) * P
HEADS, D = 16, 16
G = 4
NG = HEADS // G
QB = 512
NQ = T // QB
KEYS = T + NC
KT = NT + CT
KPAD = KT * P
CH = 512
NCH = -(-KEYS // CH)
SLOTS = 6
K_RUNS = ((0, 3), (0, 2), (0, 1))
Q_RUNS = ((0, 3), (1, 2), (2, 1))
K_LOADS, Q_LOADS = len(K_RUNS), SLOTS
SR = SLOTS * D
E, RK, FF = 8, 64, 1024
NF = FF // P
NP = E // 2
R8 = 8
LN_EPS = 1e-5
PR = 3

C_ID, C_TRI, C_ONE, C_L0, C_L1, C_EC = 0, P, 2 * P, 3 * P, 4 * P, 5 * P
C_ALL = C_EC + NP


def width(c):
    return min(CH, KEYS - c * CH)


def rows(kt):
    return P if kt < KT - 1 else TAIL


def build(nc, a, out):
    logp = np.float32(-1e-3)
    dt = np.float32(-np.log(-np.expm1(logp)))
    u_scale = float(np.float32(dt * np.exp(logp)) / dt)

    qd = nc.dram_tensor("q_parts", (3 * D, HEADS, T), BF16)
    kd = nc.dram_tensor("k_parts", (3 * D, HEADS, KPAD), BF16)
    depool = nc.dram_tensor("depool", (CT * P, C), F32)

    ctx = ExitStack()
    with ctx:
        def sb(name, shape, dtype=F32, stack=ctx):
            return stack.enter_context(nc.sbuf_tensor(name, shape, dtype))

        def sem(name):
            return ctx.enter_context(nc.semaphore(name))

        sc_ps = [ctx.enter_context(nc.psum_tensor(f"sc_ps{i}", [P, 2, 512], F32)) for i in range(2)]
        pv_ps = ctx.enter_context(nc.psum_tensor("pv_ps", [P, 512], F32))
        mx_ps = [ctx.enter_context(nc.psum_tensor(f"mx_ps{i}", [P, 512], F32)) for i in range(3)]
        tr_ps = mx_ps[2]
        out_bank = [sc_ps[0][:, 0, :], sc_ps[0][:, 1, :], sc_ps[1][:, 0, :], sc_ps[1][:, 1, :]]
        tr_bank = [pv_ps[:, :], mx_ps[0][:, :], mx_ps[1][:, :], tr_ps[:, :]]

        X = sb("X", [P, NT, C])
        cst = sb("cst", [P, C_ALL])
        ident, tri, ones = cst[:, C_ID:C_ID + P], cst[:, C_TRI:C_TRI + P], cst[:, C_ONE:C_ONE + P]
        lmat0, lmat1 = cst[:, C_L0:C_L0 + P], cst[:, C_L1:C_L1 + P]
        ident_b = sb("ident_b", [P, P], BF16)
        gates = sb("gates", [P, 4])
        gates_in = sb("gates_in", [P, 4])
        bn = sb("bn", [P, U, 6])
        mv = sb("mv", [P, NT, 2])
        lnv = sb("lnv", [P, NT])
        lns = sb("lns", [P, NT])
        rstd = sb("rstd", [P, NT])
        rstd2 = sb("rstd2", [P, NT])
        xs = [sb(f"xs{u}", [P, C]) for u in range(U)]
        hT = [sb(f"hT{u}", [P, CC, P]) for u in range(U)]
        tmp = [sb(f"tmp{u}", [P, C]) for u in range(U)]
        mvu = sb("mvu", [P, U, 2])
        xnew = [sb(f"xnew{u}", [P, C]) for u in range(U)]
        w_pr = sb("w_pr", [P, CC, C])
        b_pr = sb("b_pr", [P, C])
        attn = sb("attn", [P, NT, C])
        values = ExitStack()
        V = sb("V", [P, KT, C], F32, values)

        consts_in, x_in, ck_in, cv_in, mask_in = (sem(n) for n in ("consts_in", "x_in", "ck_in", "cv_in", "mask_in"))
        weights_in, late_w_in, iota_ready = sem("weights_in"), sem("late_w_in"), sem("iota_ready")
        pads_zero, dve, acte, idb_ready = sem("pads_zero"), sem("dve"), sem("acte"), sem("idb_ready")
        tanh_done, sq_done = sem("tanh_done"), sem("sq_done")
        sqrt_in, sqrt_out = sem("sqrt_in"), sem("sqrt_out")
        cum_in, cum_mm, hot_ready, cnt_mm, cum2_in, cum2_mm, plug_ready = (sem(n) for n in (
            "cum_in", "cum_mm", "hot_ready", "cnt_mm", "cum2_in", "cum2_mm", "plug_ready"))
        u_ready, dep_mm, dep_ev, dep_out, gathered = (sem(n) for n in ("u_ready", "dep_mm", "dep_ev", "dep_out", "gathered"))
        ck_tr, ck_p0, ck_r1, ck_p1, ck_p2 = (sem(n) for n in ("ck_tr", "ck_p0", "ck_r1", "ck_p1", "ck_p2"))
        ck_out = sem("ck_out")
        ph = {}
        for n in "abce":
            for s in ("xs_ready", "xT_mm", "hT_ready", "out_mm"):
                ph[n, s] = sem(f"{n}_{s}")
        lg_ready, ex_ready, m64_ready, m64_tr, m64_ev, lora_mm = (sem(n) for n in (
            "lg_ready", "ex_ready", "m64_ready", "m64_tr", "m64_ev", "lora_mm"))
        c_p0, c_r1, c_p1, c_p2 = (sem(n) for n in ("c_p0", "c_r1", "c_p1", "c_p2"))
        qk_out = [sem(f"qk_out{b}") for b in range(NT // U)]
        km_in = [sem(f"km_in{c}") for c in range(NCH)]
        kx_in = [sem(f"kx_in{c}") for c in range(NCH)]
        q_in = [sem(f"q_in{i}") for i in range(NQ)]
        fill_done, vg_ready, qk_mm, exp_done, pv_mm, mx_mm, mx_red = (sem(n) for n in (
            "fill_done", "vg_ready", "qk_mm", "exp_done", "pv_mm", "mx_mm", "mx_red"))
        mst_ready, mrow_mm, mrow_ready, m_in, oT_ready, oT_tr, norm_done = (sem(n) for n in (
            "mst_ready", "mrow_mm", "mrow_ready", "m_in", "oT_ready", "oT_tr", "norm_done"))
        moe_w_in, tok_in, f_xs, f_tr, f_hT, s1_mm, u_ev, s2_mm, gelu_done, s3_mm, z_ready, y_mm, y_done, y_out = (
            sem(n) for n in ("moe_w_in", "tok_in", "f_xs", "f_tr", "f_hT", "s1_mm", "u_ev", "s2_mm",
                             "gelu_done", "s3_mm", "z_ready", "y_mm", "y_done", "y_out"))

        early = ExitStack()
        w_in = sb("w_in", [P, CC, C], F32, early)
        w_b0 = sb("w_b0", [P, CC, C + 2 * R8], F32, early)
        w_qkv = sb("w_qkv", [P, CC, 3 * C], F32, early)
        w_lb = sb("w_lb", [RK, C], F32, early)
        b_in, b_b0 = sb("b_in", [P, C], F32, early), sb("b_b0", [P, C], F32, early)
        b_rt = sb("b_rt", [P, R8], F32, early)
        g_ini = sb("g_ini", [P, C], F32, early)
        g_res = sb("g_res", [P, CC], F32, early)
        ss = sb("ss", [P, CT], F32, early)
        bnc = sb("bnc", [P, CT, 6], F32, early)
        mvc = sb("mvc", [P, CT, 2], F32, early)
        crs = sb("crs", [P, CT], F32, early)
        crt = sb("crt", [P, CT], F32, early)
        sq_junk = sb("sq_junk", [P, C], F32, early)
        mask_i = sb("mask_i", [P, CT], I32, early)
        mask_f = sb("mask_f", [P, CT], F32, early)
        off = sb("off", [P, CT], F32, early)
        bidx = sb("bidx", [P, CT], F32, early)
        neg = sb("neg", [P, CT], F32, early)
        bnd = sb("bnd", [P, NT], F32, early)
        off2 = sb("off2", [P, NT], F32, early)
        plug = sb("plug", [P, NT], F32, early)
        plug_i = sb("plug_i", [P, NT], U32, early)
        lg = [sb(f"lg{u}", [P, R8], F32, early) for u in range(U)]
        lmx = [sb(f"lmx{u}", [P, 1], F32, early) for u in range(U)]
        ex = [sb(f"ex{u}", [P, R8], F32, early) for u in range(U)]
        esum = [sb(f"esum{u}", [P, 1], F32, early) for u in range(U)]
        gate = [sb(f"gate{u}", [P, R8], BF16, early) for u in range(U)]
        m64 = [sb(f"m64{u}", [P, 2 * R8, R8], F32, early) for u in range(U)]
        m64T = [sb(f"m64T{u}", [RK, P], F32, early) for u in range(U)]
        later = ExitStack()
        PB = sb("PB", [P, 3, 4, T], BF16, later)
        CP = sb("CP", [P, 3, CC, CT * P], BF16, later)
        GB = sb("GB", [P, NT, C], F32, later)
        rest = [sb(f"rest{u}", [P, 4 * P], F32, later) for u in range(U)]
        later.close()
        iota = sb("iota", [P, P], F32, early)
        CK = sb("CK", [P, CT, C], F32, early)
        UU = sb("UU", [P, CT, C], F32, early)
        sb("to_PB_end", [P, 3 * 4 * T // 2 - P - 2 * CT * C], F32, early)
        low, high = sb("low", [P, CT], F32, early), sb("high", [P, CT], F32, early)
        bidx_i, low_i, high_i = (sb(n, [P, CT], I32, early) for n in ("bidx_i", "low_i", "high_i"))
        hot_low = sb("hot_low", [P, CT, P], BF16, early)
        hot_high = sb("hot_high", [P, CT, NT], BF16, early)
        early.close()

        att = ExitStack()
        KX = sb("KX", [P, G, KEYS], BF16, att)
        Vg = sb("Vg", [P, KT, G, 2 * D], F32, att)
        PX = [sb(f"PX{i}", [P, G, QB], F32, att) for i in range(PR)]
        oT = sb("oT", [P, QB], F32, att)
        mp = sb("mp", [P, 4 * G, NCH], F32, att)
        mm = sb("mm", [P, 4, G], F32, att)
        mr = sb("mr", [P, 4, G], F32, att)
        mst = sb("mst", [P, 4, 3, G], BF16, att)
        mrow = sb("mrow", [3 * G, QB], BF16, att)
        rcp = sb("rcp", [P, 4, G], F32, att)
        KM = sb("KM", [P, G, KEYS], BF16, att)
        QS = [sb(f"QS{i}", [P, G, QB], BF16, att) for i in range(NQ)]
        att.close()
        values.close()

        moe = ExitStack()
        w1a = sb("w1a", [P, CC, E * RK], F32, moe)
        w1b = sb("w1b", [P, E, FF], F32, moe)
        w2a = sb("w2a", [P, NF, E, RK], F32, moe)
        w2b = sb("w2b", [P, NP, C], F32, moe)
        idx = sb("idx", [P, 2, T], I32, moe)
        wts = sb("wts", [P, 2, T], F32, moe)
        ecol = cst[:, C_EC:C_EC + NP]
        XT = sb("XT", [P, CC, T], F32, moe)
        UT = sb("UT", [P, NP, QB], F32, moe)
        GE = [sb(f"GE{i}", [P, 2, QB], F32, moe) for i in range(2)]
        CB = sb("CB", [P, NP, QB], F32, moe)
        CB1 = sb("CB1", [P, QB], F32, moe)
        Z = sb("Z", [P, NP, QB], F32, moe)
        moe.close()

        block = ctx.enter_context(nc.Block())

        EXP0, PV0, Y0 = 2, 3, 1

        def step_of(kt, i):
            if kt >= PR:
                return KT * i + kt - PR
            return KT * (i - 1) + max(k for k in range(KT) if k % PR == kt % PR)

        M_OPS = 4 * G * NCH
        FIRST = T // CH
        NARROW = NCH - 1
        M_ORDER = [(c, q) for c in [*range(FIRST, NARROW), *range(FIRST)] for q in range(4 * G)]
        for q in range(4 * G):
            M_ORDER.insert(8 + 7 * q, (NARROW, q))
        M_FREE = [M_ORDER.index((c, 4 * G - 1)) + 1 for c in range(NCH)]
        LEAD = 4

        def m_ops(kt):
            at = range(M_OPS * (kt + LEAD) // KT, M_OPS * (kt + 1 + LEAD) // KT)
            return [(1 + n // M_OPS, n % M_OPS) for n in at]

        NEGATE = KT - LEAD
        TURN = NEGATE + 1

        ring = []
        for qb in range(NQ):
            for kt in range(KT):
                ring += [("m", qb, kt, k) for k in range(len(m_ops(kt)))]
                ring += [("out", qb, 2, 0)] * (kt == 2) + [("turn", qb, TURN, 0)] * (kt == TURN)
        ring += [None] * (-len(ring) % 3)
        ring_at = {use: n for n, use in enumerate(ring)}

        def ring_bank(use):
            return mx_ps[ring_at[use] % 3]

        def taken(g, last_use):
            kind, qb, kt, k = last_use
            i = g * NQ + qb
            known = isinstance(g, int)
            if kind == "m":
                ahead, n = m_ops(kt)[k]
                if known and not 0 <= i + ahead < NG * NQ:
                    return None
                return mx_red, (i + ahead) * M_OPS + n + 1
            if kind == "out":
                return None if known and i < 1 else (norm_done, i)
            return None if known and not 0 <= i + 1 < NG * NQ else (mrow_ready, i + 2)

        def wait_ring(pe, g, use):
            at = ring_at[use] - 3
            while at > -len(ring):
                before = ring[at]
                got = before and taken(g if at >= 0 else g - 1, before)
                if got:
                    pe.wait_ge(*got)
                    return
                at -= 3

        XT_AT = [6, 12, 18, 24]
        DEP_PIECES = [slice(0, 5), slice(5, 9), slice(9, CT)]
        N_W = 11
        TOKB = [slice(4 * i, 4 * i + 4) for i in range(NQ)]

        BODIES = NT // U

        def all_parts_out(eng):
            for done in qk_out:
                eng.wait_ge(done, 16 * 6)

        LOOPED = BODIES - 2

        def tile(i, u, ahead):
            t = i * U + u + ahead
            if isinstance(i, int) and not 0 <= t < NT:
                return None
            return t, (u + ahead) % U

        def run_slots(eng, slot, enter=None, leave=None, mark=None):
            for u in range(-2, U):
                slot(-1, u)
            if mark:
                mark()
            with eng.Fori(0, LOOPED) as i:
                if enter:
                    enter(i)
                for u in range(U):
                    slot(i, u)
            if leave:
                leave()
            for i in range(LOOPED, BODIES):
                for u in range(U):
                    slot(i, u)

        @block.sync
        def _(sp):
            sp.dma_start(cst[:, :], a["consts"][:, :]).then_inc(consts_in, 16)
            sp.dma_start(mask_i[:, :], a["mask"]).then_inc(mask_in, 16)
            full = (CT - 1) * P
            sp.dma_start(CK[:, 0:CT - 1, :], a["ctx"][0:full, 0:C].rearrange("(j p) c -> p j c", p=P)).then_inc(ck_in, 16)
            sp.dma_start(V[:, NT:KT - 1, :], a["ctx"][0:full, C:2 * C].rearrange("(j p) c -> p j c", p=P)).then_inc(cv_in, 16)
            sp.wait_ge(pads_zero, 1)
            sp.dma_start(CK[0:TAIL, CT - 1, :], a["ctx"][full:NC, 0:C]).then_inc(ck_in, 16)
            sp.dma_start(V[0:TAIL, KT - 1, :], a["ctx"][full:NC, C:2 * C]).then_inc(cv_in, 16)
            sp.dma_start(X[:, :, :], a["x"].rearrange("(j p) c -> p j c", p=P)).then_inc(x_in, 16)
            sp.dma_start(w_qkv[:, :, :], a["w_qkv"].rearrange("(c p) n -> p c n", p=P)).then_inc(late_w_in, 16)
            sp.dma_start(w_pr[:, :, :], a["w_pr"].rearrange("(c p) n -> p c n", p=P)).then_inc(late_w_in, 16)
            for j in DEP_PIECES:
                sp.wait_ge(dep_ev, j.stop)
                sp.dma_start(depool.rearrange("(j p) c -> p j c", p=P)[:, j, :], UU[:, j, :]).then_inc(dep_out, 16)
            sp.wait_ge(ck_p2, 2 * 4)
            for s in range(3):
                sp.dma_start(kd[D * s:D * s + D].rearrange("(c d) h t -> (d h) c t", c=CC)[:, :, T:KPAD], CP[:, s, :, :]).then_inc(ck_out, 16)

            def parts_out(i):
                sp.wait_ge(c_p2, i * U + U)
                tok = slice(i * QB, i * QB + QB)
                for s in range(3):
                    sp.dma_start(kd[D * s:D * s + D].rearrange("(c d) h t -> (d h) c t", c=CC)[:, :, tok], PB[:, s, CC:2 * CC, tok]).then_inc(qk_out[i], 16)
                    sp.dma_start(qd[D * s:D * s + D].rearrange("(c d) h t -> (d h) c t", c=CC)[:, :, tok], PB[:, s, 0:CC, tok]).then_inc(qk_out[i], 16)

            def load_q(g, qb):
                at = 0
                for part, n in Q_RUNS:
                    for _ in range(n):
                        src = qd[D * part:D * part + D, bass.ds(g * G, G), qb * QB:(qb + 1) * QB]
                        sp.dma_start(QS[qb][at:at + D, :, :], src).then_inc(q_in[qb], 16)
                        at += D

            def load_k(dst, done, g, c):
                cols = slice(c * CH, c * CH + width(c))
                at = 0
                for part, n in K_RUNS:
                    src = kd[D * part:D * (part + n), bass.ds(g * G, G), cols]
                    sp.dma_start(dst[at:at + n * D, :, cols], src).then_inc(done[c], 16)
                    at += n * D

            def load_m(j):
                sp.wait_ge(mrow_ready, j + 1)
                sp.dma_start(QS[(j if isinstance(j, int) else 0) % NQ][SR:SR + 3, :, :], mrow[:, :]).then_inc(m_in, 16)

            parts_out(0)
            sp.wait_ge(ck_out, 16 * 3)
            for c in range(FIRST, NCH):
                load_k(KM, km_in, 0, c)
            for i in range(1, BODIES):
                parts_out(i)
                sp.wait_ge(qk_out[i - 1], 16 * 6)
                if i == 1:
                    load_q(0, 0)
                load_k(KM, km_in, 0, i - 1)
            all_parts_out(sp)
            load_k(KM, km_in, 0, BODIES - 1)
            load_q(0, 1)
            sp.wait_ge(fill_done, 1)
            for c in range(NCH):
                load_k(KX, kx_in, 0, c)
            load_m(0)

            def group(g, last):
                for qb in range(NQ):
                    i = g * NQ + qb
                    sp.wait_ge(qk_mm, i * 2 * KT + 1)
                    if not last or qb + 2 < NQ:
                        load_q(g + (qb + 2) // NQ, (qb + 2) % NQ)
                    if last and qb == NQ - 1:
                        continue
                    if qb == NQ - 2 and not last:
                        for c in sorted(range(NCH), key=lambda c: max(M_FREE[c], M_FREE[0])):
                            sp.wait_ge(mx_mm, (i + 1) * M_OPS + max(M_FREE[c], M_FREE[0]))
                            load_k(KM, km_in, g + 1, c)
                    if qb == NQ - 1:
                        for c in range(NCH - 2):
                            sp.wait_ge(qk_mm, i * 2 * KT + 2 * 4 * (c + 1))
                            load_k(KX, kx_in, g + 1, c)
                    sp.wait_ge(mrow_ready, i + 2)
                    sp.dma_start(QS[(qb + 1) % NQ][SR:SR + 3, :, :], mrow[:, :]).then_inc(m_in, 16)
                    if qb == NQ - 1:
                        for c in range(NCH - 2, NCH):
                            sp.wait_ge(qk_mm, i * 2 * KT + min(2 * 4 * (c + 1), 2 * KT))
                            load_k(KX, kx_in, g + 1, c)

            group(0, False)
            with sp.Fori(1, NG - 1) as g:
                group(g, False)
            group(NG - 1, True)

            sp.wait_ge(norm_done, NG * NQ)
            sp.dma_start(w1a[:, :, :], a["w1a"].rearrange("(c p) n -> p c n", p=P)).then_inc(moe_w_in, 16)
            for e in range(E):
                sp.dma_start(w1b[:, e, :], a["w1b"][e]).then_inc(moe_w_in, 16)
            sp.dma_start(w2a[:, :, :, :], a["w2a"].rearrange("(f p) e r -> p f e r", p=P)).then_inc(moe_w_in, 16)
            sp.dma_start(w2b[:, :, :], a["w2b"].rearrange("(a p) c -> p a c", p=P)).then_inc(moe_w_in, 16)
            for k in range(2):
                sp.dma_start(idx[:, k, :], a["idx"][k:k + 1, :].to_broadcast([P, T])).then_inc(tok_in, 16)
                sp.dma_start(wts[:, k, :], a["wts"][k:k + 1, :].to_broadcast([P, T])).then_inc(tok_in, 16)
            with sp.Fori(0, NQ) as b:
                sp.wait_ge(y_done, b * 4 + 4 + Y0)
                sp.dma_start(out.rearrange("(j p) c -> p j c", p=P)[:, bass.ds(b * 4, 4), :],
                             X[:, bass.ds(b * 4, 4), :]).then_inc(y_out, 16)
            sp.wait_ge(y_out, 16 * NQ)

        @block.gpsimd
        def _(pool):
            pool.iota(iota[:, :], [[1, P]], 0, 0, allow_small_or_imprecise_dtypes=True).then_inc(iota_ready, 1)
            pool.memset(CK[:, CT - 1, :], 0.0)
            pool.memset(V[:, KT - 1, :], 0.0)
            for u in range(U):
                ins = pool.memset(m64[u][:, R8:2 * R8, :], 0.0)
            ins.then_inc(pads_zero, 1)
            pool.wait_ge(dep_out, 16 * len(DEP_PIECES))
            pool.wait_ge(plug_ready, 1)
            for t in range(NT):
                pool.indirect_dma_start(out=GB[:, t, :], out_offset=None, in_=depool[:, :],
                                        in_offset=bass.IndirectOffsetOnAxis(ap=plug_i[:, t:t + 1], axis=0)).then_inc(gathered, 16)
            pool.wait_ge(c_p2, NT)
            all_parts_out(pool)
            pool.wait_ge(ck_out, 16 * 3)
            pool.memset(KX[SR:SR + 32, :, :], 1.0).then_inc(fill_done, 1)
            pool.wait_ge(fill_done, 1)
            pool.memset(Vg[:, :, :, D:2 * D], 1.0).then_inc(fill_done, 1)
            pool.wait_ge(cv_in, 32)

            def copy_v(g, c):
                n = min(4, KT - 4 * c)
                r = P if 4 * c + n < KT else TAIL
                src = V[0:r, 4 * c:4 * c + n, bass.ds(g * G * D, G * D)].rearrange("p k (h d) -> p k h d", h=G)
                pool.tensor_copy(Vg[0:r, 4 * c:4 * c + n, :, 0:D], src).then_inc(vg_ready, 1)

            for c in range(NCH):
                copy_v(0, c)
            with pool.Fori(0, NG - 1) as g:
                for c in range(NCH):
                    pool.wait_ge(pv_mm, g * (NQ * KT) + (NQ - 1) * KT + min(4 * c + 4, KT) + PV0)
                    copy_v(g + 1, c)

        @block.scalar
        def _(act):
            act.dma_start(gates_in[:, 0:4], a["gates"].to_broadcast([P, 4])).then_inc(weights_in, 16)
            act.dma_start(w_in[:, :, :], a["w_in"].rearrange("(c p) n -> p c n", p=P)).then_inc(weights_in, 16)
            act.dma_start(w_b0[:, :, :], a["w_b0"].rearrange("(c p) n -> p c n", p=P)).then_inc(weights_in, 16)
            act.dma_start(w_lb[:, :], a["w_lb"]).then_inc(weights_in, 16)
            act.dma_start(b_in[:, :], a["b_in"].to_broadcast([P, C])).then_inc(weights_in, 16)
            act.dma_start(b_b0[:, :], a["b_b0"].to_broadcast([P, C])).then_inc(weights_in, 16)
            act.dma_start(b_pr[:, :], a["b_pr"].to_broadcast([P, C])).then_inc(weights_in, 16)
            act.dma_start(b_rt[:, :], a["b_rt"].to_broadcast([P, R8])).then_inc(weights_in, 16)
            act.dma_start(g_ini[:, :], a["g_ini"].to_broadcast([P, C])).then_inc(weights_in, 16)
            act.dma_start(g_res[:, :], a["g_res"]).then_inc(weights_in, 16)
            act.dma_start(bn[:, 0, :], a["consts"][:, 0:6]).then_inc(weights_in, 16)
            act.wait_ge(weights_in, 16 * N_W)
            act.activation(gates[:, :], gates_in[:, :], ACT.Tanh).then_inc(tanh_done, 1)
            act.wait_ge(ck_in, 32)
            for j in range(CT):
                act.activation(sq_junk[:, :], CK[:, j, :], ACT.Square, accum_out=ss[:, j:j + 1]).then_inc(sq_done, 1)
                act.wait_ge(sq_done, j + 1)

            def sqrt(dst, src, n):
                act.wait_ge(sqrt_in, n)
                act.activation(dst, src, ACT.Sqrt).then_inc(sqrt_out, 1)

            sqrt(crt[:, :], crs[:, :], 1)
            for k in range(2 * 4):
                blk, c = divmod(k, CC)
                n = min(4, CT - 4 * blk) * P
                cols = slice(blk * QB, blk * QB + n)
                act.wait_ge(ck_tr, k + 1)
                act.activation(CP[:, 0, c, cols], tr_bank[k % 4][:, 0:n], ACT.Copy).then_inc(ck_p0, 1)
                act.wait_ge(ck_r1, k + 1)
                act.activation(CP[:, 1, c, cols], rest[k % 4][:, 0:n], ACT.Copy).then_inc(ck_p1, 1)

            sqrt(lns[:, :], lnv[:, :], 2)
            sqrt(lns[:, :], lnv[:, :], 3)
            def slot_a(i, u):
                if at := tile(i, u, 4):
                    act.wait_ge(ph["a", "xT_mm"], at[0] + 1)
                    for c in range(CC):
                        ins = act.activation(hT[at[1]][:, c, :], tr_bank[at[1]][:, c * P:(c + 1) * P], ACT.Copy, scale=g_res[:, c:c + 1])
                    ins.then_inc(ph["a", "hT_ready"], 1)

            run_slots(act, slot_a)

            def copy_hT(n, at):
                if at:
                    t, u = at
                    act.wait_ge(ph[n, "xT_mm"], t + 1)
                    act.activation(hT[u][:, :, :].rearrange("p c t -> p (c t)"), tr_bank[u][:, 0:C], ACT.Copy).then_inc(ph[n, "hT_ready"], 1)

            sqrt(lns[:, :], lnv[:, :], 4)
            def slot_b(i, u):
                if at := tile(i, u, 3):
                    t, w = at
                    act.wait_ge(lg_ready, t + 1)
                    act.activation(ex[w][:, :], lg[w][:, :], ACT.Exp, accum_out=esum[w][:, :]).then_inc(ex_ready, 1)
                if at := tile(i, u, 2):
                    t, w = at
                    act.wait_ge(m64_tr, t + 1)
                    act.activation(m64T[w][:, :], tr_bank[w][0:RK, C:C + P], ACT.Copy, scale=2.0).then_inc(m64_ev, 1)
                copy_hT("b", tile(i, u, 5))

            run_slots(act, slot_b)

            sqrt(lns[:, :], lnv[:, :], 5)
            def slot_c(i, u):
                if at := tile(i, u, 1):
                    t, w = at
                    act.wait_ge(ph["c", "out_mm"], t + 1)
                    act.activation(PB[:, 0, :, bass.ds(t * P, P)], out_bank[w].rearrange("p (k t) -> p k t", k=4), ACT.Copy).then_inc(c_p0, 1)
                if at := tile(i, u, 0):
                    t, w = at
                    act.wait_ge(c_r1, t + 1)
                    act.activation(PB[:, 1, :, bass.ds(t * P, P)], rest[w][:, :].rearrange("p (k t) -> p k t", k=4), ACT.Copy).then_inc(c_p1, 1)
                copy_hT("c", tile(i, u, 3))

            run_slots(act, slot_c)

            all_parts_out(act)
            act.wait_ge(ck_out, 16 * 3)
            act.wait_ge(c_p2, NT)
            act.sem_inc(exp_done, EXP0)

            def keep_turned(j, qb):
                act.wait_ge(mrow_mm, j + 1)
                if not (isinstance(j, int) and j == 0):
                    act.wait_ge(m_in, 16 * j)
                act.activation(mrow[:, :], ring_bank(("turn", qb, TURN, 0))[0:3 * G, :], ACT.Copy).then_inc(mrow_ready, 1)

            def evacuate(i):
                act.wait_ge(pv_mm, PV0 + KT * (i + 1))
                if not (isinstance(i, int) and i == 0):
                    act.wait_ge(oT_tr, i)
                act.activation(oT[:, :], pv_ps[:, :], ACT.Copy).then_inc(oT_ready, 1)

            def group_exps(g):
                for qb in range(NQ):
                    i = g * NQ + qb
                    known = isinstance(g, int)
                    for kt in range(KT):
                        r = rows(kt)
                        if kt == TURN + 1 and not (known and i + 1 >= NG * NQ):
                            keep_turned(i + 1, qb)
                        for p in range(2):
                            if p == 0:
                                act.wait_ge(pv_mm, PV0 + step_of(kt, i) + 1)
                            act.wait_ge(qk_mm, i * 2 * KT + 2 * kt + p + 1)
                            act.activation(PX[kt % PR][0:r, 2 * p:2 * p + 2, :], sc_ps[p][0:r, :, :], ACT.Exp,
                                           scale=D ** -0.5).then_inc(exp_done, 1)
                        if kt == 0 and not (known and i == 0):
                            evacuate(i - 1)

            keep_turned(0, NQ - 1)
            group_exps(0)
            with act.Fori(1, NG - 1) as g:
                group_exps(g)
            group_exps(NG - 1)
            evacuate(NG * NQ - 1)

            run_slots(act, lambda i, u: copy_hT("e", tile(i, u, 4)))

            sqrt(lns[:, :], lnv[:, :], 6)
            def keep_xT(b, u):
                act.wait_ge(f_tr, b * 4 + u + 1)
                act.activation(XT[:, :, bass.ds(b * QB + u * P, P)], mx_ps[u % 2][:, 0:C].rearrange("p (c t) -> p c t", c=CC),
                               ACT.Copy).then_inc(f_hT, 1)

            def token_block(b, last):
                for p in range(NP):
                    act.wait_ge(s1_mm, b * NP + p + 1)
                    act.activation(UT[:, p, :], mx_ps[p % 2][:, :], ACT.Copy).then_inc(u_ev, 1)
                for n in range(NP * NF):
                    act.wait_ge(s2_mm, b * (NP * NF) + n + 1)
                    act.activation(GE[n % 2][:, :, :], sc_ps[n % 2][:, :, :], ACT.Gelu).then_inc(gelu_done, 1)
                    if n in XT_AT and not last:
                        keep_xT(b + 1, XT_AT.index(n))

            for u in range(4):
                keep_xT(0, u)
            with act.Fori(0, NQ - 1) as b:
                token_block(b, False)
            token_block(NQ - 1, True)

        @block.vector
        def _(v):
            cnt = [0]
            base = [0]

            def steps(ins):
                cnt[0] += 1
                ins.then_inc(dve, 1)
                return cnt[0]

            def after(n):
                v.wait_ge(dve, base[0] + n)

            def link(ins):
                after(steps(ins))

            def enter(i, per):
                base[0] = fixed[0] + i * per
                cnt[0] = 0

            def leave(n, per):
                assert cnt[0] == per, (cnt[0], per)
                fixed[0] += n * per
                base[0], cnt[0] = fixed[0], 0

            def mark():
                fixed[0] = base[0] + cnt[0]

            fixed = [0]

            v.wait_ge(consts_in, 16)
            link(v.tensor_copy(ident_b[:, :], ident))
            v.wait_ge(mask_in, 16)
            v.tensor_copy(mask_f[:, :], mask_i[:, :]).then_inc(cum_in, 1)
            v.wait_ge(cum_mm, 1)
            link(v.tensor_tensor_scan(off[:, :], ones[:, 0:CT], tr_bank[0][:, CT:2 * CT], 0.0, ALU.mult, ALU.add))
            link(v.tensor_tensor(out=off[:, :], in0=off[:, :], in1=tr_bank[0][:, CT:2 * CT], op=ALU.subtract))
            link(v.scalar_tensor_tensor(out=bidx[:, :], in0=off[:, :], scalar=-1.0, in1=tr_bank[0][:, 0:CT], op0=ALU.add, op1=ALU.add))
            link(v.tensor_scalar(neg[:, :], bidx[:, :], 0.0, float(T), ALU.is_lt, ALU.mult))
            link(v.tensor_tensor(out=bidx[:, :], in0=bidx[:, :], in1=neg[:, :], op=ALU.add))
            v.wait_ge(iota_ready, 1)
            link(v.tensor_copy(bidx_i[:, :], bidx[:, :]))
            link(v.tensor_scalar(low_i[:, :], bidx_i[:, :], P - 1, None, ALU.bitwise_and))
            link(v.tensor_scalar(high_i[:, :], bidx_i[:, :], P.bit_length() - 1, None, ALU.arith_shift_right))
            link(v.tensor_copy(low[:, :], low_i[:, :]))
            link(v.tensor_copy(high[:, :], high_i[:, :]))
            v.tensor_tensor(out=hot_high[:, :, :], in0=iota[:, 0:NT].unsqueeze(1).to_broadcast([P, CT, NT]),
                            in1=high[:, :].unsqueeze(2).to_broadcast([P, CT, NT]), op=ALU.is_equal).then_inc(hot_ready, 1)
            v.tensor_tensor(out=hot_low[:, :, :], in0=iota[:, :].unsqueeze(1).to_broadcast([P, CT, P]),
                            in1=low[:, :].unsqueeze(2).to_broadcast([P, CT, P]), op=ALU.is_equal).then_inc(hot_ready, 1)
            v.wait_ge(cnt_mm, 1)
            v.tensor_scalar(bnd[:, :], tr_bank[1][:, 0:NT], 1.0, None, ALU.min).then_inc(cum2_in, 1)
            v.wait_ge(cum2_mm, 1)
            link(v.tensor_tensor_scan(off2[:, :], ones[:, 0:NT], tr_bank[2][:, NT:2 * NT], 0.0, ALU.mult, ALU.add))
            link(v.tensor_tensor(out=off2[:, :], in0=off2[:, :], in1=tr_bank[2][:, NT:2 * NT], op=ALU.subtract))
            link(v.scalar_tensor_tensor(out=plug[:, :], in0=off2[:, :], scalar=-1.0, in1=tr_bank[2][:, 0:NT], op0=ALU.add, op1=ALU.add))
            v.tensor_scalar(plug_i[:, :], plug[:, :], 0.0, float(NC - 1), ALU.max, ALU.min).then_inc(plug_ready, 1)
            v.wait_ge(cv_in, 32)
            for j in range(CT):
                steps(v.bn_stats(bnc[:, j, :], V[:, NT + j, :]))
                if j:
                    after(cnt[0] - 1)
                    steps(v.bn_aggr(mvc[:, j - 1, :], bnc[:, j - 1, :]))
            after(cnt[0])
            link(v.bn_aggr(mvc[:, CT - 1, :], bnc[:, CT - 1, :]))
            link(v.tensor_tensor(out=crt[:, :], in0=mvc[:, :, 0], in1=mvc[:, :, 0], op=ALU.mult))
            link(v.tensor_tensor(out=crt[:, :], in0=crt[:, :], in1=mvc[:, :, 1], op=ALU.add))
            v.wait_ge(sq_done, CT)
            link(v.scalar_tensor_tensor(out=crs[:, :], in0=crt[:, :], scalar=float(C), in1=ss[:, :], op0=ALU.mult, op1=ALU.add))
            v.tensor_scalar(crs[:, :], crs[:, :], 1.0 / (2 * C), 1e-5, ALU.mult, ALU.add).then_inc(sqrt_in, 1)
            v.wait_ge(sqrt_out, 1)
            link(v.reciprocal(crs[:, :], crt[:, :]))
            link(v.tensor_scalar(crs[:, :], crs[:, :], u_scale, None, ALU.mult))
            v.wait_ge(weights_in, 16 * N_W)
            for j in range(CT):
                v.scalar_tensor_tensor(out=UU[:, j, :], in0=CK[:, j, :], scalar=crs[:, j:j + 1], in1=g_ini[:, :],
                                       op0=ALU.mult, op1=ALU.mult).then_inc(u_ready, 1)
            for j in range(CT):
                v.wait_ge(dep_mm, min(j + 2, CT))
                v.tensor_tensor(out=UU[:, j, :].rearrange("p (h d) -> p d h", h=HEADS),
                                in0=out_bank[j % 4][:, 0:C].rearrange("p (d h) -> p d h", h=HEADS),
                                in1=b_in[:, :].rearrange("p (h d) -> p d h", h=HEADS), op=ALU.add).then_inc(dep_ev, 1)
            for k in range(2 * 4):
                blk, c = divmod(k, CC)
                n = min(4, CT - 4 * blk) * P
                cols = slice(blk * QB, blk * QB + n)
                v.wait_ge(ck_p0, k + 1)
                v.tensor_tensor(out=rest[k % 4][:, 0:n], in0=tr_bank[k % 4][:, 0:n], in1=CP[:, 0, c, cols], op=ALU.subtract).then_inc(ck_r1, 1)
                v.wait_ge(ck_p1, k + 1)
                v.tensor_tensor(out=CP[:, 2, c, cols], in0=rest[k % 4][:, 0:n], in1=CP[:, 1, c, cols], op=ALU.subtract).then_inc(ck_p2, 1)

            def update(fresh, stats, n, bias, gate, beside, source, ahead):
                beside = iter(beside)

                def between():
                    for step in beside:
                        step()
                        return

                between()
                if stats:
                    ts, us = stats
                    n_stats = steps(v.bn_stats(bn[:, us, :], xnew[us][:, :]))
                if fresh:
                    tf, uf = fresh
                    v.wait_ge(lora_mm if n == "b" else ph[n, "out_mm"], tf + 1)
                    n_sum = steps(v.tensor_tensor(out=tmp[uf][:, :], in0=out_bank[uf][:, 0:C], in1=bias(tf), op=ALU.add))
                between()
                if stats:
                    after(n_stats)
                    steps(v.tensor_scalar(X[:, ts, :], xnew[us][:, :], 1.0, None, ALU.mult))
                    n_aggr = steps(v.bn_aggr(mvu[:, us, :], bn[:, us, :]))
                between()
                if fresh:
                    after(n_sum)
                    n_new = steps(v.scalar_tensor_tensor(out=xnew[uf][:, :], in0=tmp[uf][:, :], scalar=gates[:, gate:gate + 1],
                                                         in1=X[:, tf, :], op0=ALU.mult, op1=ALU.add))
                between()
                if stats:
                    after(n_aggr)
                    steps(v.tensor_scalar(mv[:, ts, :], mvu[:, us, :], 1.0, None, ALU.mult))
                for step in beside:
                    step()
                source(ahead)
                if fresh:
                    after(n_new)

            def layernorm_scale(n):
                v.tensor_scalar(lnv[:, :], mv[:, :, 1], 1.0, LN_EPS, ALU.mult, ALU.add).then_inc(sqrt_in, 1)
                v.wait_ge(sqrt_out, n)
                link(v.reciprocal(rstd[:, :], lns[:, :]))

            def normalise(at, scale, done):
                if not at:
                    return
                t, u = at
                v.tensor_scalar(xs[u][:, :], X[:, t, :], mv[:, t, 0:1], scale[:, bass.ds(t, 1)],
                                ALU.subtract, ALU.mult).then_inc(done, 1)

            v.wait_ge(x_in, 16)
            mark()
            for t in range(NT):
                steps(v.bn_stats(bn[:, t % U, :], X[:, t, :]))
                if t:
                    after(cnt[0] - 1)
                    steps(v.bn_aggr(mv[:, t - 1, :], bn[:, (t - 1) % U, :]))
            after(cnt[0])
            link(v.bn_aggr(mv[:, NT - 1, :], bn[:, (NT - 1) % U, :]))
            layernorm_scale(2)
            link(v.tensor_tensor(out=rstd2[:, :], in0=rstd[:, :], in1=rstd[:, :], op=ALU.mult))
            link(v.tensor_tensor(out=rstd2[:, :], in0=rstd2[:, :], in1=mv[:, :, 1], op=ALU.mult))
            v.tensor_scalar(lnv[:, :], rstd2[:, :], 1.0, 1e-5, ALU.mult, ALU.add).then_inc(sqrt_in, 1)
            v.wait_ge(sqrt_out, 3)
            link(v.reciprocal(rstd2[:, :], lns[:, :]))
            link(v.tensor_tensor(out=rstd[:, :], in0=rstd[:, :], in1=rstd2[:, :], op=ALU.mult))
            v.wait_ge(tanh_done, 1)
            def slots(slot, per):
                run_slots(v, slot, lambda i: enter(i, per * U), lambda: leave(LOOPED, per * U), mark)
                after(cnt[0])
                mark()

            def linear_slots(n, source, bias, gate, ready=lambda: None):
                def slot(i, u):
                    fresh, stats = tile(i, u, 1), tile(i, u, 0)
                    if fresh and not stats:
                        ready()
                    update(fresh, stats, n, bias, gate, [], source, tile(i, u, 5))

                slots(slot, 6)

            linear_slots("a", lambda at: normalise(at, rstd, ph["a", "xs_ready"]), lambda t: GB[:, t, :], 0,
                         lambda: v.wait_ge(gathered, 16 * NT))

            layernorm_scale(4)
            def slot_b(i, u):
                beside = []
                at3, at2 = tile(i, u, 3), tile(i, u, 2)
                number = {}
                if at3:
                    t3, w3 = at3

                    def logits():
                        v.wait_ge(ph["b", "out_mm"], t3 + 1)
                        number["lg"] = steps(v.tensor_tensor(out=lg[w3][:, :], in0=out_bank[w3][:, C:C + R8], in1=b_rt[:, :], op=ALU.add))

                    def logits_max():
                        after(number["lg"])
                        number["max"] = steps(v.reduce_max(lmx[w3][:, :], lg[w3][:, :], AX))

                    def logits_less_max():
                        after(number["max"])
                        v.tensor_scalar(lg[w3][:, :], lg[w3][:, :], lmx[w3][:, :], None, ALU.subtract).then_inc(lg_ready, 1)
                if at2:
                    t2, w2 = at2

                    def one_over_sum():
                        v.wait_ge(ex_ready, t2 + 1)
                        number["rcp"] = steps(v.reciprocal(esum[w2][:, :], esum[w2][:, :]))

                    def gate_weights():
                        after(number["rcp"])
                        number["gate"] = steps(v.tensor_scalar(gate[w2][:, :], ex[w2][:, :], esum[w2][:, :], None, ALU.mult))

                    def gated_rows():
                        after(number["gate"])
                        v.tensor_tensor(out=m64[w2][:, 0:R8, :],
                                        in0=out_bank[w2][:, C + R8:C + 2 * R8].unsqueeze(1).to_broadcast([P, R8, R8]),
                                        in1=gate[w2][:, :].unsqueeze(2).to_broadcast([P, R8, R8]), op=ALU.mult).then_inc(m64_ready, 1)
                if at2:
                    one_over_sum()
                if at3:
                    logits()
                if at2:
                    gate_weights()
                    beside.append(gated_rows)
                if at3:
                    beside += [logits_max, logits_less_max]
                update(tile(i, u, 1), tile(i, u, 0), "b", lambda t: b_b0[:, :], 1, beside,
                       lambda at: normalise(at, rstd, ph["b", "xs_ready"]), tile(i, u, 6))

            slots(slot_b, 10)

            layernorm_scale(5)
            def slot_c(i, u):
                if at := tile(i, u, 0):
                    t, w = at
                    v.wait_ge(c_p0, t + 1)
                    v.tensor_tensor(out=rest[w][:, :].rearrange("p (k t) -> p k t", k=4),
                                    in0=out_bank[w].rearrange("p (k t) -> p k t", k=4), in1=PB[:, 0, :, bass.ds(t * P, P)],
                                    op=ALU.subtract).then_inc(c_r1, 1)
                    link(v.tensor_copy(V[:, t, :], tr_bank[w][:, C:2 * C]))
                    v.wait_ge(c_p1, t + 1)
                    v.tensor_tensor(out=PB[:, 2, :, bass.ds(t * P, P)], in0=rest[w][:, :].rearrange("p (k t) -> p k t", k=4),
                                    in1=PB[:, 1, :, bass.ds(t * P, P)], op=ALU.subtract).then_inc(c_p2, 1)
                normalise(tile(i, u, 4), rstd, ph["c", "xs_ready"])

            slots(slot_c, 1)

            v.wait_ge(ck_out, 16 * 3)

            def maxima(g, qb, kt, part=slice(0, None)):
                for k, (ahead, n) in list(enumerate(m_ops(kt)))[part]:
                    if isinstance(g, int) and not 0 <= g * NQ + qb + ahead < NG * NQ:
                        continue
                    c, q = M_ORDER[n]
                    v.wait_ge(mx_mm, (g * NQ + qb + ahead) * M_OPS + n + 1)
                    v.reduce_max(mp[:, q, c:c + 1], ring_bank(("m", qb, kt, k))[:, 0:width(c)], AX).then_inc(mx_red, 1)

            def negated_maxima(j):
                at = [0]

                def first():
                    v.wait_ge(mx_red, (j + 1) * M_OPS)
                    link(v.reduce_max(mm[:, :, :].rearrange("p t h -> p (t h)"), mp[:, :, :], AX))

                def part_0():
                    at[0] = steps(v.tensor_scalar(mst[:, :, 0, :], mm[:, :, :], -1.0, None, ALU.mult))

                def what_is_left():
                    after(at[0])
                    at[0] = steps(v.scalar_tensor_tensor(out=mr[:, :, :], in0=mm[:, :, :], scalar=-1.0, in1=mst[:, :, 0, :],
                                                         op0=ALU.mult, op1=ALU.subtract))

                def part_1():
                    after(at[0])
                    at[0] = steps(v.tensor_copy(mst[:, :, 1, :], mr[:, :, :]))

                def part_2():
                    after(at[0])
                    v.tensor_tensor(out=mst[:, :, 2, :], in0=mr[:, :, :], in1=mst[:, :, 1, :], op=ALU.subtract).then_inc(mst_ready, 1)

                return [first, part_0, what_is_left, part_1, part_2]

            def normalise_out(g, qb, bank):
                i = g * NQ + qb
                v.wait_ge(oT_tr, i + 1)
                ps = bank[:, :].rearrange("p (t h d) -> p t h d", t=4, h=G)
                link(v.reciprocal(rcp[:, :, :], ps[:, :, :, D]))
                v.tensor_tensor(out=attn[:, TOKB[qb], bass.ds(g * G * D, G * D)].rearrange("p t (h d) -> p t h d", h=G),
                                in0=ps[:, :, :, 0:D], in1=rcp[:, :, :].unsqueeze(3).to_broadcast([P, 4, G, D]),
                                op=ALU.mult).then_inc(norm_done, 1)

            def group(g, blocks=range(NQ), kts=range(KT), exps=True):
                for qb in blocks:
                    i = g * NQ + qb
                    known = isinstance(g, int)
                    follows = not (known and i + 1 >= NG * NQ)
                    behind = exps and not (known and i == 0)
                    for kt in kts:
                        if kt == 3 and behind:
                            normalise_out(g - (qb == 0), (qb - 1) % NQ, ring_bank(("out", qb, 2, 0)))
                        chain = negated_maxima(i + 1) if kt == NEGATE and follows else []
                        for k in range(len(m_ops(kt))):
                            if chain:
                                chain.pop(0)()
                            maxima(g, qb, kt, slice(k, k + 1))
                        for step in chain:
                            step()

            for kt in range(NEGATE, KT):
                maxima(-1, NQ - 2, kt)
            group(-1, [NQ - 1], range(KT), False)

            group(0)
            mark()
            per = 5 * NQ
            with v.Fori(1, NG - 1) as g:
                enter(g - 1, per)
                group(g)
            leave(NG - 2, per)
            group(NG - 1)
            normalise_out(NG - 1, NQ - 1, mx_ps[0])

            v.wait_ge(norm_done, NG * NQ)
            def take_attn(at):
                if at:
                    v.tensor_copy(xs[at[1]][:, :], attn[:, at[0], :]).then_inc(ph["e", "xs_ready"], 1)

            linear_slots("e", take_attn, lambda t: b_pr[:, :], 2)

            layernorm_scale(6)
            for u in range(4):
                normalise((u, u), rstd, f_xs)
            v.sem_inc(y_done, Y0)
            v.wait_ge(tok_in, 64)
            mark()

            def token_block(b, last):
                tok = bass.ds(b * QB, QB)
                for p in range(NP):
                    v.scalar_tensor_tensor(out=CB[:, p, :], in0=idx[:, 0, tok], scalar=ecol[:, p:p + 1], in1=wts[:, 0, tok],
                                           op0=ALU.is_equal, op1=ALU.mult)
                    link(v.scalar_tensor_tensor(out=CB1[:, :], in0=idx[:, 1, tok], scalar=ecol[:, p:p + 1], in1=wts[:, 1, tok],
                                                op0=ALU.is_equal, op1=ALU.mult))
                    link(v.tensor_tensor(out=CB[:, p, :], in0=CB[:, p, :], in1=CB1[:, :], op=ALU.add))
                if not last:
                    v.wait_ge(f_tr, b * 4 + 4)
                    for u in range(4):
                        normalise((b * 4 + 4 + u, u), rstd, f_xs)
                for p in range(NP):
                    v.wait_ge(s3_mm, b * (NP * NF) + (p + 1) * NF)
                    v.tensor_tensor(out=Z[:, p, :], in0=(pv_ps, tr_ps)[p % 2][:, :], in1=CB[:, p, :], op=ALU.mult).then_inc(z_ready, 1)
                for u in range(4):
                    t = b * 4 + u
                    v.wait_ge(y_mm, t + 1)
                    v.scalar_tensor_tensor(out=X[:, t, :], in0=out_bank[u][:, 0:C], scalar=gates[:, 3:4],
                                           in1=X[:, t, :], op0=ALU.mult, op1=ALU.add).then_inc(y_done, 1)

            with v.Fori(0, NQ - 1) as b:
                enter(b, 2 * NP)
                token_block(b, False)
            leave(NQ - 1, 2 * NP)
            token_block(NQ - 1, True)

        @block.tensor
        def _(pe):
            def mm2(o, l, r, start=True, stop=True):
                return pe.matmul(o, l, r, start=start, stop=stop)

            pe.wait_ge(consts_in, 16)
            pe.wait_ge(cum_in, 1)
            mm2(tr_bank[0][:, 0:CT], tri, mask_f[:, :])
            mm2(tr_bank[0][:, CT:2 * CT], ones, mask_f[:, :]).then_inc(cum_mm, 1)
            pe.wait_ge(hot_ready, 2)
            for j in range(CT):
                r = P if j < CT - 1 else TAIL
                ins = mm2(tr_bank[1][:, 0:NT], hot_low[0:r, j, :], hot_high[0:r, j, :], j == 0, j == CT - 1)
            ins.then_inc(cnt_mm, 1)
            pe.wait_ge(cum2_in, 1)
            mm2(tr_bank[2][:, 0:NT], tri, bnd[:, :])
            mm2(tr_bank[2][:, NT:2 * NT], ones, bnd[:, :]).then_inc(cum2_mm, 1)
            for j in range(CT):
                pe.wait_ge(u_ready, j + 1)
                if j >= 4:
                    pe.wait_ge(dep_ev, j - 3)
                ins = mm2(out_bank[j % 4][:, 0:C], lmat0, UU[:, j, :], True, j == 0)
                if j:
                    ins = mm2(out_bank[j % 4][:, 0:C], lmat1, UU[:, j - 1, :], False, True)
                ins.then_inc(dep_mm, 1)
            for k in range(2 * 4):
                blk, c = divmod(k, CC)
                if k >= 4:
                    pe.wait_ge(ck_p2, k - 3)
                elif k in (0, 1, 2):
                    pe.wait_ge(plug_ready, 1)
                for jj in range(min(4, CT - 4 * blk)):
                    ins = pe.transpose(tr_bank[k % 4][:, jj * P:(jj + 1) * P], CK[:, 4 * blk + jj, c * P:(c + 1) * P], ident)
                ins.then_inc(ck_tr, 1)
            pe.wait_ge(ck_p2, 8)

            def turn(n, at):
                if at:
                    t, u = at
                    pe.wait_ge(ph[n, "xs_ready"], t + 1)
                    for c in range(CC):
                        ins = pe.transpose(tr_bank[u][:, c * P:(c + 1) * P], xs[u][:, c * P:(c + 1) * P], ident)
                    ins.then_inc(ph[n, "xT_mm"], 1)

            def project(n, at, w, stop=True):
                t, u = at
                pe.wait_ge(ph[n, "hT_ready"], t + 1)
                for c in range(CC):
                    ins = mm2(out_bank[u][:, 0:C], hT[u][:, c, :], w[:, c, 0:C], c == 0, stop and c == CC - 1)
                return ins

            def linear_slot(n, w):
                def slot(i, u):
                    turn(n, tile(i, u, 4))
                    if at := tile(i, u, 3):
                        project(n, at, w).then_inc(ph[n, "out_mm"], 1)
                return slot

            pe.wait_ge(weights_in, 16 * N_W)
            run_slots(pe, linear_slot("a", w_in))

            def base_and_router(at):
                if at:
                    t, u = at
                    pe.wait_ge(ph["b", "hT_ready"], t + 1)
                    for c in range(CC):
                        mm2(out_bank[u][:, C:C + 2 * R8], hT[u][:, c, :], w_b0[:, c, C:C + 2 * R8], c == 0, c == CC - 1)
                    project("b", at, w_b0, stop=False).then_inc(ph["b", "out_mm"], 1)

            def slot_b(i, u):
                at = tile(i, u, 2)
                if at:
                    t, w = at
                    pe.wait_ge(m64_ready, t + 1)
                    pe.transpose(tr_bank[w][:, C:C + P], m64[w][:, :, :].rearrange("p e r -> p (e r)"), ident).then_inc(m64_tr, 1)
                turn("b", tile(i, u, 5))
                base_and_router(tile(i, u, 4))
                if at:
                    pe.wait_ge(m64_ev, t + 1)
                    mm2(out_bank[w][:, 0:C], m64T[w][:, :], w_lb[:, :], False, True).then_inc(lora_mm, 1)

            run_slots(pe, slot_b)

            def slot_c(i, u):
                turn("c", tile(i, u, 3))
                if at := tile(i, u, 2):
                    t, w = at
                    pe.wait_ge(ph["c", "hT_ready"], t + 1)
                    for c in range(CC):
                        mm2(tr_bank[w][:, C:2 * C], hT[w][:, c, :], w_qkv[:, c, 2 * C:3 * C], c == 0, c == CC - 1)
                    for k in range(4):
                        for c in range(CC):
                            ins = mm2(out_bank[w][:, k * P:(k + 1) * P], w_qkv[:, c, k * P:(k + 1) * P], hT[w][:, c, :],
                                      c == 0, c == CC - 1)
                    ins.then_inc(ph["c", "out_mm"], 1)

            pe.wait_ge(late_w_in, 32)
            run_slots(pe, slot_c)

            pe.wait_ge(c_p2, NT)
            pe.sem_inc(pv_mm, PV0)

            def maxima(g, qb, kt, part):
                for k, (ahead, n) in list(enumerate(m_ops(kt)))[part]:
                    if isinstance(g, int) and not 0 <= g * NQ + qb + ahead < NG * NQ:
                        continue
                    c, q = M_ORDER[n]
                    t, h = divmod(q, G)
                    gj, qj = g + (qb + ahead) // NQ, (qb + ahead) % NQ
                    if n == 0:
                        pe.wait_ge(q_in[qj], 16 * Q_LOADS * (gj + 1))
                    if q == 0 and qj == 0:
                        pe.wait_ge(km_in[c], 16 * K_LOADS * (gj + 1))
                    wait_ring(pe, g, ("m", qb, kt, k))
                    pe.matmul(ring_bank(("m", qb, kt, k))[:, 0:width(c)], QS[qj][0:SR, h, t * P:(t + 1) * P],
                              KM[0:SR, h, c * CH:c * CH + width(c)], start=True, stop=True).then_inc(mx_mm, 1)

            def turn_maxima(g, qb):
                pe.wait_ge(mst_ready, g * NQ + qb + 2)
                use = ("turn", qb, TURN, 0)
                wait_ring(pe, g, use)
                for t in range(4):
                    ins = pe.matmul(ring_bank(use)[0:3 * G, t * P:(t + 1) * P], mst[:, t, :, :].rearrange("p r h -> p (r h)"), ident_b[:, :],
                                    start=True, stop=True)
                ins.then_inc(mrow_mm, 1)

            def scores(g, qb, kt, p):
                i = g * NQ + qb
                r = rows(kt)
                if qb == 0 and p == 0 and kt % 4 == 0:
                    pe.wait_ge(kx_in[kt // 4], 16 * K_LOADS * (g + 1))
                pe.wait_ge(exp_done, i * 2 * KT + 2 * kt + p - 1 + EXP0)
                for h in (2 * p, 2 * p + 1):
                    ins = pe.matmul(sc_ps[p][0:r, h % 2, :], KX[0:SR + 3, h, kt * P:kt * P + r], QS[qb][0:SR + 3, h, :],
                                    start=True, stop=True)
                ins.then_inc(qk_mm, 1)

            def weigh(g, qb, kt):
                i = g * NQ + qb
                r = rows(kt)
                if qb == 0 and kt % 4 == 0:
                    pe.wait_ge(vg_ready, g * NCH + kt // 4 + 1)
                pe.wait_ge(exp_done, i * 2 * KT + 2 * kt + 2 + EXP0)
                for h in range(G):
                    ins = pe.matmul(pv_ps[32 * h:32 * h + 32, :], Vg[0:r, kt, h, :], PX[kt % PR][0:r, h, :],
                                    start=kt == 0, stop=kt == KT - 1)
                ins.then_inc(pv_mm, 1)

            def turn_out(i, bank):
                pe.wait_ge(oT_ready, i + 1)
                for t in range(4):
                    ins = pe.transpose(bank[:, t * P:(t + 1) * P], oT[:, t * P:(t + 1) * P], ident)
                ins.then_inc(oT_tr, 1)

            for kt in range(NEGATE, KT):
                maxima(-1, NQ - 2, kt, slice(0, None))
            for kt in range(KT):
                maxima(-1, NQ - 1, kt, slice(0, None))
                if kt == TURN:
                    turn_maxima(-1, NQ - 1)
            pe.wait_ge(fill_done, 2)

            def group(g):
                for qb in range(NQ):
                    i = g * NQ + qb
                    known = isinstance(g, int)
                    follows = not (known and i + 1 >= NG * NQ)
                    behind = not (known and i == 0)
                    pe.wait_ge(m_in, 16 * (i + 1))
                    for kt in range(KT):
                        scores(g, qb, kt, 0)
                        maxima(g, qb, kt, slice(0, 1))
                        scores(g, qb, kt, 1)
                        maxima(g, qb, kt, slice(1, 3))
                        if kt:
                            if kt == 1 and behind:
                                pe.wait_ge(oT_ready, i)
                            weigh(g, qb, kt - 1)
                        elif behind:
                            weigh(g - (qb == 0), (qb - 1) % NQ, KT - 1)
                        maxima(g, qb, kt, slice(3, None))
                        if kt == 2 and behind:
                            wait_ring(pe, g, ("out", qb, 2, 0))
                            turn_out(i - 1, ring_bank(("out", qb, 2, 0)))
                        if kt == TURN and follows:
                            turn_maxima(g, qb)

            group(0)
            with pe.Fori(1, NG - 1) as g:
                group(g)
            group(NG - 1)
            weigh(NG - 1, NQ - 1, KT - 1)
            pe.wait_ge(mx_red, NG * NQ * M_OPS)
            pe.wait_ge(mrow_ready, NG * NQ)
            pe.wait_ge(norm_done, NG * NQ - 1)
            turn_out(NG * NQ - 1, mx_ps[0])
            pe.wait_ge(norm_done, NG * NQ)

            run_slots(pe, linear_slot("e", w_pr))


            def turn_tokens(b, u):
                t = b * 4 + u
                pe.wait_ge(f_xs, t + 1)
                if u >= 2:
                    pe.wait_ge(f_hT, t - 1)
                for c in range(CC):
                    ins = pe.transpose(mx_ps[u % 2][:, c * P:(c + 1) * P], xs[u][:, c * P:(c + 1) * P], ident)
                ins.then_inc(f_tr, 1)

            def token_block(b, last):
                pe.wait_ge(f_hT, b * 4 + 4)
                for p in range(NP):
                    if p >= 2:
                        pe.wait_ge(u_ev, b * NP + p - 1)
                    for c in range(CC):
                        ins = mm2(mx_ps[p % 2][:, :], w1a[:, c, p * P:(p + 1) * P], XT[:, c, bass.ds(b * QB, QB)], c == 0, c == CC - 1)
                    ins.then_inc(s1_mm, 1)

                def up(p, f):
                    n = p * NF + f
                    if f == 0:
                        pe.wait_ge(u_ev, b * NP + p + 1)
                    if n == 0:
                        pe.wait_ge(y_done, b * 4 + Y0)
                    if n >= 2:
                        pe.wait_ge(gelu_done, b * (NP * NF) + n - 1)
                    for e in range(2):
                        ins = mm2(sc_ps[f % 2][:, e, :], w1b[:, 2 * p + e, f * P:(f + 1) * P], UT[:, p, :])
                    ins.then_inc(s2_mm, 1)

                def down(p, f):
                    n = p * NF + f
                    if f == 0 and p >= 2:
                        pe.wait_ge(z_ready, b * NP + p - 1)
                    pe.wait_ge(gelu_done, b * (NP * NF) + n + 1)
                    for e in range(2):
                        ins = mm2((pv_ps, tr_ps)[p % 2][RK * e:RK * e + RK, :], w2a[:, f, 2 * p + e, :], GE[f % 2][:, e, :], f == 0, f == NF - 1)
                    ins.then_inc(s3_mm, 1)

                for n in range(NP * NF + 1):
                    if n < NP * NF:
                        up(*divmod(n, NF))
                    if n:
                        down(*divmod(n - 1, NF))
                    if n in XT_AT and not last:
                        turn_tokens(b + 1, XT_AT.index(n))
                pe.wait_ge(z_ready, b * NP + NP)
                for u in range(4):
                    for p in range(NP):
                        ins = mm2(out_bank[u][:, 0:C], Z[:, p, u * P:(u + 1) * P], w2b[:, p, :], p == 0, p == NP - 1)
                    ins.then_inc(y_mm, 1)

            for u in range(4):
                turn_tokens(0, u)
            pe.wait_ge(moe_w_in, 16 * (E + 3))
            with pe.Fori(0, NQ - 1) as b:
                token_block(b, False)
            token_block(NQ - 1, True)


def constants():
    logp = np.float32(-1e-3)
    dt = np.float32(-np.log(-np.expm1(logp)))
    factor = np.float64(np.exp(-dt))
    c = np.zeros((P, C_ALL), np.float32)
    q, p = np.arange(P)[:, None], np.arange(P)[None, :]
    c[:, C_ID:C_ID + P] = q == p
    c[:, C_TRI:C_TRI + P] = q <= p
    c[:, C_ONE:C_ONE + P] = 1
    c[:, C_L0:C_L0 + P] = np.where(q <= p, factor ** np.maximum(p - q, 0), 0)
    c[:, C_L1:C_L1 + P] = factor ** (p + P - q)
    c[:, C_EC:C_EC + NP] = 2 * np.arange(NP)[None, :] + q // RK
    return c


def kernel(**inputs):
    import concourse.bacc as _bacc
    from concourse import mybir as _mybir
    from concourse.bass_utils import run_bass_kernel_spmd as _run

    x = {k: np.asarray(v) for k, v in inputs.items()}
    mask = np.zeros((CT * P,), np.int32)
    mask[:NC] = x["mask_BxS2_if0"][0]
    w1b = np.zeros((E, P, FF), np.float32)
    for e in range(E):
        w1b[e, RK * (e % 2):RK * (e % 2) + RK] = x["L1_ffn_w1_B"].reshape(E, RK, FF)[e]
    w_qkv = x["L1_xattn_w_qkv"].T

    def by_dim(w):
        return w.reshape(-1, HEADS, D).transpose(0, 2, 1).reshape(-1, C)

    arrays = {
        "x": x["x"][0], "ctx": np.concatenate([by_dim(x["ctx_2048"][0, :, :C]), x["ctx_2048"][0, :, C:]], 1), "mask": mask.reshape(CT, P).T, "consts": constants(),
        "gates": np.stack([x["g_xattn"], x["g_ffn"]], 1).reshape(1, 4),
        "w_in": x["L0_xattn_W_in"].T, "b_in": x["L0_xattn_b_in"][None], "g_res": x["L0_xattn_g_res"].reshape(CC, P).T,
        "g_ini": by_dim(x["L0_xattn_g_init"][None, :C]),
        "w_b0": np.concatenate([x["L0_ffn_base_w"].T, x["L0_ffn_router_w"].T, x["L0_ffn_lora_A"]], 1),
        "b_b0": x["L0_ffn_base_b"][None], "b_rt": x["L0_ffn_router_b"][None],
        "w_lb": x["L0_ffn_lora_B"].reshape(RK, C),
        "w_qkv": np.concatenate([by_dim(w_qkv[:, :C]), by_dim(w_qkv[:, C:2 * C]), w_qkv[:, 2 * C:]], 1), "w_pr": x["L1_xattn_w_proj"].T, "b_pr": x["L1_xattn_b_proj"][None],
        "idx": x["L1_ffn_expert_indices"].T, "wts": x["L1_ffn_expert_weights"].T,
        "w1a": x["L1_ffn_w1_A"].T, "w1b": w1b,
        "w2a": x["L1_ffn_w2_A"].reshape(E, RK, FF).transpose(2, 0, 1), "w2b": x["L1_ffn_w2_B"],
    }
    nc = _bacc.Bacc("TRN2", target_bir_lowering=False, num_devices=1)
    feeds, aps = {}, {}
    for name, arr in arrays.items():
        arr = np.ascontiguousarray(arr)
        feeds["in_" + name] = arr
        aps[name] = nc.dram_tensor("in_" + name, arr.shape, _mybir.dt.from_np(arr.dtype), kind="ExternalInput").ap()
    out = nc.dram_tensor("out_0", (T, C), _mybir.dt.float32, kind="ExternalOutput").ap()
    build(nc, aps, out)
    r = _run(nc, [feeds], core_ids=[0])
    return r.results[0]["out_0"].reshape(1, T, C)
```
